# Optimizing a Trainium2 kernel written in Bass

```python
import numpy as np
import jax
import jax.numpy as jnp

def _softmax(x, axis=-1):
    return jax.nn.softmax(x, axis=axis)

def _gelu(x):
    return jax.nn.gelu(x, approximate=True)

def _silu(x):
    return jax.nn.silu(x)

def _sigmoid(x):
    return jax.nn.sigmoid(x)

def _layernorm(x, axis=-1, eps=1e-05):
    m = jnp.mean(x, axis=axis, keepdims=True)
    v = jnp.var(x, axis=axis, keepdims=True)
    return (x - m) / jnp.sqrt(v + eps)

def _scatter_add(tgt, idx, src, axis=0):
    return tgt.at[idx].add(src)

def _segment_sum(src, seg, n):
    return jax.ops.segment_sum(src, seg, n)
kernel_name = 'mk_gnn_resnorm_d4_gnn_r16_b88301'

def setup_inputs(seed: int=0):
    np.random.seed(seed)
    _w = jnp.asarray

    def _rec_inputs():
        import jax
        import jax.numpy as jnp
        _gk = jax.random.key(seed)
        x = -8.776e-05 + 1 * jax.random.normal(jax.random.fold_in(_gk, 1), (3125, 256), jnp.float32)
        _s = jax.random.randint(jax.random.fold_in(_gk, 2), (25000,), 0, 3125, jnp.int32)
        _d = jax.random.randint(jax.random.fold_in(_gk, 3), (25000,), 0, 3125, jnp.int32)
        _loop = jnp.arange(3125, dtype=jnp.int32)
        src = jnp.concatenate([_s, _d, _loop])
        dst = jnp.concatenate([_d, _s, _loop])
        _o = jnp.argsort(dst, stable=True)
        src = src[_o]
        dst = dst[_o]
        edge_type_16 = jax.random.randint(jax.random.fold_in(_gk, 13), (53125,), 0, 16, jnp.int32)
        edge_weight = jax.random.uniform(jax.random.fold_in(_gk, 14), (53125,), jnp.float32, 0.0, 0.999999)
        return (x, src, dst, edge_type_16, edge_weight)
    x, src, dst, edge_type_16, edge_weight = _rec_inputs()

    def _L0_gnn_setup():
        import jax, jax.numpy as jnp
        import numpy as np
        N_NODES = 1250
        N_EDGES = 20000
        D = 256
        N_LAYERS = 3
        BN_EPS = 1e-05
        key = jax.random.key(seed)
        ks = jax.random.split(key, 5)
        x = jax.random.normal(ks[0], (N_NODES, D), dtype=jnp.float32)
        src = jax.random.randint(ks[1], (N_EDGES,), 0, N_NODES)
        dst = jax.random.randint(ks[2], (N_EDGES,), 0, N_NODES)
        scale = 1.0 / np.sqrt(D)
        thetas = jax.random.normal(ks[3], (N_LAYERS, D, D), dtype=jnp.float32) * scale
        phis = jax.random.normal(ks[4], (N_LAYERS, D, D), dtype=jnp.float32) * scale
        gammas = jnp.ones((N_LAYERS, D), dtype=jnp.float32)
        betas = jnp.zeros((N_LAYERS, D), dtype=jnp.float32)
        return {'x': x, 'src': src, 'dst': dst, 'thetas': thetas, 'phis': phis, 'gammas': gammas, 'betas': betas}
    _L0_gnn_all = _L0_gnn_setup()
    _L0_gnn_in = {k: v for k, v in _L0_gnn_all.items() if k in ('thetas', 'phis', 'gammas', 'betas')}
    del _L0_gnn_all

    def _L1_gnn_setup():
        import jax, jax.numpy as jnp
        import numpy as np
        N = 3125
        E = 50000
        D = 256
        R = 16
        B = 8
        LN_EPS = 1e-05

        def _layer_norm(x, g, b):
            mu = jnp.mean(x, axis=-1, keepdims=True)
            var = jnp.mean(jnp.square(x - mu), axis=-1, keepdims=True)
            return (x - mu) * jax.lax.rsqrt(var + LN_EPS) * g + b

        def _rgcn_layer(x, edge_index, edge_type, edge_attr, basis, att, root, bias):
            n = x.shape[0]
            r = att.shape[0]
            weight = jnp.einsum('rb,bio->rio', att, basis)
            H = jnp.einsum('ni,rio->nro', x, weight)
            loop = jnp.arange(n, dtype=edge_index.dtype)
            src = jnp.concatenate([edge_index[0], loop])
            dst = jnp.concatenate([edge_index[1], loop])
            et = jnp.concatenate([edge_type, jnp.full((n,), r - 1, dtype=edge_type.dtype)])
            ea = jnp.concatenate([edge_attr, jnp.ones((n,), dtype=x.dtype)])
            msg = H[src, et] * ea[:, None]
            summ = jax.ops.segment_sum(msg, dst, num_segments=n)
            cnt = jax.ops.segment_sum(jnp.ones_like(ea), dst, num_segments=n)
            agg = summ / cnt[:, None]
            return agg + x @ root + bias
        key = jax.random.key(seed)
        ks = jax.random.split(key, 20)
        s_basis = np.sqrt(2.0 / (D + D)).astype(np.float32)
        s_att = np.sqrt(2.0 / (R + B)).astype(np.float32)
        inp = {'x': jax.random.normal(ks[0], (N, D), dtype=jnp.float32), 'edge_index': jax.random.randint(ks[1], (2, E), 0, N), 'edge_type': jax.random.randint(ks[2], (E,), 0, R), 'edge_attr': jax.random.uniform(ks[3], (E,), dtype=jnp.float32), 'basis1': jax.random.normal(ks[4], (B, D, D), dtype=jnp.float32) * s_basis, 'att1': jax.random.normal(ks[5], (R, B), dtype=jnp.float32) * s_att, 'root1': jax.random.normal(ks[6], (D, D), dtype=jnp.float32) * s_basis, 'bias1': jnp.zeros((D,), dtype=jnp.float32), 'ln1_g': jnp.ones((D,), dtype=jnp.float32), 'ln1_b': jnp.zeros((D,), dtype=jnp.float32), 'basis2': jax.random.normal(ks[7], (B, D, D), dtype=jnp.float32) * s_basis, 'att2': jax.random.normal(ks[8], (R, B), dtype=jnp.float32) * s_att, 'root2': jax.random.normal(ks[9], (D, D), dtype=jnp.float32) * s_basis, 'bias2': jnp.zeros((D,), dtype=jnp.float32), 'ln2_g': jnp.ones((D,), dtype=jnp.float32), 'ln2_b': jnp.zeros((D,), dtype=jnp.float32)}
        return inp
    _L1_gnn_all = _L1_gnn_setup()
    _L1_gnn_in = {k: v for k, v in _L1_gnn_all.items() if k in ('basis1', 'att1', 'root1', 'bias1', 'ln1_g', 'ln1_b', 'basis2', 'att2', 'root2', 'bias2', 'ln2_g', 'ln2_b')}
    del _L1_gnn_all

    def _L2_gnn_setup():
        import jax, jax.numpy as jnp
        import numpy as np
        N_NODES = 3125
        key = jax.random.key(seed)
        k1, k2, k3 = jax.random.split(key, 3)
        x = jax.random.normal(k1, (N_NODES, 256), dtype=jnp.float32)
        edge_index = jax.random.randint(k2, (2, 100000), 0, N_NODES, dtype=jnp.int64)
        W = jax.random.normal(k3, (256, 256), dtype=jnp.float32) / np.sqrt(256.0)
        b = jnp.zeros((256,), dtype=jnp.float32)
        return {'x': x, 'edge_index': edge_index, 'W': W, 'b': b}
    _L2_gnn_all = _L2_gnn_setup()
    _L2_gnn_in = {k: v for k, v in _L2_gnn_all.items() if k in ('W', 'b')}
    del _L2_gnn_all

    def _L3_gnn_setup():
        import jax, jax.numpy as jnp
        import numpy as np
        N = 2500
        E = 40000
        D = 256
        H = 8
        DH = D // H
        DFF = 4 * D
        SCALE = D ** (-0.5)
        EPS = 1e-05

        def layernorm(x, g, b):
            mu = jnp.mean(x, axis=-1, keepdims=True)
            var = jnp.mean(jnp.square(x - mu), axis=-1, keepdims=True)
            return (x - mu) * jax.lax.rsqrt(var + EPS) * g + b
        key = jax.random.key(seed)
        ks = jax.random.split(key, 12)
        inv = 1.0 / np.sqrt(D)
        invf = 1.0 / np.sqrt(DFF)
        return {'triplet_h': jax.random.normal(ks[0], (N, D), dtype=jnp.float32), 'src': jax.random.randint(ks[1], (E,), 0, N, dtype=jnp.int32), 'dst': jax.random.randint(ks[2], (E,), 0, N, dtype=jnp.int32), 'Wqkv': jax.random.uniform(ks[3], (D, 3 * D), jnp.float32, -inv, inv), 'bqkv': jax.random.uniform(ks[4], (3 * D,), jnp.float32, -inv, inv), 'ln_attn_g': jnp.ones((D,), jnp.float32), 'ln_attn_b': jnp.zeros((D,), jnp.float32), 'ln_res_g': jnp.ones((D,), jnp.float32), 'ln_res_b': jnp.zeros((D,), jnp.float32), 'W_in': jax.random.uniform(ks[5], (D, DFF), jnp.float32, -inv, inv), 'b_in': jax.random.uniform(ks[6], (DFF,), jnp.float32, -inv, inv), 'W_out': jax.random.uniform(ks[7], (DFF, D), jnp.float32, -invf, invf), 'b_out': jax.random.uniform(ks[8], (D,), jnp.float32, -invf, invf)}
    _L3_gnn_all = _L3_gnn_setup()
    _L3_gnn_in = {k: v for k, v in _L3_gnn_all.items() if k in ('Wqkv', 'bqkv', 'ln_attn_g', 'ln_attn_b', 'ln_res_g', 'ln_res_b', 'W_in', 'b_in', 'W_out', 'b_out')}
    del _L3_gnn_all
    return {'x': x, 'src': src, 'dst': dst, 'edge_type_16': edge_type_16, 'edge_weight': edge_weight, 'L0_gnn_thetas': _L0_gnn_in['thetas'], 'L0_gnn_phis': _L0_gnn_in['phis'], 'L0_gnn_gammas': _L0_gnn_in['gammas'], 'L0_gnn_betas': _L0_gnn_in['betas'], 'L1_gnn_basis1': _L1_gnn_in['basis1'], 'L1_gnn_att1': _L1_gnn_in['att1'], 'L1_gnn_root1': _L1_gnn_in['root1'], 'L1_gnn_bias1': _L1_gnn_in['bias1'], 'L1_gnn_ln1_g': _L1_gnn_in['ln1_g'], 'L1_gnn_ln1_b': _L1_gnn_in['ln1_b'], 'L1_gnn_basis2': _L1_gnn_in['basis2'], 'L1_gnn_att2': _L1_gnn_in['att2'], 'L1_gnn_root2': _L1_gnn_in['root2'], 'L1_gnn_bias2': _L1_gnn_in['bias2'], 'L1_gnn_ln2_g': _L1_gnn_in['ln2_g'], 'L1_gnn_ln2_b': _L1_gnn_in['ln2_b'], 'L2_gnn_W': _L2_gnn_in['W'], 'L2_gnn_b': _L2_gnn_in['b'], 'L3_gnn_Wqkv': _L3_gnn_in['Wqkv'], 'L3_gnn_bqkv': _L3_gnn_in['bqkv'], 'L3_gnn_ln_attn_g': _L3_gnn_in['ln_attn_g'], 'L3_gnn_ln_attn_b': _L3_gnn_in['ln_attn_b'], 'L3_gnn_ln_res_g': _L3_gnn_in['ln_res_g'], 'L3_gnn_ln_res_b': _L3_gnn_in['ln_res_b'], 'L3_gnn_W_in': _L3_gnn_in['W_in'], 'L3_gnn_b_in': _L3_gnn_in['b_in'], 'L3_gnn_W_out': _L3_gnn_in['W_out'], 'L3_gnn_b_out': _L3_gnn_in['b_out']}

def reference(x, src, dst, edge_type_16, edge_weight, L0_gnn_thetas, L0_gnn_phis, L0_gnn_gammas, L0_gnn_betas, L1_gnn_basis1, L1_gnn_att1, L1_gnn_root1, L1_gnn_bias1, L1_gnn_ln1_g, L1_gnn_ln1_b, L1_gnn_basis2, L1_gnn_att2, L1_gnn_root2, L1_gnn_bias2, L1_gnn_ln2_g, L1_gnn_ln2_b, L2_gnn_W, L2_gnn_b, L3_gnn_Wqkv, L3_gnn_bqkv, L3_gnn_ln_attn_g, L3_gnn_ln_attn_b, L3_gnn_ln_res_g, L3_gnn_ln_res_b, L3_gnn_W_in, L3_gnn_b_in, L3_gnn_W_out, L3_gnn_b_out):
    import jax
    import jax.numpy as jnp

    def _L0_gnn_ref(x, src, dst, thetas, phis, gammas, betas):
        import jax, jax.numpy as jnp
        import numpy as np
        N_NODES = 1250
        N_EDGES = 20000
        D = 256
        N_LAYERS = 3
        BN_EPS = 1e-05
        N = x.shape[0]
        for l in range(thetas.shape[0]):
            xi = x[src]
            xj = x[dst]
            e = jax.nn.relu((xj - xi) @ thetas[l].T + xi @ phis[l].T)
            agg = jax.ops.segment_max(e, src, num_segments=N)
            agg = jnp.where(agg < -1e+30, 0.0, agg)
            mu = agg.mean(axis=0)
            var = agg.var(axis=0)
            x = jax.nn.relu((agg - mu) * jax.lax.rsqrt(var + BN_EPS) * gammas[l] + betas[l])
        return x

    def _L1_gnn_ref(x, edge_index, edge_type, edge_attr, basis1, att1, root1, bias1, ln1_g, ln1_b, basis2, att2, root2, bias2, ln2_g, ln2_b):
        import jax, jax.numpy as jnp
        import numpy as np
        N = 3125
        E = 50000
        D = 256
        R = 16
        B = 8
        LN_EPS = 1e-05

        def _layer_norm(x, g, b):
            mu = jnp.mean(x, axis=-1, keepdims=True)
            var = jnp.mean(jnp.square(x - mu), axis=-1, keepdims=True)
            return (x - mu) * jax.lax.rsqrt(var + LN_EPS) * g + b

        def _rgcn_layer(x, edge_index, edge_type, edge_attr, basis, att, root, bias):
            n = x.shape[0]
            r = att.shape[0]
            weight = jnp.einsum('rb,bio->rio', att, basis)
            H = jnp.einsum('ni,rio->nro', x, weight)
            loop = jnp.arange(n, dtype=edge_index.dtype)
            src = jnp.concatenate([edge_index[0], loop])
            dst = jnp.concatenate([edge_index[1], loop])
            et = jnp.concatenate([edge_type, jnp.full((n,), r - 1, dtype=edge_type.dtype)])
            ea = jnp.concatenate([edge_attr, jnp.ones((n,), dtype=x.dtype)])
            msg = H[src, et] * ea[:, None]
            summ = jax.ops.segment_sum(msg, dst, num_segments=n)
            cnt = jax.ops.segment_sum(jnp.ones_like(ea), dst, num_segments=n)
            agg = summ / cnt[:, None]
            return agg + x @ root + bias
        h = x
        h_out = _rgcn_layer(h, edge_index, edge_type, edge_attr, basis1, att1, root1, bias1)
        h = jax.nn.relu(_layer_norm(h + h_out, ln1_g, ln1_b))
        h_out = _rgcn_layer(h, edge_index, edge_type, edge_attr, basis2, att2, root2, bias2)
        h = jax.nn.relu(_layer_norm(h + h_out, ln2_g, ln2_b))
        return h

    def _L2_gnn_ref(x, edge_index, W, b):
        import jax, jax.numpy as jnp
        import numpy as np
        N_NODES = 3125
        n = x.shape[0]
        self_loops = jnp.arange(n, dtype=edge_index.dtype)
        src = jnp.concatenate([edge_index[0], self_loops])
        dst = jnp.concatenate([edge_index[1], self_loops])
        deg = jax.ops.segment_sum(jnp.ones_like(dst, dtype=x.dtype), dst, num_segments=n)
        dinv = jnp.where(deg > 0, jax.lax.rsqrt(deg), 0.0)
        norm = dinv[src] * dinv[dst]
        xw = x @ W
        msgs = xw[src] * norm[:, None]
        agg = jax.ops.segment_sum(msgs, dst, num_segments=n)
        return jax.nn.relu(agg + b)

    def _L3_gnn_ref(triplet_h, src, dst, Wqkv, bqkv, ln_attn_g, ln_attn_b, ln_res_g, ln_res_b, W_in, b_in, W_out, b_out):
        import jax, jax.numpy as jnp
        import numpy as np
        N = 2500
        E = 40000
        D = 256
        H = 8
        DH = D // H
        DFF = 4 * D
        SCALE = D ** (-0.5)
        EPS = 1e-05

        def layernorm(x, g, b):
            mu = jnp.mean(x, axis=-1, keepdims=True)
            var = jnp.mean(jnp.square(x - mu), axis=-1, keepdims=True)
            return (x - mu) * jax.lax.rsqrt(var + EPS) * g + b
        n = triplet_h.shape[0]
        h = layernorm(triplet_h, ln_attn_g, ln_attn_b)
        qkv = (h @ Wqkv + bqkv).reshape(n, 3, H, DH)
        q = qkv[:, 0] * SCALE
        k = qkv[:, 1]
        v = qkv[:, 2]
        scores = jnp.einsum('ehd,ehd->eh', q[src], k[dst])
        m = jax.ops.segment_max(scores, dst, num_segments=n)
        e = jnp.exp(scores - m[dst])
        s = jax.ops.segment_sum(e, dst, num_segments=n)
        sa = e / s[dst]
        he = (v[src] * sa[:, :, None]).reshape(-1, D)
        agg = jax.ops.segment_sum(he, dst, num_segments=n)
        x = triplet_h + agg
        y = layernorm(x, ln_res_g, ln_res_b)
        y = jax.nn.gelu(y @ W_in + b_in, approximate=False) @ W_out + b_out
        return x + y
    edge_index = jnp.stack([src, dst])
    x = _layernorm(x + _L0_gnn_ref(x, src, dst, L0_gnn_thetas, L0_gnn_phis, L0_gnn_gammas, L0_gnn_betas), axis=-1)
    x = _layernorm(x + _L1_gnn_ref(x, edge_index, edge_type_16, edge_weight, L1_gnn_basis1, L1_gnn_att1, L1_gnn_root1, L1_gnn_bias1, L1_gnn_ln1_g, L1_gnn_ln1_b, L1_gnn_basis2, L1_gnn_att2, L1_gnn_root2, L1_gnn_bias2, L1_gnn_ln2_g, L1_gnn_ln2_b), axis=-1)
    x = _layernorm(x + _L2_gnn_ref(x, edge_index, L2_gnn_W, L2_gnn_b), axis=-1)
    x = _layernorm(x + _L3_gnn_ref(x, src, dst, L3_gnn_Wqkv, L3_gnn_bqkv, L3_gnn_ln_attn_g, L3_gnn_ln_attn_b, L3_gnn_ln_res_g, L3_gnn_ln_res_b, L3_gnn_W_in, L3_gnn_b_in, L3_gnn_W_out, L3_gnn_b_out), axis=-1)
    return x

_drawn_inputs = setup_inputs


def setup_inputs(seed=0):
    import zlib

    import numpy as np

    out = dict(_drawn_inputs(seed))
    spreads = {'L0_gnn_gammas': (1.0, 0.2),
     'L0_gnn_betas': (0.0, 0.1),
     'L1_gnn_bias1': (0.0, 0.1),
     'L1_gnn_ln1_g': (1.0, 0.2),
     'L1_gnn_ln1_b': (0.0, 0.1),
     'L1_gnn_bias2': (0.0, 0.1),
     'L1_gnn_ln2_g': (1.0, 0.2),
     'L1_gnn_ln2_b': (0.0, 0.1),
     'L2_gnn_b': (0.0, 0.1),
     'L3_gnn_ln_attn_g': (1.0, 0.6),
     'L3_gnn_ln_attn_b': (0.0, 0.274),
     'L3_gnn_ln_res_g': (1.0, 0.6),
     'L3_gnn_ln_res_b': (0.0, 0.8)}
    factors = {'L3_gnn_bqkv': 3.181, 'L3_gnn_b_in': 8.0, 'L3_gnn_b_out': 6.515}
    for name, (base, spread) in spreads.items():
        noise = np.random.default_rng([zlib.crc32(name.encode()), seed]).standard_normal(out[name].shape)
        drawn = base * np.exp(spread * noise) if base else spread * noise
        out[name] = jnp.asarray(drawn.astype(out[name].dtype))
    for name, factor in factors.items():
        out[name] = (out[name] * factor).astype(out[name].dtype)
    return out
```

```python
import itertools
from contextlib import ExitStack, contextmanager

import numpy as np

import concourse.bass as bass
from concourse import mybir
from concourse.alu_op_type import AluOpType as ALU

FP32 = mybir.dt.float32
BF16 = mybir.dt.bfloat16
FP16 = mybir.dt.float16
I32 = mybir.dt.int32
ACT = mybir.ActivationFunctionType
AX = mybir.AxisListType

P = 128
N = 3125
D = 256
E = 53125
TILES = -(-N // P)
ROWS = TILES * P
LAST = N - (TILES - 1) * P
STEPS = -(-E // P // 8) * 8
SLOTS = P * STEPS
TAIL = E - (P - 1) * STEPS
GROUP = 8
GROUPS = STEPS // GROUP
RING = 4
LAYERS = 3
CHUNK = 5
TYPES = 16
BASES = 8
HEADS = 8
DH = D // HEADS
DFF = 4 * D
EPS = 1e-5
NEG = -1e30
ROUND = 12582912.0


SERIAL = itertools.count()


def buffer(stack, nc, name, cols, dt=FP32):
    return stack.enter_context(nc.sbuf_tensor(f"{name}_{next(SERIAL)}", [P, cols], dt))


class Env:
    pass


@contextmanager
def phase(nc, *names):
    with ExitStack() as stack:
        sems = [stack.enter_context(nc.semaphore(f"{n}_{next(SERIAL)}")) for n in names]
        yield sems
        with nc.Block() as block:
            @block.gpsimd
            def _(pool):
                pool.dma_reset(range(min(s.num for s in sems), max(s.num for s in sems) + 1))
                for s in sems:
                    pool.sem_clear(s)


def counted_steps(engine, sem):
    done = itertools.count(1)

    def then(instruction):
        instruction.then_inc(sem, 1)
        engine.wait_ge(sem, next(done))
    return then


def later(g):
    return not isinstance(g, int) or g >= 2


def bulk(ap, tiles=TILES):
    return ap.rearrange("p (a d) -> p a d", a=tiles)


def constants(nc, env):
    with phase(nc, "filled", "shaped") as (filled, shaped), nc.Block() as block:
        @block.gpsimd
        def _(pool):
            pool.memset(env.ident[:], 0.0).then_inc(filled, 1)
            pool.memset(env.ones[:], 1.0).then_inc(filled, 1)
            pool.iota(env.iota_p[:], pattern=[[1, P]], base=0, channel_multiplier=0,
                      allow_small_or_imprecise_dtypes=True).then_inc(filled, 1)
            pool.iota(env.iota_steps[:], pattern=[[1, STEPS]], base=0, channel_multiplier=0,
                      allow_small_or_imprecise_dtypes=True).then_inc(filled, 1)
            pool.iota(env.iota_a1[:], pattern=[[1, TILES]], base=1, channel_multiplier=0,
                      allow_small_or_imprecise_dtypes=True).then_inc(filled, 1)
            pool.iota(env.own[:], pattern=[[0, 1]], base=0, channel_multiplier=1,
                      allow_small_or_imprecise_dtypes=True).then_inc(filled, 1)
            pool.wait_ge(filled, 6)
            pool.affine_select(out=env.ident[:], in_=env.ident[:], compare_op=ALU.not_equal, fill=1.0,
                               base=0, pattern=[[-1, P]], channel_multiplier=1).then_inc(shaped, 1)
            pool.affine_select(out=env.after[:], in_=env.ones[:], compare_op=ALU.is_gt, fill=0.0,
                               base=0, pattern=[[1, P]], channel_multiplier=-1).then_inc(shaped, 1)
            pool.affine_select(out=env.before[:], in_=env.ones[:], compare_op=ALU.is_gt, fill=0.0,
                               base=0, pattern=[[-1, P]], channel_multiplier=1).then_inc(shaped, 1)
            pool.wait_ge(shaped, 3)
            pool.tensor_copy(env.ident16[:], env.ident[:]).then_inc(filled, 1)

        @block.vector
        def _(dve):
            dve.wait_ge(filled, 6)
            nc.vector.reciprocal(env.inv_a1[:], env.iota_a1[:])


def edge_columns(nc, env, node_dram, other_dram, type_dram=None, weight_dram=None):
    typed = type_dram is not None
    with ExitStack() as stack:
        node, other, part = (buffer(stack, nc, n, STEPS, I32) for n in ("node", "other", "part"))
        loads = [(node, node_dram), (other, other_dram)]
        if typed:
            kind = buffer(stack, nc, "kind", STEPS, I32)
            weight = buffer(stack, nc, "weight", STEPS)
            loads += [(kind, type_dram), (weight, weight_dram)]
        with phase(nc, "padded", "loaded", "step") as (padded, loaded, step), nc.Block() as block:
            @block.sync
            def _(sp):
                sp.wait_ge(padded, len(loads))
                for tile, dram in loads:
                    sp.dma_start(tile[0:P - 1, :], dram[0:(P - 1) * STEPS].rearrange("(p t) -> p t", t=STEPS)).then_inc(loaded, 16)
                    sp.dma_start(tile[P - 1:P, 0:TAIL], dram[(P - 1) * STEPS:E].unsqueeze(0)).then_inc(loaded, 16)

            @block.vector
            def _(dve):
                then = counted_steps(dve, step)

                nc.vector.memset(node[:], ROWS - 1).then_inc(padded, 1)
                nc.vector.memset(other[:], ROWS - 1).then_inc(padded, 1)
                if typed:
                    nc.vector.memset(kind[:], 0).then_inc(padded, 1)
                    nc.vector.memset(weight[:], 0.0).then_inc(padded, 1)
                dve.wait_ge(loaded, 2 * len(loads) * 16)
                then(nc.vector.tensor_single_scalar(part[:], node[:], 7, op=ALU.logical_shift_right))
                then(nc.vector.tensor_scalar(out=env.col_a1[:], in0=part[:], scalar1=1.0, scalar2=None, op0=ALU.add))
                then(nc.vector.tensor_single_scalar(part[:], node[:], 127, op=ALU.bitwise_and))
                then(nc.vector.tensor_copy(env.col_b[:], part[:]))
                if typed:
                    record = env.records[:].rearrange("p (t c) -> p t c", c=2)
                    then(nc.vector.tensor_single_scalar(other[:], other[:], 4, op=ALU.logical_shift_left))
                    then(nc.vector.tensor_tensor(out=other[:], in0=other[:], in1=kind[:], op=ALU.bitwise_or))
                    then(nc.vector.tensor_copy(record[:, :, 0], other[:]))
                    then(nc.vector.tensor_copy(record[:, :, 1], weight[:]))
                else:
                    then(nc.vector.tensor_single_scalar(part[:], other[:], 8, op=ALU.logical_shift_right))
                    then(nc.vector.tensor_copy(env.piece[0][:], part[:]))
                    then(nc.vector.tensor_single_scalar(part[:], other[:], 255, op=ALU.bitwise_and))
                    then(nc.vector.tensor_copy(env.piece[1][:], part[:]))


SCATTER_GROUP = 16
SCATTER_SEMS = ("scatter_staged", "landed0", "landed1", "scatter_held")


class Nothing:

    def share(self, nc, block, sems, groups):
        pass


NOTHING = Nothing()


class Scatter:

    def __init__(self, stack, nc, records, dram):
        self.records, self.dram, self.done = records, dram, 0
        self.place = buffer(stack, nc, "scatter_place", STEPS, I32)
        self.index = [buffer(stack, nc, "scatter_index", SCATTER_GROUP, I32) for _ in range(2)]
        self.record = [buffer(stack, nc, "scatter_record", 2 * SCATTER_GROUP) for _ in range(2)]

    def share(self, nc, block, sems, groups):
        staged, landed = sems[0], sems[1:3]
        first = self.done
        self.done += groups

        @block.gpsimd
        def _(pool):
            def send(g, h, n):
                at = (first + g) * SCATTER_GROUP
                if not isinstance(n, int) or n > 0:
                    pool.wait_ge(landed[h], n * (16 * SCATTER_GROUP))
                    pool.sem_inc(sems[3], 1)
                pool.tensor_copy(self.index[h][:], self.place[:, bass.ds(at, SCATTER_GROUP)]).then_inc(staged, 1)
                pool.tensor_copy(self.record[h][:], self.records[:, bass.ds(at * 2, 2 * SCATTER_GROUP)]).then_inc(staged, 1)
                pool.wait_ge(staged, 2 * g + 2)
                pool.sem_inc(sems[3], 1)
                for u in range(SCATTER_GROUP):
                    pool.indirect_dma_start(
                        out=self.dram, out_offset=bass.IndirectOffsetOnAxis(ap=self.index[h][:, u:u + 1], axis=0),
                        in_=self.record[h][:, 2 * u:2 * u + 2], in_offset=None).then_inc(landed[h], 16)
            for g in range(min(2, groups)):
                send(g, g, 0)
            if groups // 2 > 1:
                with pool.Fori(1, groups // 2) as i:
                    for h in range(2):
                        send(2 * i + h, h, i)
            if groups % 2 and groups > 2:
                send(groups - 1, 0, groups // 2)
            for h in range(2):
                if (groups + 1 - h) // 2:
                    pool.wait_ge(landed[h], (groups + 1 - h) // 2 * 16 * SCATTER_GROUP)


def edge_order(nc, env, order, beside):
    col_a1, col_b = env.col_a1, env.col_b
    with ExitStack() as stack:
        rank, place, sq = order.keep, order.anew, env.tmp
        counting = stack.enter_context(ExitStack())
        def sc(name, shape, dt=FP32):
            return buffer(counting, nc, name, shape[1], dt)
        wt = sc("wt", [P, STEPS * P], BF16)
        count = sc("count", [P, STEPS * TILES])
        hot_a = sc("hot_a", [P, STEPS * TILES], BF16)
        ring = stack.enter_context(ExitStack())
        w = buffer(ring, nc, "w", 2 * GROUP * P, BF16)

        def tile_of(buffer, g, u, width):
            return buffer[:, bass.ds(g * (GROUP * width) + u * width, width)]

        names = ("hot", "w_ready", "turned", "copied", "counted", "count_kept", "compared", "ranked", "held") + SCATTER_SEMS
        with phase(nc, *names) as (hot, w_ready, turned, copied, counted, count_kept, compared, ranked, held, *scatter_sems), \
                nc.Block() as block:
            beside.share(nc, block, scatter_sems, 13)
            turn_bank = [env.bank[h][:].bitcast(BF16) for h in range(2)]
            count_bank = [env.bank[2 + h] for h in range(2)]
            eq_bank = [env.bank[4:6], env.bank[6:8]]

            @block.vector
            def _(dve):
                def make_w(g, h):
                    if later(g):
                        dve.wait_ge(counted, g - 1)
                    for u in range(GROUP):
                        t = g * GROUP + u
                        last = nc.vector.tensor_scalar(
                            out=w[:, (h * GROUP + u) * P:(h * GROUP + u + 1) * P], in0=env.iota_p[:],
                            scalar1=col_b[:, bass.ds(t, 1)], scalar2=col_a1[:, bass.ds(t, 1)],
                            op0=ALU.is_equal, op1=ALU.mult)
                    last.then_inc(w_ready, 1)

                def finish(g, h):
                    dve.wait_ge(counted, g + 1)
                    nc.vector.tensor_tensor(
                        out=bulk(count[:, bass.ds(g * (GROUP * TILES), GROUP * TILES)], GROUP),
                        in0=bulk(count_bank[h][:, 0:GROUP * TILES], GROUP),
                        in1=env.inv_a1[:].unsqueeze(1).broadcast_to([P, GROUP, TILES]), op=ALU.mult).then_inc(count_kept, 1)
                    dve.wait_ge(compared, g + 1)
                    for u in range(GROUP):
                        t = g * GROUP + u
                        products = eq_bank[h][u // 4][:, (u % 4) * P:(u % 4 + 1) * P]
                        last = nc.vector.scalar_tensor_tensor(
                            out=products, in0=products, scalar=sq[:, bass.ds(t, 1)],
                            in1=env.after[:], op0=ALU.is_equal, op1=ALU.mult,
                            accum_out=rank[:, bass.ds(t, 1)])
                    last.then_inc(ranked, 1)

                nc.vector.tensor_tensor(out=sq[:], in0=col_a1[:], in1=col_a1[:], op=ALU.mult).then_inc(hot, 1)
                nc.vector.tensor_tensor(
                    out=bulk(hot_a[:], STEPS), in0=col_a1[:].unsqueeze(2).broadcast_to([P, STEPS, TILES]),
                    in1=env.iota_a1[:].unsqueeze(1).broadcast_to([P, STEPS, TILES]), op=ALU.is_equal).then_inc(hot, 1)
                dve.wait_ge(hot, 2)
                make_w(0, 0)
                make_w(1, 1)
                finish(0, 0)
                with dve.Fori(1, GROUPS // 2) as i:
                    make_w(2 * i, 0)
                    finish(2 * i - 1, 1)
                    make_w(2 * i + 1, 1)
                    finish(2 * i, 0)
                finish(GROUPS - 1, 1)

            @block.tensor
            def _(pe):
                def turn(g, h):
                    pe.wait_ge(w_ready, g + 1)
                    pe.sem_inc(held, 1)
                    if later(g):
                        pe.wait_ge(copied, g - 1)
                        pe.sem_inc(held, 1)
                        pe.wait_ge(count_kept, g - 1)
                        pe.sem_inc(held, 1)
                    for u in range(GROUP):
                        wu = w[:, (h * GROUP + u) * P:(h * GROUP + u + 1) * P]
                        last = nc.tensor.transpose(turn_bank[h][:, u * P:(u + 1) * P], wu, env.ident16[:])
                    last.then_inc(turned, 1)
                    for u in range(GROUP):
                        wu = w[:, (h * GROUP + u) * P:(h * GROUP + u + 1) * P]
                        last = nc.tensor.matmul(count_bank[h][:, u * TILES:(u + 1) * TILES], wu,
                                                tile_of(hot_a, g, u, TILES), start=True, stop=True)
                    last.then_inc(counted, 1)

                def compare(g, h):
                    pe.wait_ge(copied, g + 1)
                    pe.sem_inc(held, 1)
                    if later(g):
                        pe.wait_ge(ranked, g - 1)
                        pe.sem_inc(held, 1)
                    for u in range(GROUP):
                        wtu = tile_of(wt, g, u, P)
                        last = nc.tensor.matmul(eq_bank[h][u // 4][:, (u % 4) * P:(u % 4 + 1) * P], wtu, wtu,
                                                start=True, stop=True)
                    last.then_inc(compared, 1)

                pe.wait_ge(hot, 2)
                for g in range(2):
                    turn(g, g)
                    compare(g, g)
                with pe.Fori(1, GROUPS // 2) as i:
                    for h in range(2):
                        turn(2 * i + h, h)
                        compare(2 * i + h, h)

            @block.scalar
            def _(act):
                with act.Fori(0, GROUPS // 2) as i:
                    for h in range(2):
                        g = 2 * i + h
                        act.wait_ge(turned, g + 1)
                        act.sem_inc(held, 1)
                        nc.scalar.copy(wt[:, bass.ds(g * (GROUP * P), GROUP * P)], turn_bank[h][:, 0:GROUP * P]).then_inc(copied, 1)

        ring.close()
        with ExitStack() as inner:
            total = buffer(inner, nc, "total", TILES, FP32)
            base = order.start
            with phase(nc, "summed", "totalled", "step") as (summed, totalled, step), nc.Block() as block:
                @block.vector
                def _(dve):
                    nc.vector.tensor_scalar(out=count[:], in0=count[:], scalar1=ROUND, scalar2=ROUND,
                                            op0=ALU.add, op1=ALU.subtract).then_inc(step, 1)
                    dve.wait_ge(step, 1)
                    cols = count[:].rearrange("p (t a) -> p a t", a=TILES)
                    for a in range(TILES):
                        nc.vector.tensor_tensor_scan(
                            out=cols[:, a, :], data0=env.ones[:, 0:1].broadcast_to([P, STEPS]),
                            data1=cols[:, a, :], initial=0.0, op0=ALU.mult, op1=ALU.add).then_inc(step, 1)
                    dve.wait_ge(step, 1 + TILES)
                    nc.vector.tensor_copy(total[:], count[:, (STEPS - 1) * TILES:]).then_inc(summed, 1)
                    dve.wait_ge(totalled, 1)
                    nc.vector.tensor_tensor_scan(
                        out=base[:], data0=env.ones[:, 0:TILES], data1=env.bank[1][:, 0:TILES], initial=0.0,
                        op0=ALU.mult, op1=ALU.add).then_inc(step, 1)
                    dve.wait_ge(step, 2 + TILES)
                    nc.vector.tensor_tensor(out=base[:], in0=base[:], in1=env.bank[1][:, 0:TILES], op=ALU.subtract).then_inc(step, 1)
                    dve.wait_ge(step, 3 + TILES)
                    nc.vector.tensor_tensor(out=base[:], in0=base[:], in1=env.bank[0][:, 0:TILES], op=ALU.add).then_inc(step, 1)
                    nc.vector.tensor_copy(order.count[:], total[:]).then_inc(step, 1)

                @block.tensor
                def _(pe):
                    pe.wait_ge(summed, 1)
                    nc.tensor.matmul(env.bank[0][:, 0:TILES], env.after[:], total[:], start=True, stop=True)
                    nc.tensor.matmul(env.bank[1][:, 0:TILES], env.ones[:], total[:], start=True, stop=True).then_inc(totalled, 1)

        with ExitStack() as inner:
            W1, W2 = GROUP * TILES, GROUP * 2 * TILES
            part = buffer(inner, nc, "part", 2 * W1)
            high_low = buffer(inner, nc, "high_low", 2 * W2, BF16)
            found = buffer(inner, nc, "found", 2 * W2)
            names = ("added", "cut_high", "cut", "looked_up", "picked", "placed", "held") + SCATTER_SEMS
            with phase(nc, *names) as (added, cut_high, cut, looked_up, picked, placed, held, *scatter_sems), \
                    nc.Block() as block:
                beside.share(nc, block, scatter_sems, 5)

                def part_of(h):
                    return bulk(part[:, h * W1:(h + 1) * W1], GROUP)

                def high_low_of(h):
                    return bulk(high_low[:, h * W2:(h + 1) * W2], GROUP)

                @block.vector
                def _(dve):
                    def add(g, h):
                        if later(g):
                            dve.wait_ge(cut, g - 1)
                        nc.vector.tensor_tensor(
                            out=part_of(h), in0=bulk(count[:, bass.ds(g * W1, W1)], GROUP),
                            in1=base[:].unsqueeze(1).broadcast_to([P, GROUP, TILES]), op=ALU.add).then_inc(added, 1)

                    def low(g, h):
                        dve.wait_ge(cut_high, g + 1)
                        nc.vector.tensor_tensor(out=high_low_of(h)[:, :, TILES:], in0=part_of(h), in1=high_low_of(h)[:, :, 0:TILES],
                                                op=ALU.subtract).then_inc(cut, 1)

                    def pick(g, h):
                        dve.wait_ge(looked_up, g + 1)
                        if later(g):
                            dve.wait_ge(placed, g - 1)
                        nc.vector.tensor_tensor(
                            out=found[:, h * W2:(h + 1) * W2].rearrange("p (u s a) -> p u s a", u=GROUP, s=2),
                            in0=env.bank[h][:, 0:W2].rearrange("p (u s a) -> p u s a", u=GROUP, s=2),
                            in1=bulk(hot_a[:, bass.ds(g * W1, W1)], GROUP).unsqueeze(2).broadcast_to([P, GROUP, 2, TILES]),
                            op=ALU.mult).then_inc(picked, 1)

                    def total_up(g, h):
                        dve.wait_ge(picked, g + 1)
                        nc.vector.tensor_reduce(out=place[:, bass.ds(g * GROUP, GROUP)], in_=bulk(found[:, h * W2:(h + 1) * W2], GROUP),
                                                axis=AX.X, op=ALU.add).then_inc(placed, 1)

                    add(0, 0)
                    add(1, 1)
                    low(0, 0)
                    for g in range(2):
                        add(g + 2, g)
                        pick(g, g)
                        low(g + 1, 1 - g)
                        total_up(g, g)
                    with dve.Fori(1, GROUPS // 2 - 1) as i:
                        for h in range(2):
                            add(2 * i + h + 2, h)
                            pick(2 * i + h, h)
                            low(2 * i + h + 1, 1 - h)
                            total_up(2 * i + h, h)
                    pick(GROUPS - 2, 0)
                    low(GROUPS - 1, 1)
                    total_up(GROUPS - 2, 0)
                    pick(GROUPS - 1, 1)
                    total_up(GROUPS - 1, 1)

                @block.scalar
                def _(act):
                    def high(g, h):
                        act.wait_ge(added, g + 1)
                        act.sem_inc(held, 1)
                        if later(g):
                            act.wait_ge(looked_up, g - 1)
                            act.sem_inc(held, 1)
                        nc.scalar.copy(high_low_of(h)[:, :, 0:TILES], part_of(h)).then_inc(cut_high, 1)
                    for g in range(2):
                        high(g, g)
                    with act.Fori(1, GROUPS // 2) as i:
                        for h in range(2):
                            high(2 * i + h, h)

                @block.tensor
                def _(pe):
                    def look_up(g, h):
                        pe.wait_ge(cut, g + 1)
                        pe.sem_inc(held, 1)
                        if later(g):
                            pe.wait_ge(picked, g - 1)
                            pe.sem_inc(held, 1)
                        for u in range(GROUP):
                            last = nc.tensor.matmul(
                                env.bank[h][:, u * 2 * TILES:(u + 1) * 2 * TILES], tile_of(wt, g, u, P),
                                high_low[:, h * W2 + u * 2 * TILES:h * W2 + (u + 1) * 2 * TILES], start=True, stop=True)
                        last.then_inc(looked_up, 1)
                    for g in range(2):
                        look_up(g, g)
                    with pe.Fori(1, GROUPS // 2) as i:
                        for h in range(2):
                            look_up(2 * i + h, h)
        counting.close()

        with ExitStack() as inner:
            def si(name, shape, dt=FP32):
                return buffer(inner, nc, name, shape[1], dt)
            blk, stp = si("blk", [P, STEPS]), si("stp", [P, STEPS])
            n_blk, n_stp = si("n_blk", [P, TILES]), si("n_stp", [P, TILES])
            l_blk, l_stp = si("l_blk", [P, TILES]), si("l_stp", [P, TILES])
            last, crosses = si("last", [P, TILES]), si("crosses", [P, TILES])
            piece_a = si("piece_a", [P, TILES])
            with phase(nc, "step") as (step,), nc.Block() as block:
                @block.vector
                def _(dve):
                    then = counted_steps(dve, step)

                    def locate(at, b, s):
                        then(nc.vector.tensor_scalar(out=b[:], in0=at[:], scalar1=0.5, scalar2=1.0 / STEPS, op0=ALU.add, op1=ALU.mult))
                        then(nc.vector.tensor_scalar(out=b[:], in0=b[:], scalar1=-0.5, scalar2=ROUND, op0=ALU.add, op1=ALU.add))
                        then(nc.vector.tensor_scalar(out=b[:], in0=b[:], scalar1=-ROUND, scalar2=None, op0=ALU.add))
                        then(nc.vector.scalar_tensor_tensor(out=s[:], in0=b[:], scalar=-float(STEPS), in1=at[:], op0=ALU.mult, op1=ALU.add))

                    then(nc.vector.reciprocal(blk[:], col_a1[:]))
                    then(nc.vector.tensor_tensor(out=place[:], in0=place[:], in1=blk[:], op=ALU.mult))
                    then(nc.vector.tensor_scalar(out=place[:], in0=place[:], scalar1=ROUND, scalar2=-ROUND, op0=ALU.add, op1=ALU.add))
                    then(nc.vector.scalar_tensor_tensor(out=place[:], in0=place[:], scalar=-1.0, in1=rank[:], op0=ALU.add, op1=ALU.subtract))
                    locate(place, blk, stp)
                    locate(order.start, n_blk, n_stp)
                    then(nc.vector.tensor_scalar(out=order.some[:], in0=order.count[:], scalar1=1.0, scalar2=None, op0=ALU.min))
                    then(nc.vector.tensor_tensor(out=last[:], in0=order.start[:], in1=order.count[:], op=ALU.add))
                    then(nc.vector.tensor_scalar(out=last[:], in0=last[:], scalar1=-1.0, scalar2=0.0, op0=ALU.add, op1=ALU.max))
                    locate(last, l_blk, l_stp)
                    then(nc.vector.tensor_copy(order.last[:], last[:]))
                    then(nc.vector.tensor_tensor(out=crosses[:], in0=l_blk[:], in1=n_blk[:], op=ALU.is_gt))
                    then(nc.vector.tensor_tensor(out=crosses[:], in0=crosses[:], in1=order.some[:], op=ALU.mult))
                    then(nc.vector.tensor_scalar(out=order.stays[:], in0=crosses[:], scalar1=-1.0, scalar2=-NEG, op0=ALU.add, op1=ALU.mult))
                    then(nc.vector.scalar_tensor_tensor(out=l_blk[:], in0=l_blk[:], scalar=1.0, in1=crosses[:], op0=ALU.add, op1=ALU.mult))
                    then(nc.vector.tensor_scalar(out=order.end_block[:], in0=l_blk[:], scalar1=-1.0, scalar2=None, op0=ALU.add))
                    then(nc.vector.tensor_scalar(out=piece_a[:], in0=env.iota_a1[:], scalar1=-1.0, scalar2=None, op0=ALU.add))
                    then(nc.vector.tensor_tensor(out=piece_a[:], in0=piece_a[:], in1=order.some[:], op=ALU.mult))
                    then(nc.vector.tensor_scalar(out=last[:], in0=order.some[:], scalar1=env.own[:, 0:1], scalar2=None, op0=ALU.mult))

            order.place_edges(nc, env, place, blk, stp, beside)
            permute(nc, env, n_blk, n_stp, [order.some, piece_a, last], TILES, 1, NOTHING, 0)
            segments(nc, env, order)


def permute(nc, env, blk, stp, pieces, tiles, group, beside, shares):
    n = len(pieces)
    body = 2 * group
    whole = tiles // body
    with ExitStack() as stack:
        hot_step = buffer(stack, nc, "hot_step", body * STEPS, BF16)
        hot_block = buffer(stack, nc, "hot_block", body * n * P, BF16)
        with phase(nc, "hot", "used", "held", *SCATTER_SEMS) as (hot, used, held, *scatter_sems), nc.Block() as block:
            beside.share(nc, block, scatter_sems, shares)

            @block.vector
            def _(dve):
                def make(g, h):
                    if later(g):
                        dve.wait_ge(used, g - 1)
                    for u in range(group):
                        t = g * group + u
                        v = h * group + u
                        nc.vector.tensor_scalar(out=hot_step[:, v * STEPS:(v + 1) * STEPS], in0=env.iota_steps[:],
                                                scalar1=stp[:, bass.ds(t, 1)], scalar2=None, op0=ALU.is_equal)
                        for i, piece in enumerate(pieces):
                            last = nc.vector.tensor_scalar(
                                out=hot_block[:, (v * n + i) * P:(v * n + i + 1) * P], in0=env.iota_p[:],
                                scalar1=blk[:, bass.ds(t, 1)], scalar2=piece[:, bass.ds(t, 1)],
                                op0=ALU.is_equal, op1=ALU.mult)
                    last.then_inc(hot, 1)

                make(0, 0)
                make(1, 1)
                with dve.Fori(1, whole) as i:
                    make(2 * i, 0)
                    make(2 * i + 1, 1)
                if tiles % body:
                    make(2 * whole, 0)

            @block.tensor
            def _(pe):
                def add(g, h, first=False, final=False):
                    pe.wait_ge(hot, g + 1)
                    pe.sem_inc(held, 1)
                    for u in range(group):
                        v = h * group + u
                        for i in range(n):
                            last = nc.tensor.matmul(
                                env.bank[i][:, 0:STEPS], hot_block[:, (v * n + i) * P:(v * n + i + 1) * P],
                                hot_step[:, v * STEPS:(v + 1) * STEPS], start=first and u == 0, stop=final and u == group - 1)
                    last.then_inc(used, 1)

                odd = bool(tiles % body)
                add(0, 0, first=True)
                add(1, 1)
                with pe.Fori(1, whole - 1) as i:
                    add(2 * i, 0)
                    add(2 * i + 1, 1)
                add(2 * whole - 2, 0)
                add(2 * whole - 1, 1, final=not odd)
                if odd:
                    add(2 * whole, 0, final=True)


def segments(nc, env, order):
    with ExitStack() as stack:
        def sb(name, shape, dt=FP32):
            return buffer(stack, nc, name, shape[1], dt)
        ident_v, row = sb("ident_v", [P, 2 * P]), sb("row", [P, P])
        open_all, carry = sb("open_all", [P, 1]), sb("carry", [P, 1])
        node, at = sb("node", [P, STEPS]), sb("at", [P, STEPS])
        with phase(nc, "step", "spread", "spread_done") as (step, spread, spread_done), nc.Block() as block:
            @block.vector
            def _(dve):
                then = counted_steps(dve, step)

                first, node_a, node_b = (env.bank[i][:, 0:STEPS] for i in range(3))
                then(nc.vector.tensor_scalar(out=order.keep[:], in0=first, scalar1=-1.0, scalar2=1.0, op0=ALU.mult, op1=ALU.add))
                then(nc.vector.tensor_scalar(out=order.anew[:], in0=first, scalar1=NEG, scalar2=None, op0=ALU.mult))
                then(nc.vector.tensor_reduce(out=open_all[:], in_=order.keep[:], axis=AX.X, op=ALU.min))
                then(nc.vector.tensor_copy(at[:], node_b))
                then(nc.vector.scalar_tensor_tensor(out=at[:], in0=node_a, scalar=float(P), in1=at[:], op0=ALU.mult, op1=ALU.add))
                then(nc.vector.tensor_tensor_scan(out=node[:], data0=at[:], data1=at[:], initial=0.0, op0=ALU.max, op1=ALU.max))
                nc.vector.tensor_scalar(out=ident_v[:, 0:P], in0=env.ident[:], scalar1=open_all[:, 0:1], scalar2=None, op0=ALU.mult).then_inc(spread, 1)
                nc.vector.tensor_scalar(out=ident_v[:, P:], in0=env.ident[:], scalar1=node[:, STEPS - 1:STEPS], scalar2=None, op0=ALU.mult).then_inc(spread, 1)
                dve.wait_ge(spread_done, 1)
                then(nc.vector.tensor_copy(order.open_row[:], env.bank[4][:, 0:P]))
                then(nc.vector.tensor_scalar(out=order.shut_row[:], in0=order.open_row[:], scalar1=-1.0, scalar2=-NEG, op0=ALU.add, op1=ALU.mult))
                then(nc.vector.tensor_tensor(out=row[:], in0=env.bank[5][:, 0:P], in1=env.before[:], op=ALU.mult))
                then(nc.vector.tensor_reduce(out=carry[:], in_=row[:], axis=AX.X, op=ALU.max))
                if order.node is not None:
                    then(nc.vector.tensor_scalar(out=order.node[:], in0=node[:], scalar1=carry[:, 0:1], scalar2=None, op0=ALU.max))

            @block.tensor
            def _(pe):
                pe.wait_ge(spread, 2)
                nc.tensor.matmul(env.bank[4][:, 0:P], env.ones[:], ident_v[:, 0:P], start=True, stop=True)
                nc.tensor.matmul(env.bank[5][:, 0:P], env.ones[:], ident_v[:, P:], start=True, stop=True).then_inc(spread_done, 1)


class Order:

    def __init__(self, stack, nc, name):
        def sb(what, cols, dt=FP32):
            return buffer(stack, nc, f"{name}_{what}", cols, dt)
        self.start = sb("start", TILES)
        self.count = sb("count", TILES)
        self.some = sb("some", TILES)
        self.last = sb("last", TILES, I32)
        self.stays = sb("stays", TILES)
        self.end_block = sb("end_block", TILES)
        self.keep = sb("keep", STEPS)
        self.anew = sb("anew", STEPS)
        self.open_row = sb("open_row", P)
        self.shut_row = sb("shut_row", P)
        self.node = None
        self.row = sb("row", STEPS, I32)
        self.name = name

    def spread_ends(self, stack, nc, env):
        order = self
        order.end_row = buffer(stack, nc, "end_row", ROWS, BF16)
        with ExitStack() as inner:
            spread_v = buffer(inner, nc, "spread_v", TILES * P)
            with phase(nc, "spread", "summed", "kept") as (spread, summed, kept), nc.Block() as block:
                @block.vector
                def _(dve):
                    nc.vector.tensor_tensor(out=bulk(spread_v[:]), in0=env.ident[:].unsqueeze(1).broadcast_to([P, TILES, P]),
                                            in1=order.end_block[:].unsqueeze(2).broadcast_to([P, TILES, P]), op=ALU.mult).then_inc(spread, 1)

                @block.tensor
                def _(pe):
                    pe.wait_ge(spread, 1)
                    for b, at_col in enumerate(range(0, TILES * P, 512)):
                        width = min(512, TILES * P - at_col)
                        nc.tensor.matmul(env.bank[b][:, 0:width], env.ones[:], spread_v[:, at_col:at_col + width],
                                         start=True, stop=True).then_inc(summed, 1)

                @block.scalar
                def _(act):
                    for b, at_col in enumerate(range(0, TILES * P, 512)):
                        width = min(512, TILES * P - at_col)
                        act.wait_ge(summed, b + 1)
                        nc.scalar.copy(order.end_row[:, at_col:at_col + width], env.bank[b][:, 0:width]).then_inc(kept, 1)


class BySource(Order):
    def place_edges(self, nc, env, place, blk, stp, beside):
        permute(nc, env, blk, stp, env.piece, STEPS, 4, beside, STEPS // SCATTER_GROUP - 18)
        with phase(nc, "step") as (step,), nc.Block() as block:
            @block.vector
            def _(dve):
                then = counted_steps(dve, step)
                then(nc.vector.tensor_copy(env.tmp[:], env.bank[1][:, 0:STEPS]))
                then(nc.vector.scalar_tensor_tensor(out=self.row[:], in0=env.bank[0][:, 0:STEPS], scalar=256.0, in1=env.tmp[:],
                                                    op0=ALU.mult, op1=ALU.add))


class ByTarget(Order):
    def __init__(self, stack, nc, name):
        super().__init__(stack, nc, name)
        self.node = buffer(stack, nc, f"{name}_node", STEPS, I32)
        self.source = buffer(stack, nc, f"{name}_source", STEPS, I32)
        self.weight = buffer(stack, nc, f"{name}_weight", STEPS)
        self.inverse = buffer(stack, nc, f"{name}_inverse", TILES)
        self.root_inverse = buffer(stack, nc, f"{name}_root_inverse", TILES)

    def place_edges(self, nc, env, place, blk, stp, beside):
        with phase(nc, "step") as (step,), nc.Block() as block:
            @block.vector
            def _(dve):
                counted_steps(dve, step)(nc.vector.tensor_copy(self.scatter.place[:], place[:]))

    def take(self, nc, env):
        with phase(nc, "loaded", "step", "rooted") as (loaded, step, rooted), nc.Block() as block:
            records = self.scatter.records

            @block.sync
            def _(sp):
                sp.dma_start(records[:], self.scatter.dram.rearrange("(p t) c -> p (t c)", t=STEPS)).then_inc(loaded, 16)

            @block.vector
            def _(dve):
                then = counted_steps(dve, step)
                then(nc.vector.tensor_scalar(out=self.inverse[:], in0=self.count[:], scalar1=1.0, scalar2=None, op0=ALU.add))
                then(nc.vector.reciprocal(self.inverse[:], self.inverse[:]))
                dve.wait_ge(loaded, 16)
                then(nc.vector.tensor_copy(self.row[:], records[:].rearrange("p (t c) -> p t c", c=2)[:, :, 0]))
                then(nc.vector.tensor_copy(self.weight[:], records[:].rearrange("p (t c) -> p t c", c=2)[:, :, 1]))
                then(nc.vector.tensor_single_scalar(self.source[:], self.row[:], 4, op=ALU.logical_shift_right))

            @block.scalar
            def _(act):
                act.wait_ge(step, 2)
                nc.scalar.activation(self.root_inverse[:], self.inverse[:], ACT.Sqrt).then_inc(rooted, 1)


def shared(stack, nc):
    env = Env()

    def sb(name, cols, dt=FP32):
        return buffer(stack, nc, name, cols, dt)
    env.bank = [stack.enter_context(nc.psum_tensor(f"bank{i}", [P, 512], FP32)) for i in range(8)]
    env.ident, env.ident16, env.ones = sb("ident", P), sb("ident16", P, BF16), sb("ones", P)
    env.after, env.before = sb("after", P), sb("before", P)
    env.iota_p, env.iota_steps, env.own = sb("iota_p", P, BF16), sb("iota_steps", STEPS, FP16), sb("own", 1)
    env.iota_a1, env.inv_a1 = sb("iota_a1", TILES), sb("inv_a1", TILES)
    env.tmp = sb("tmp", STEPS)
    return env


def edge_buffers(stack, nc, env):
    env.col_a1, env.col_b = buffer(stack, nc, "col_a1", STEPS), buffer(stack, nc, "col_b", STEPS)


def ring_use(i, h, chunk, chunks, banks):
    at = h * chunks + chunk
    return at % banks, i * (2 * chunks // banks) + at // banks


def pairs(engine, body):
    body(0, 0)
    body(0, 1)
    with engine.Fori(1, TILES // 2) as i:
        body(i, 0)
        body(i, 1)
    body(TILES // 2, 0)


def project(nc, env, x, w, cols, chunks, stores, banks):
    n = len(chunks)
    with ExitStack() as stack:
        staged_x = [buffer(stack, nc, "staged_x", D) for _ in range(2)]
        xt = [buffer(stack, nc, "xt", D) for _ in range(2)]
        names = ["staged", "turned", "copied", "projected", "held"] + [f"filled{b}" for b in range(banks)] \
            + [f"read{b}" for b in range(banks)] + ["stored0", "stored1"]
        with phase(nc, *names) as sems, nc.Block() as block:
            staged, turned, copied, projected, held = sems[:5]
            filled, read, stored = sems[5:5 + banks], sems[5 + banks:5 + 2 * banks], sems[5 + 2 * banks:]

            @block.gpsimd
            def _(pool):
                def stage(i, h):
                    if not isinstance(i, int) or i > 0:
                        pool.wait_ge(turned, 2 * i + h - 1)
                        pool.sem_inc(held, 1)
                    pool.tensor_copy(staged_x[h][:], x[:, bass.ds((2 * i + h) * D, D)]).then_inc(staged, 1)
                pairs(pool, stage)

            @block.tensor
            def _(pe):
                def turn(i, h):
                    pe.wait_ge(staged, 2 * i + h + 1)
                    pe.sem_inc(held, 1)
                    if not isinstance(i, int) or i > 0:
                        pe.wait_ge(copied, 2 * i + h - 1)
                        pe.sem_inc(held, 1)
                    for s in range(2):
                        last = nc.tensor.transpose(env.bank[6 + h][:, s * P:(s + 1) * P], staged_x[h][:, s * P:(s + 1) * P], env.ident[:])
                    last.then_inc(turned, 1)

                def multiply(i, h):
                    pe.wait_ge(copied, 2 * i + h + 1)
                    pe.sem_inc(held, 1)
                    for c, (at, width, _, _) in enumerate(chunks):
                        b, uses = ring_use(i, h, c, n, banks)
                        if not isinstance(uses, int) or uses > 0:
                            pe.wait_ge(read[b], uses)
                            pe.sem_inc(held, 1)
                        nc.tensor.matmul(env.bank[b][:, 0:width], xt[h][:, 0:P], w[:, at:at + width], start=True, stop=False)
                        nc.tensor.matmul(env.bank[b][:, 0:width], xt[h][:, P:], w[:, cols + at:cols + at + width],
                                         start=False, stop=True).then_inc(filled[b], 1)

                turn(0, 0)
                turn(0, 1)
                multiply(0, 0)
                with pe.Fori(1, TILES // 2) as i:
                    turn(i, 0)
                    multiply(i - 1, 1)
                    turn(i, 1)
                    multiply(i, 0)
                turn(TILES // 2, 0)
                multiply(TILES // 2 - 1, 1)
                multiply(TILES // 2, 0)

            def consume(engine, name, i, h):
                first_tile = isinstance(i, int) and i == 0
                if stores and not first_tile:
                    engine.wait_ge(stored[h], i * (16 * len(stores)))
                    engine.sem_inc(held, 1)
                for c, (_, width, who, use) in enumerate(chunks):
                    if who == name:
                        b, uses = ring_use(i, h, c, n, banks)
                        engine.wait_ge(filled[b], uses + 1)
                        engine.sem_inc(held, 1)
                        use(engine, i, h, env.bank[b][:, 0:width], lambda cc: after(engine, i, h, cc)).then_inc(read[b], 1)

            def after(engine, i, h, c):
                b, uses = ring_use(i, h, c, n, banks)
                engine.wait_ge(read[b], uses + 1)
                engine.sem_inc(held, 1)

            @block.vector
            def _(dve):
                pairs(dve, lambda i, h: consume(dve, "vector", i, h))

            @block.scalar
            def _(act):
                def body(i, h):
                    act.wait_ge(turned, 2 * i + h + 1)
                    act.sem_inc(held, 1)
                    if not isinstance(i, int) or i > 0:
                        b, uses = ring_use(i - 1, h, n - 1, n, banks)
                        act.wait_ge(filled[b], uses + 1)
                        act.sem_inc(held, 1)
                    nc.scalar.copy(xt[h][:], env.bank[6 + h][:, 0:D]).then_inc(copied, 1)
                    if not (isinstance(i, int) and i == 0 and h == 0):
                        back = (i, 0) if h else (i - 1, 1)
                        consume(act, "scalar", *back)
                pairs(act, body)
                consume(act, "scalar", TILES // 2, 0)

            @block.sync
            def _(sp):
                def body(i, h):
                    for needs, dram, sbuf in stores:
                        for c in needs:
                            after(sp, i, h, c)
                        sp.dma_start(dram(2 * i + h), sbuf(h)).then_inc(stored[h], 16)
                pairs(sp, body)
                for h in range(2):
                    if stores:
                        sp.wait_ge(stored[h], 16 * len(stores) * (TILES // 2 + (1 - h)))


def edge_pass(nc, env, order, table, states, fold, tail):
    with ExitStack() as stack:
        index = [buffer(stack, nc, "index", GROUP, I32) for _ in range(RING)]
        rows = [buffer(stack, nc, "rows", GROUP * D) for _ in range(RING)]
        state = [buffer(stack, nc, "state", GROUP * D) for _ in range(RING)]
        rounds = GROUPS // RING
        marks, op0, op1, start = (order.anew, ALU.add, ALU.max, NEG) if fold == "max" else (order.keep, ALU.mult, ALU.add, 0.0)
        index_of = order.source if fold == "sum" else order.row
        names = ["indexed", "weighed", "chain", "held"] + [f"gathered{b}" for b in range(RING)] + [f"stored{b}" for b in range(RING)]
        with phase(nc, *names) as sems, nc.Block() as block:
            indexed, weighed, chain, held = sems[:4]
            gathered, stored = sems[4:4 + RING], sems[4 + RING:]

            @block.gpsimd
            def _(pool):
                def gather(i, h):
                    pool.wait_ge(indexed, RING * i + h + 1)
                    pool.sem_inc(held, 1)
                    for u in range(GROUP):
                        pool.indirect_dma_start(
                            out=rows[h][:, u * D:(u + 1) * D], out_offset=None, in_=table,
                            in_offset=bass.IndirectOffsetOnAxis(ap=index[h][:, u:u + 1], axis=0)).then_inc(gathered[h], 16)
                for h in range(RING):
                    gather(0, h)
                with pool.Fori(1, rounds) as i:
                    for h in range(RING):
                        gather(i, h)

            if fold == "weighted":
                @block.scalar
                def _(act):
                    with act.Fori(0, rounds) as i:
                        for h in range(RING):
                            act.wait_ge(gathered[h], (i + 1) * (16 * GROUP))
                            act.sem_inc(held, 1)
                            for u in range(GROUP):
                                row = rows[h][:, u * D:(u + 1) * D]
                                nc.scalar.activation(row, row, ACT.Copy, scale=order.weight[:, bass.ds((RING * i + h) * GROUP + u, 1)]
                                                     ).then_inc(weighed, 1)

            @block.vector
            def _(dve):
                def look(g, h):
                    nc.vector.tensor_copy(index[h][:], index_of[:, bass.ds(g * GROUP, GROUP)]).then_inc(indexed, 1)

                def fold_group(i, h, more=True):
                    g = RING * i + h
                    dve.wait_ge(gathered[h], (i + 1) * (16 * GROUP))
                    dve.sem_inc(held, 1)
                    if not isinstance(i, int) or i > 0:
                        dve.wait_ge(stored[h], i * 16)
                        dve.sem_inc(held, 1)
                    for u in range(GROUP):
                        before = state[h][:, (u - 1) * D:u * D] if u else state[h - 1][:, (GROUP - 1) * D:]
                        if fold == "weighted":
                            dve.wait_ge(weighed, g * GROUP + u + 1)
                            dve.sem_inc(held, 1)
                        dve.wait_ge(chain, g * GROUP + u + 1)
                        nc.vector.scalar_tensor_tensor(
                            out=state[h][:, u * D:(u + 1) * D], in0=before, scalar=marks[:, bass.ds(g * GROUP + u, 1)],
                            in1=rows[h][:, u * D:(u + 1) * D], op0=op0, op1=op1).then_inc(chain, 1)
                    if more:
                        look(g + RING, h)

                nc.vector.memset(state[RING - 1][:, (GROUP - 1) * D:], start).then_inc(chain, 1)
                for h in range(RING):
                    look(h, h)
                for h in range(RING):
                    fold_group(0, h)
                with dve.Fori(1, rounds - 1) as i:
                    for h in range(RING):
                        fold_group(i, h)
                for h in range(RING):
                    fold_group(rounds - 1, h, more=False)
                dve.wait_ge(chain, STEPS + 1)
                nc.vector.tensor_copy(tail[:], state[RING - 1][:, (GROUP - 1) * D:])

            @block.sync
            def _(sp):
                blocks = states.rearrange("(p t) d -> p (t d)", t=STEPS)
                with sp.Fori(0, rounds) as i:
                    for h in range(RING):
                        sp.wait_ge(chain, (RING * i + h + 1) * GROUP + 1)
                        sp.sem_inc(held, 1)
                        sp.dma_start(blocks[:, bass.ds((RING * i + h) * (GROUP * D), GROUP * D)], state[h][:]).then_inc(stored[h], 16)
                for h in range(RING):
                    sp.wait_ge(stored[h], rounds * 16)


def tile_at(values, a, tiles=1):
    return values[:, a * D:(a + tiles) * D]


class Finish:
    lags = ()
    has_bent = False
    has_total = False

    @property
    def steps(self):
        return len(self.lags)

    def prepare(self, dve, then):
        pass


class FinishRelative(Finish):
    lags, has_bent, has_total = (1,), True, True

    def __init__(self, nc, env, order, own):
        self.nc, self.env, self.order, self.own = nc, env, order, own

    def step(self, out, a, k):
        return self.nc.vector.tensor_tensor(out=tile_at(out, a), in0=tile_at(out, a), in1=tile_at(self.own, a), op=ALU.add)

    def bent(self, out, a):
        return self.nc.scalar.activation(tile_at(out, a), tile_at(out, a), ACT.Relu, scale=self.order.some[:, a:a + 1])

    def total(self, out, a):
        return column_sum(self.nc, self.env, self.env.bank[0], out, a)


class FinishRelational(Finish):
    lags = (1, 2)

    def __init__(self, nc, order, own, bias, y, stats):
        self.nc, self.order, self.own, self.bias, self.y, self.stats = nc, order, own, bias, y, stats

    def prepare(self, dve, then):
        then(self.nc.vector.tensor_tensor(out=bulk(self.own[:]), in0=bulk(self.own[:]), in1=over_tiles(self.bias[:]), op=ALU.add))
        then(self.nc.vector.tensor_tensor(out=self.own[:], in0=self.own[:], in1=self.y[:], op=ALU.add))

    def step(self, out, a, k):
        if k == 0:
            return self.nc.vector.scalar_tensor_tensor(out=tile_at(out, a), in0=tile_at(out, a), scalar=self.order.inverse[:, a:a + 1],
                                                       in1=tile_at(self.own, a), op0=ALU.mult, op1=ALU.add)
        return self.nc.vector.bn_stats(self.stats[:, a * 6:(a + 1) * 6], tile_at(out, a))


class FinishNormalised(Finish):
    lags, has_bent = (1, 4, 5), True

    def __init__(self, nc, order, own, bias, x, stats):
        self.nc, self.order, self.own, self.bias, self.x, self.stats = nc, order, own, bias, x, stats

    def prepare(self, dve, then):
        then(self.nc.vector.tensor_tensor(out=bulk(self.own[:]), in0=bulk(self.own[:]), in1=over_row(self.order.root_inverse[:]), op=ALU.mult))
        then(self.nc.vector.tensor_tensor(out=bulk(self.own[:]), in0=bulk(self.own[:]), in1=over_tiles(self.bias[:]), op=ALU.add))

    def step(self, out, a, k):
        tile = tile_at(out, a)
        if k == 0:
            return self.nc.vector.scalar_tensor_tensor(out=tile, in0=tile, scalar=self.order.root_inverse[:, a:a + 1],
                                                       in1=tile_at(self.own, a), op0=ALU.mult, op1=ALU.add)
        if k == 1:
            return self.nc.vector.tensor_tensor(out=tile, in0=tile, in1=tile_at(self.x, a), op=ALU.add)
        return self.nc.vector.bn_stats(self.stats[:, a * 6:(a + 1) * 6], tile)

    def bent(self, out, a):
        return self.nc.scalar.activation(tile_at(out, a), tile_at(out, a), ACT.Relu)


def column_sum(nc, env, bank, values, a):
    valid = P if a < TILES - 1 else LAST
    return nc.tensor.matmul(bank[:, 0:D], env.ones[0:valid, :], values[0:valid, a * D:(a + 1) * D], start=a == 0, stop=a == TILES - 1)


def collect(nc, env, order, states, fold, tail, out, finish):
    with ExitStack() as stack:
        prefix = buffer(stack, nc, "prefix", 2 * (P + 1))
        carry = buffer(stack, nc, "carry", D)
        hot = buffer(stack, nc, "hot", ROWS)
        row, op0, op1, start = (order.shut_row, ALU.add, ALU.max, NEG) if fold == "max" else (order.open_row, ALU.mult, ALU.add, 0.0)
        acts = finish.has_bent
        names = ["turned", "cleared", "scanned", "back", "carried", "marked", "picked", "joined", "step", "curved", "totalled"] \
            + [f"stepped{k}" for k in range(finish.steps)] + [f"gathered{c}" for c in range(TILES // CHUNK)]
        slots = 6

        def slot(a):
            return env.bank[2 + a % slots][:, 0:D]

        with phase(nc, *names) as sems, nc.Block() as block:
            turned, cleared, scanned, back, carried, marked, picked, joined, step, curved, totalled = sems[:11]
            stepped, gathered = sems[11:11 + finish.steps], sems[11 + finish.steps:]

            @block.gpsimd
            def _(pool):
                for a in range(TILES):
                    pool.indirect_dma_start(out=tile_at(out, a), out_offset=None, in_=states,
                                            in_offset=bass.IndirectOffsetOnAxis(ap=order.last[:, a:a + 1], axis=0)
                                            ).then_inc(gathered[a // CHUNK], 16)

            @block.tensor
            def _(pe):
                for s in range(2):
                    last = nc.tensor.transpose(env.bank[0][:, s * P:(s + 1) * P], tail[:, s * P:(s + 1) * P], env.ident[:])
                last.then_inc(turned, 1)
                pe.wait_ge(scanned, 2)
                for s in range(2):
                    last = nc.tensor.transpose(env.bank[1][:, s * P:(s + 1) * P], prefix[:, s * (P + 1):s * (P + 1) + P], env.ident[:])
                last.then_inc(back, 1)
                pe.wait_ge(carried, 1)
                pe.wait_ge(marked, 1)
                for a in range(TILES):
                    if a >= slots:
                        pe.wait_ge(joined, a - slots + 1)
                    nc.tensor.matmul(slot(a), hot[:, a * P:(a + 1) * P], carry[:], start=True, stop=True).then_inc(picked, 1)
                if finish.has_total:
                    for a in range(TILES):
                        pe.wait_ge(curved, a + 1)
                        last = finish.total(out, a)
                    last.then_inc(totalled, 1)

            if acts:
                @block.scalar
                def _(act):
                    for a in range(TILES):
                        act.wait_ge(stepped[0], a + 1)
                        finish.bent(out, a).then_inc(curved, 1)

            @block.vector
            def _(dve):
                then = counted_steps(dve, step)
                nc.vector.memset(prefix[:], start).then_inc(cleared, 1)
                dve.wait_ge(turned, 1)
                dve.wait_ge(cleared, 1)
                for s in range(2):
                    nc.vector.tensor_tensor_scan(
                        out=prefix[:, s * (P + 1) + 1:(s + 1) * (P + 1)], data0=row[:], data1=env.bank[0][:, s * P:(s + 1) * P],
                        initial=start, op0=op0, op1=op1).then_inc(scanned, 1)
                nc.vector.tensor_scalar(out=hot[:], in0=order.end_row[:], scalar1=env.own[:, 0:1], scalar2=None, op0=ALU.is_equal).then_inc(marked, 1)
                dve.wait_ge(back, 1)
                nc.vector.tensor_copy(carry[:], env.bank[1][:, 0:D]).then_inc(carried, 1)
                finish.prepare(dve, then)

                def join(a):
                    if a % CHUNK == 0:
                        dve.wait_ge(gathered[a // CHUNK], 16 * CHUNK)
                    dve.wait_ge(picked, a + 1)
                    own = tile_at(out, a)
                    if fold == "max":
                        nc.vector.scalar_tensor_tensor(out=own, in0=slot(a), scalar=order.stays[:, a:a + 1],
                                                       in1=own, op0=ALU.add, op1=ALU.max).then_inc(joined, 1)
                    else:
                        nc.vector.scalar_tensor_tensor(out=own, in0=own, scalar=order.some[:, a:a + 1],
                                                       in1=slot(a), op0=ALU.mult, op1=ALU.add).then_inc(joined, 1)

                lags = finish.lags
                for a in range(TILES + lags[-1]):
                    if a < TILES:
                        join(a)
                    for k, lag in enumerate(lags):
                        if 0 <= a - lag < TILES:
                            if k == 0:
                                dve.wait_ge(joined, a - lag + 1)
                            elif acts and k == 1:
                                dve.wait_ge(curved, a - lag + 1)
                            else:
                                dve.wait_ge(stepped[k - 1], a - lag + 1)
                            finish.step(out, a - lag, k).then_inc(stepped[k], 1)


def over_tiles(row, tiles=TILES):
    return row.unsqueeze(1).broadcast_to([P, tiles, D])


def over_row(column):
    return column.unsqueeze(2).broadcast_to([P, TILES, D])


def load_nodes(nc, dram, x):
    with phase(nc, "cleared", "loaded") as (cleared, loaded), nc.Block() as block:
        @block.vector
        def _(dve):
            nc.vector.memset(x[:, (TILES - 1) * D:], 0.0).then_inc(cleared, 1)

        @block.sync
        def _(sp):
            sp.dma_start(bulk(x[:, 0:(TILES - 1) * D], TILES - 1),
                         dram[0:(TILES - 1) * P, :].rearrange("(a p) d -> p a d", p=P)).then_inc(loaded, 16)
            sp.wait_ge(cleared, 1)
            sp.dma_start(x[0:LAST, (TILES - 1) * D:], dram[(TILES - 1) * P:N, :]).then_inc(loaded, 16)
            sp.wait_ge(loaded, 32)


def store_nodes(nc, x, dram):
    with phase(nc, "stored") as (stored,), nc.Block() as block:
        @block.sync
        def _(sp):
            sp.dma_start(dram[0:(TILES - 1) * P, :].rearrange("(a p) d -> p a d", p=P),
                         bulk(x[:, 0:(TILES - 1) * D], TILES - 1)).then_inc(stored, 16)
            sp.dma_start(dram[(TILES - 1) * P:N, :], x[0:LAST, (TILES - 1) * D:]).then_inc(stored, 16)
            sp.wait_ge(stored, 32)


def load_all(nc, *loads):
    with phase(nc, "loaded") as (loaded,), nc.Block() as block:
        @block.sync
        def _(sp):
            for tile, dram in loads:
                sp.dma_start(tile, dram).then_inc(loaded, 16)
            sp.wait_ge(loaded, 16 * len(loads))


def halves(w, cols):
    return w[:].rearrange("p (s o) -> p s o", s=2)


def by_halves(dram):
    return dram.rearrange("(s p) o -> p s o", p=P)


def spread(dram):
    return dram.partition_broadcast(P)


def row_norm(nc, x, out, gain=None, shift=None, relu=False, stats=None):
    with ExitStack() as stack:
        given = stats is not None
        if not given:
            stats = buffer(stack, nc, "stats", TILES * 6)
        moments = buffer(stack, nc, "moments", TILES * 2)
        factor, offset = buffer(stack, nc, "factor", TILES), buffer(stack, nc, "offset", TILES)
        chunks = TILES // CHUNK
        by_act = TILES if gain is not None else 2 * CHUNK
        with phase(nc, "variance", "rooted", "step", "ready", "normed", "shaped") as (variance, rooted, step, ready, normed, shaped), \
                nc.Block() as block:
            mom = moments[:].rearrange("p (a m) -> p a m", m=2)

            @block.vector
            def _(dve):
                if not given:
                    for a in range(TILES):
                        nc.vector.bn_stats(stats[:, a * 6:(a + 1) * 6], tile_at(x, a)).then_inc(step, 1)
                for a in range(TILES):
                    if not given:
                        dve.wait_ge(step, a + 1)
                    last = nc.vector.bn_aggr(moments[:, a * 2:(a + 1) * 2], stats[:, a * 6:(a + 1) * 6])
                done = (0 if given else TILES) + 1
                last.then_inc(step, 1)
                dve.wait_ge(step, done)
                nc.vector.tensor_scalar(out=factor[:], in0=mom[:, :, 1], scalar1=EPS, scalar2=None, op0=ALU.add).then_inc(variance, 1)
                dve.wait_ge(rooted, 1)
                nc.vector.reciprocal(factor[:], factor[:]).then_inc(step, 1)
                dve.wait_ge(step, done + 1)
                nc.vector.scalar_tensor_tensor(out=offset[:], in0=mom[:, :, 0], scalar=-1.0, in1=factor[:], op0=ALU.mult, op1=ALU.mult).then_inc(ready, 1)
                for a in range(by_act, TILES):
                    nc.vector.tensor_scalar(out=tile_at(out, a), in0=tile_at(x, a), scalar1=moments[:, 2 * a:2 * a + 1],
                                            scalar2=factor[:, a:a + 1], op0=ALU.subtract, op1=ALU.mult)
                if gain is not None:
                    for c in range(chunks):
                        part = bulk(tile_at(out, c * CHUNK, CHUNK), CHUNK)
                        dve.wait_ge(normed, (c + 1) * CHUNK)
                        nc.vector.tensor_tensor(out=part, in0=part, in1=over_tiles(gain, CHUNK), op=ALU.mult).then_inc(step, 1)
                        dve.wait_ge(step, done + 2 + c)
                        nc.vector.tensor_tensor(out=part, in0=part, in1=over_tiles(shift, CHUNK), op=ALU.add).then_inc(shaped, 1)

            @block.scalar
            def _(act):
                act.wait_ge(variance, 1)
                nc.scalar.activation(factor[:], factor[:], ACT.Sqrt).then_inc(rooted, 1)
                act.wait_ge(ready, 1)

                def rectify(c):
                    act.wait_ge(shaped, c + 1)
                    nc.scalar.activation(tile_at(out, c * CHUNK, CHUNK), tile_at(out, c * CHUNK, CHUNK), ACT.Relu)
                for a in range(by_act):
                    nc.scalar.activation(tile_at(out, a), tile_at(x, a), ACT.Identity, bias=offset[:, a:a + 1],
                                         scale=factor[:, a:a + 1]).then_inc(normed, 1)
                if relu:
                    for c in range(chunks):
                        rectify(c)


def add_all(nc, out, *steps):
    with phase(nc, "step") as (step,), nc.Block() as block:
        @block.vector
        def _(dve):
            then = counted_steps(dve, step)
            for other, op in steps:
                then(nc.vector.tensor_tensor(out=bulk(out[:]), in0=bulk(out[:]), in1=other, op=op))


def relative_layer(nc, env, order, y, best, own, weights, gain, shift, table, states):
    with ExitStack() as stack:
        staged_p = [buffer(stack, nc, "staged_p", D) for _ in range(2)]
        rows_of = table.rearrange("(a p) d -> a p d", p=P)

        def use_p(engine, i, h, bank, after):
            return nc.scalar.copy(staged_p[h][:], bank)

        def use_q(engine, i, h, bank, after):
            return nc.vector.tensor_copy(own[:, bass.ds((2 * i + h) * D, D)], bank)
        project(nc, env, y, weights, 2 * D, [(0, D, "scalar", use_p), (D, D, "vector", use_q)],
                [([0], lambda k: rows_of[bass.ds(k, 1)].squeeze(0) if not isinstance(k, int) else rows_of[k], lambda h: staged_p[h][:])], 4)
    with ExitStack() as stack:
        tail = buffer(stack, nc, "tail", D)
        edge_pass(nc, env, order, table, states, "max", tail)
        collect(nc, env, order, states, "max", tail, best, FinishRelative(nc, env, order, own))
    with ExitStack() as stack:
        mean, scale = buffer(stack, nc, "mean", D), buffer(stack, nc, "scale", D)
        chunks = TILES // CHUNK
        with phase(nc, "centred", "squared", "summed", "variance", "rooted", "step", "shaped") as \
                (centred, squared, summed, variance, rooted, step, shaped), nc.Block() as block:
            @block.vector
            def _(dve):
                then = counted_steps(dve, step)
                then(nc.vector.tensor_scalar(out=mean[:], in0=env.bank[0][:, 0:D], scalar1=1.0 / N, scalar2=None, op0=ALU.mult))
                for c in range(chunks):
                    part = bulk(tile_at(best, c * CHUNK, CHUNK), CHUNK)
                    nc.vector.tensor_tensor(out=part, in0=part, in1=over_tiles(mean[:], CHUNK), op=ALU.subtract).then_inc(centred, 1)
                dve.wait_ge(summed, 1)
                nc.vector.tensor_scalar(out=scale[:], in0=env.bank[1][:, 0:D], scalar1=1.0 / N, scalar2=EPS, op0=ALU.mult, op1=ALU.add).then_inc(variance, 1)
                dve.wait_ge(rooted, 1)
                then(nc.vector.reciprocal(scale[:], scale[:]))
                then(nc.vector.tensor_tensor(out=scale[:], in0=scale[:], in1=gain[:], op=ALU.mult))
                for c in range(chunks):
                    part = bulk(tile_at(best, c * CHUNK, CHUNK), CHUNK)
                    then(nc.vector.tensor_tensor(out=part, in0=part, in1=over_tiles(scale[:], CHUNK), op=ALU.mult))
                    nc.vector.tensor_tensor(out=part, in0=part, in1=over_tiles(shift[:], CHUNK), op=ALU.add).then_inc(shaped, 1)

            @block.tensor
            def _(pe):
                for a in range(TILES):
                    pe.wait_ge(squared, a // CHUNK + 1)
                    last = column_sum(nc, env, env.bank[1], own, a)
                last.then_inc(summed, 1)

            @block.scalar
            def _(act):
                for c in range(chunks):
                    act.wait_ge(centred, c + 1)
                    nc.scalar.activation(tile_at(own, c * CHUNK, CHUNK), tile_at(best, c * CHUNK, CHUNK), ACT.Square).then_inc(squared, 1)
                act.wait_ge(variance, 1)
                nc.scalar.activation(scale[:], scale[:], ACT.Sqrt).then_inc(rooted, 1)
                for c in range(chunks):
                    act.wait_ge(shaped, c + 1)
                    nc.scalar.activation(tile_at(y, c * CHUNK, CHUNK), tile_at(best, c * CHUNK, CHUNK), ACT.Relu)


def relative_block(nc, env, order, y, best, own, theta_dram, phi_dram, gains, shifts, table, states, layers=LAYERS):
    with ExitStack() as stack:
        weights = buffer(stack, nc, "weights", 2 * 2 * D)
        gain, shift = buffer(stack, nc, "gain", D), buffer(stack, nc, "shift", D)
        halves_of = weights[:].rearrange("p (s o) -> p s o", s=2)
        with nc.Fori(0, layers) as layer:
            def of_layer(dram):
                return dram[bass.ds(layer, 1)].squeeze(0)
            load_all(nc, (halves_of[:, :, 0:D], by_halves(of_layer(theta_dram))),
                     (halves_of[:, :, D:], by_halves(of_layer(phi_dram))),
                     (gain[:], spread(of_layer(gains))), (shift[:], spread(of_layer(shifts))))
            with phase(nc, "step") as (step,), nc.Block() as block:
                @block.vector
                def _(dve):
                    nc.vector.tensor_tensor(out=halves_of[:, :, D:], in0=halves_of[:, :, D:], in1=halves_of[:, :, 0:D], op=ALU.subtract).then_inc(step, 1)
                    dve.wait_ge(step, 1)
            relative_layer(nc, env, order, y, best, own, weights, gain, shift, table, states)


def typed_rows(nc, env, y, turned_y, own, inverse, basis_dram, att_dram, root_dram, table):
    pair, banks, slots = 2 * D, 5, 10
    chunks = TYPES // 2
    reads = TILES
    with ExitStack() as stack:
        basis, att = buffer(stack, nc, "basis", BASES * 2 * D), buffer(stack, nc, "att", TYPES * BASES)
        weights = [buffer(stack, nc, "weights", 2 * pair) for _ in range(2)]
        root = buffer(stack, nc, "root", 2 * D)
        staged = [buffer(stack, nc, "staged", pair) for _ in range(slots)]
        names = ["loaded", "root_loaded", "turned", "copied", "mixed", "filled", "read_act", "read_dve", "scaled",
                 "rooted", "joined", "held"] + [f"stored{s}" for s in range(slots)]
        with phase(nc, *names) as sems, nc.Block() as block:
            loaded, root_loaded, turned, copied, mixed, filled, read_act, read_dve, scaled, rooted, joined, held = sems[:12]
            stored = sems[12:]
            last_pair = chunks // 2 - 1

            def first(i):
                return isinstance(i, int) and i == 0

            def over_pairs(engine, body):
                body(0)
                with engine.Fori(1, last_pair) as i:
                    body(i)
                body(last_pair)

            def wait_read(engine, i, m):
                if m >= 0:
                    engine.wait_ge((read_act, read_dve)[m % 2], i * reads + m // 2 + 1)
                    engine.sem_inc(held, 1)

            @block.sync
            def _(sp):
                sp.dma_start(att[:], spread(att_dram.rearrange("r b -> (r b)"))).then_inc(loaded, 16)
                sp.dma_start(basis[:].rearrange("p (b s o) -> p b s o", b=BASES, s=2), basis_dram.rearrange("b (s p) o -> p b s o", p=P)).then_inc(loaded, 16)
                sp.dma_start(halves(root, D), by_halves(root_dram)).then_inc(root_loaded, 16)
                rows_of = table.rearrange("(a p r) o -> a p (r o)", p=P, r=TYPES)

                def body(i):
                    for h in range(2):
                        for a in range(TILES):
                            m = h * TILES + a
                            wait_read(sp, i, m)
                            sp.dma_start(rows_of[a][:, bass.ds((2 * i + h) * pair, pair)], staged[m % slots][:]).then_inc(stored[m % slots], 16)
                with sp.Fori(0, chunks // 2) as i:
                    body(i)
                for s in range(slots):
                    sp.wait_ge(stored[s], 16 * (chunks * TILES // slots))
                sp.wait_ge(root_loaded, 16)

            @block.tensor
            def _(pe):
                for a in range(TILES):
                    if a >= banks:
                        pe.wait_ge(copied, a - banks + 1)
                    for s in range(2):
                        last = nc.tensor.transpose(env.bank[a % banks][:, s * P:(s + 1) * P], y[:, a * D + s * P:a * D + (s + 1) * P], env.ident[:])
                    last.then_inc(turned, 1)
                pe.wait_ge(copied, TILES)
                pe.wait_ge(root_loaded, 16)

                def body(i):
                    final = isinstance(i, int) and i == last_pair
                    for h in range(2):
                        pe.wait_ge(mixed, (2 * i + h + 1) * (2 * BASES))
                        pe.sem_inc(held, 1)
                        for a in range(TILES):
                            m = h * TILES + a
                            bank = env.bank[a % banks]
                            if m >= banks:
                                wait_read(pe, i, m - banks)
                            elif not first(i):
                                wait_read(pe, i - 1, m - banks + 2 * TILES)
                            if final and h == 1 and a >= banks:
                                pe.wait_ge(scaled, a - banks + 1)
                            for s in range(2):
                                last = nc.tensor.matmul(bank[:, 0:pair], turned_y[:, a * D + s * P:a * D + (s + 1) * P],
                                                        weights[h][:, s * pair:(s + 1) * pair], start=s == 0, stop=s == 1)
                            last.then_inc(filled, 1)
                            if final and h == 1:
                                if a >= 2:
                                    pe.wait_ge(joined, a - 1)
                                for s in range(2):
                                    last = nc.tensor.matmul(env.bank[banks + a % 2][:, 0:D], turned_y[:, a * D + s * P:a * D + (s + 1) * P],
                                                            root[:, s * D:(s + 1) * D], start=s == 0, stop=s == 1)
                                last.then_inc(rooted, 1)
                over_pairs(pe, body)

            def copy_out(engine, copy, read, i, h, a):
                m = h * TILES + a
                engine.wait_ge(filled, i * (2 * TILES) + m + 1)
                engine.sem_inc(held, 1)
                if m >= slots or not first(i):
                    engine.wait_ge(stored[m % slots], (i * (2 * TILES // slots) + m // slots) * 16)
                    engine.sem_inc(held, 1)
                copy(staged[m % slots][:], env.bank[a % banks][:, 0:pair]).then_inc(read, 1)

            @block.scalar
            def _(act):
                for a in range(TILES):
                    act.wait_ge(turned, a + 1)
                    nc.scalar.copy(tile_at(turned_y, a), env.bank[a % banks][:, 0:D]).then_inc(copied, 1)

                def body(i):
                    for m in range(0, 2 * TILES, 2):
                        copy_out(act, nc.scalar.copy, read_act, i, m // TILES, m % TILES)
                over_pairs(act, body)

            @block.vector
            def _(dve):
                def mix(c, h, k):
                    b, r = k // 2, k % 2
                    if k == 0 and not isinstance(c, int) or isinstance(c, int) and c >= 2 and k == 0:
                        dve.wait_ge(filled, (c - 1) * TILES)
                        dve.sem_inc(held, 1)
                    w_r = weights[h][:].rearrange("p (s o) -> p s o", s=2)[:, :, r * D:(r + 1) * D]
                    basis_b = basis[:, b * 2 * D:(b + 1) * 2 * D].rearrange("p (s o) -> p s o", s=2)
                    factor = att[:, bass.ds(c * (2 * BASES) + r * BASES + b, 1)]
                    if b == 0:
                        nc.vector.tensor_scalar(out=w_r, in0=basis_b, scalar1=factor, scalar2=None, op0=ALU.mult).then_inc(mixed, 1)
                    else:
                        dve.wait_ge(mixed, c * (2 * BASES) + k - 1)
                        nc.vector.scalar_tensor_tensor(out=w_r, in0=basis_b, scalar=factor, in1=w_r,
                                                       op0=ALU.mult, op1=ALU.add).then_inc(mixed, 1)

                def body(i):
                    final = isinstance(i, int) and i == last_pair
                    for h in range(2):
                        ahead = iter(range(0 if final and h == 1 else 2 * BASES))
                        for a in range(TILES):
                            if (h * TILES + a) % 2:
                                copy_out(dve, nc.vector.tensor_copy, read_dve, i, h, a)
                                for k in itertools.islice(ahead, 2):
                                    mix(2 * i + h + 1, 1 - h, k)
                            if final and h == 1:
                                wait_read(dve, i, TILES + a)
                                nc.vector.tensor_scalar(out=tile_at(own, a), in0=env.bank[a % banks][:, D:pair], scalar1=inverse[:, a:a + 1],
                                                        scalar2=None, op0=ALU.mult).then_inc(scaled, 1)
                                dve.wait_ge(rooted, a + 1)
                                dve.wait_ge(scaled, a + 1)
                                nc.vector.tensor_tensor(out=tile_at(own, a), in0=tile_at(own, a), in1=env.bank[banks + a % 2][:, 0:D],
                                                        op=ALU.add).then_inc(joined, 1)
                dve.wait_ge(loaded, 32)
                for k in range(2 * BASES):
                    mix(0, 0, k)
                over_pairs(dve, body)


def relational_layer(nc, env, order, y, out, own, basis_dram, att_dram, root_dram, bias_dram, gain_dram, shift_dram,
                     table, states):
    typed_rows(nc, env, y, out, own, order.inverse, basis_dram, att_dram, root_dram, table)
    with ExitStack() as stack:
        tail = buffer(stack, nc, "tail", D)
        bias, gain, shift = (buffer(stack, nc, n, D) for n in ("bias", "gain", "shift"))
        load_all(nc, (bias[:], spread(bias_dram)), (gain[:], spread(gain_dram)), (shift[:], spread(shift_dram)))
        edge_pass(nc, env, order, table, states, "weighted", tail)
        stats = buffer(stack, nc, "stats", TILES * 6)
        collect(nc, env, order, states, "weighted", tail, out, FinishRelational(nc, order, own, bias, y, stats))
        row_norm(nc, out, y, gain[:], shift[:], relu=True, stats=stats)


def normalised_layer(nc, env, order, x, out, own, w_dram, bias_dram, table, states):
    with ExitStack() as stack:
        weights, bias, tail = buffer(stack, nc, "weights", 2 * D), buffer(stack, nc, "bias", D), buffer(stack, nc, "tail", D)
        staged = [buffer(stack, nc, "staged", D) for _ in range(2)]
        root = order.root_inverse
        load_all(nc, (halves(weights, D), by_halves(w_dram)), (bias[:], spread(bias_dram)))
        rows_of = table.rearrange("(a p) d -> a p d", p=P)

        def use_own(engine, i, h, bank, after):
            return nc.vector.tensor_scalar(out=own[:, bass.ds((2 * i + h) * D, D)], in0=bank,
                                           scalar1=root[:, bass.ds(2 * i + h, 1)], scalar2=None, op0=ALU.mult)

        def use_staged(engine, i, h, bank, after):
            return nc.scalar.activation(staged[h][:], bank, ACT.Copy, scale=root[:, bass.ds(2 * i + h, 1)])
        project(nc, env, x, weights, D, [(0, D, "vector", use_own), (0, D, "scalar", use_staged)],
                [([1], lambda k: rows_of[bass.ds(k, 1)].squeeze(0), lambda h: staged[h][:])], 4)
        edge_pass(nc, env, order, table, states, "sum", tail)
        stats = buffer(stack, nc, "stats", TILES * 6)
        collect(nc, env, order, states, "sum", tail, out, FinishNormalised(nc, order, own, bias, x, stats))
        row_norm(nc, out, x, stats=stats)


WIDE = HEADS * (DH + 1)
STATE = WIDE + HEADS
QV = D + WIDE
FEW = 8


def by_head(ap, rows=1):
    return ap.rearrange("p (h d) -> p h d", d=DH + 1)


def attention_pass(nc, env, order, qv_table, k_table, states, tail, spare):
    with ExitStack() as stack:
        def ring(name, cols, count=RING, dt=FP32):
            return [buffer(stack, nc, name, cols, dt) for _ in range(count)]
        index, qv, k = ring("index", 2 * FEW, dt=I32), ring("qv", FEW * QV), ring("k", FEW * D)
        lent = spare[:].shape[1] // (FEW * STATE)
        state = [spare[:, b * FEW * STATE:(b + 1) * FEW * STATE] for b in range(lent)] + ring("state", FEW * STATE, RING - lent)
        top, score, power = ring("top", (FEW + 1) * HEADS), ring("score", FEW * HEADS), ring("power", 2 * FEW * HEADS)
        groups = STEPS // FEW
        body = groups // RING
        names = ["indexed", "scores", "topped", "differed", "raised", "chain", "marked", "held", "cleared", "copied"] \
            + [f"gathered{b}" for b in range(RING)] + [f"stored{b}" for b in range(RING)]
        with phase(nc, *names) as sems, nc.Block() as block:
            indexed, scores, topped, differed, raised, chain, marked, held, cleared, copied = sems[:10]
            gathered, stored = sems[10:10 + RING], sems[10 + RING:]

            def first(i):
                return isinstance(i, int) and i == 0

            @block.gpsimd
            def _(pool):
                def gather(i, b):
                    g = RING * i + b
                    pool.wait_ge(indexed, g + 1)
                    pool.sem_inc(held, 1)
                    for u in range(FEW):
                        pool.indirect_dma_start(
                            out=qv[b][:, u * QV:(u + 1) * QV], out_offset=None, in_=qv_table,
                            in_offset=bass.IndirectOffsetOnAxis(ap=index[b][:, u:u + 1], axis=0)).then_inc(gathered[b], 16)
                        pool.indirect_dma_start(
                            out=k[b][:, u * D:(u + 1) * D], out_offset=None, in_=k_table,
                            in_offset=bass.IndirectOffsetOnAxis(ap=index[b][:, FEW + u:FEW + u + 1], axis=0)).then_inc(gathered[b], 16)
                for b in range(RING):
                    gather(0, b)
                with pool.Fori(1, body) as i:
                    for b in range(RING):
                        gather(i, b)

            @block.vector
            def _(dve):
                def look(g, b):
                    nc.vector.tensor_copy(index[b][:, 0:FEW], order.source[:, bass.ds(g * FEW, FEW)])
                    nc.vector.tensor_copy(index[b][:, FEW:], order.node[:, bass.ds(g * FEW, FEW)]).then_inc(indexed, 1)

                def multiply_scores(i, b):
                    g = RING * i + b
                    dve.wait_ge(gathered[b], (i + 1) * (2 * FEW * 16))
                    dve.sem_inc(held, 1)
                    q3 = qv[b][:].rearrange("p (u c) -> p u c", u=FEW)[:, :, 0:D]
                    nc.vector.tensor_tensor(out=bulk(k[b][:], FEW), in0=bulk(k[b][:], FEW), in1=q3, op=ALU.mult).then_inc(scores, 1)
                    if not first(i):
                        dve.wait_ge(copied, g - RING + 1)
                        dve.sem_inc(held, 1)
                    dve.wait_ge(scores, 2 * g + 1)
                    nc.vector.tensor_reduce(out=score[b][:], in_=k[b][:].rearrange("p (s d) -> p s d", d=DH), axis=AX.X, op=ALU.add).then_inc(scores, 1)

                def top_step(i, b, u):
                    g = RING * i + b
                    if u == 0:
                        dve.wait_ge(scores, 2 * g + 2)
                        dve.sem_inc(held, 1)
                    dve.wait_ge(topped, (FEW + 1) * g + u + 1)
                    before = top[b][:, u * HEADS:(u + 1) * HEADS] if u else top[b - 1][:, FEW * HEADS:]
                    nc.vector.scalar_tensor_tensor(
                        out=top[b][:, (u + 1) * HEADS:(u + 2) * HEADS], in0=before, scalar=order.anew[:, bass.ds(g * FEW + u, 1)],
                        in1=score[b][:, u * HEADS:(u + 1) * HEADS], op0=ALU.add, op1=ALU.max).then_inc(topped, 1)

                def exponents(i, b):
                    g = RING * i + b
                    nc.vector.tensor_copy(top[b][:, 0:HEADS], top[b - 1][:, FEW * HEADS:]).then_inc(topped, 1)
                    dve.wait_ge(topped, (FEW + 1) * (g + 1) + 1)
                    new = top[b][:, HEADS:]
                    nc.vector.tensor_tensor(out=power[b][:, 0:FEW * HEADS], in0=top[b][:, 0:FEW * HEADS], in1=new, op=ALU.subtract).then_inc(marked, 1)
                    nc.vector.tensor_tensor(out=power[b][:, FEW * HEADS:], in0=score[b][:], in1=new, op=ALU.subtract).then_inc(differed, 1)
                    dve.wait_ge(marked, g + 1)
                    scale = power[b][:, 0:FEW * HEADS].rearrange("p (u h) -> p u h", u=FEW)
                    nc.vector.tensor_tensor(out=scale, in0=scale,
                                            in1=order.anew[:, bass.ds(g * FEW, FEW)].unsqueeze(2).broadcast_to([P, FEW, HEADS]),
                                            op=ALU.add).then_inc(differed, 1)

                def weigh(b, u):
                    value = by_head(qv[b][:, u * QV + D:(u + 1) * QV])
                    nc.vector.tensor_tensor(
                        out=value, in0=value,
                        in1=power[b][:, (FEW + u) * HEADS:(FEW + u + 1) * HEADS].unsqueeze(2).broadcast_to([P, HEADS, DH + 1]),
                        op=ALU.mult).then_inc(chain, 1)

                def steps(scored, folded, more=True):
                    if scored:
                        multiply_scores(*scored)
                    if folded:
                        i, b = folded
                        g = RING * i + b
                        dve.wait_ge(raised, g + 1)
                        dve.sem_inc(held, 1)
                        if not first(i):
                            dve.wait_ge(stored[b], i * 16)
                            dve.sem_inc(held, 1)
                        weigh(b, 0)
                    for u in range(FEW):
                        if folded:
                            before = state[b][:, (u - 1) * STATE:(u - 1) * STATE + WIDE] if u else state[b - 1][:, (FEW - 1) * STATE:(FEW - 1) * STATE + WIDE]
                            now = state[b][:, u * STATE:u * STATE + WIDE]
                            dve.wait_ge(chain, g * (3 * FEW) + 3 * u + 1)
                            nc.vector.tensor_tensor(out=by_head(now), in0=by_head(before),
                                                    in1=power[b][:, u * HEADS:(u + 1) * HEADS].unsqueeze(2).broadcast_to([P, HEADS, DH + 1]),
                                                    op=ALU.mult).then_inc(chain, 1)
                        if scored:
                            top_step(*scored, u)
                        if folded:
                            dve.wait_ge(chain, g * (3 * FEW) + 3 * u + 3)
                            nc.vector.tensor_tensor(out=now, in0=now, in1=qv[b][:, u * QV + D:(u + 1) * QV], op=ALU.add).then_inc(chain, 1)
                            if u < FEW - 1:
                                weigh(b, u + 1)
                    if folded and more:
                        look(g + RING, b)
                    if scored:
                        exponents(*scored)

                nc.vector.memset(state[RING - 1][:, (FEW - 1) * STATE:], 0.0).then_inc(chain, 1)
                nc.vector.memset(top[RING - 1][:, FEW * HEADS:], NEG).then_inc(topped, 1)
                for b in range(RING):
                    look(b, b)
                steps((0, 0), None)
                for b in range(1, RING):
                    steps((0, b), (0, b - 1))
                with dve.Fori(1, body - 1) as i:
                    steps((i, 0), (i - 1, RING - 1))
                    for b in range(1, RING):
                        steps((i, b), (i, b - 1))
                steps((body - 1, 0), (body - 2, RING - 1))
                for b in range(1, RING):
                    steps((body - 1, b), (body - 1, b - 1), more=False)
                steps(None, (body - 1, RING - 1), more=False)
                dve.wait_ge(chain, 3 * STEPS + 1)
                dve.wait_ge(copied, groups)
                nc.vector.tensor_copy(tail[:], state[RING - 1][:, (FEW - 1) * STATE:])

            @block.scalar
            def _(act):
                def raise_group(i, b):
                    g = RING * i + b
                    act.wait_ge(differed, 2 * g + 2)
                    act.sem_inc(held, 1)
                    nc.scalar.activation(power[b][:], power[b][:], ACT.Exp).then_inc(raised, 1)
                    if not first(i):
                        act.wait_ge(stored[b], i * 16)
                        act.sem_inc(held, 1)
                    nc.scalar.copy(state[b][:].rearrange("p (u c) -> p u c", u=FEW)[:, :, WIDE:],
                                   top[b][:, HEADS:].rearrange("p (u h) -> p u h", u=FEW)).then_inc(copied, 1)
                for b in range(RING):
                    raise_group(0, b)
                with act.Fori(1, body) as i:
                    for b in range(RING):
                        raise_group(i, b)

            @block.sync
            def _(sp):
                blocks = states.rearrange("(p t) d -> p (t d)", t=STEPS)
                with sp.Fori(0, body) as i:
                    for b in range(RING):
                        g = RING * i + b
                        sp.wait_ge(chain, (g + 1) * (3 * FEW) + 1)
                        sp.sem_inc(held, 1)
                        sp.wait_ge(copied, g + 1)
                        sp.sem_inc(held, 1)
                        sp.dma_start(blocks[:, bass.ds(g * (FEW * STATE), FEW * STATE)], state[b][:]).then_inc(stored[b], 16)
                for b in range(RING):
                    sp.wait_ge(stored[b], body * 16)


def attention_collect(nc, env, order, states, tail, x):
    third = WIDE // 3
    with ExitStack() as stack:
        def sb(name, cols, dt=FP32):
            return buffer(stack, nc, name, cols, dt)
        own, other = sb("own", TILES * STATE), sb("other", TILES * STATE)
        top_in, rise, fall = sb("top_in", P + 1), sb("rise", P), sb("fall", P)
        spread_heads, factors, prefix = sb("spread_heads", WIDE), sb("factors", 3 * P), sb("prefix", 3 * (P + 1))
        carry, into = sb("carry", STATE), sb("into", HEADS)
        tops, part = sb("tops", 2 * TILES * HEADS), sb("part", TILES * HEADS)
        hot = [sb("hot", P) for _ in range(2)]
        names = ("gathered", "shaped", "turned", "step", "raised", "expanded", "back", "carried", "marked", "picked", "kept", "exped", "held")
        with phase(nc, *names) as (gathered, shaped, turned, step, raised, expanded, back, carried, marked, picked, kept, exped, held), \
                nc.Block() as block:
            @block.gpsimd
            def _(pool):
                pool.memset(spread_heads[0:HEADS, :], 1.0).then_inc(shaped, 1)
                pool.wait_ge(shaped, 1)
                pool.affine_select(out=spread_heads[0:HEADS, :], in_=spread_heads[0:HEADS, :], compare_op=ALU.is_ge, fill=0.0,
                                   base=0, pattern=[[1, WIDE]], channel_multiplier=-(DH + 1)).then_inc(shaped, 1)
                pool.wait_ge(shaped, 2)
                pool.affine_select(out=spread_heads[0:HEADS, :], in_=spread_heads[0:HEADS, :], compare_op=ALU.is_ge, fill=0.0,
                                   base=DH, pattern=[[-1, WIDE]], channel_multiplier=DH + 1).then_inc(shaped, 1)
                for a in range(TILES):
                    pool.indirect_dma_start(out=own[:, a * STATE:(a + 1) * STATE], out_offset=None, in_=states,
                                            in_offset=bass.IndirectOffsetOnAxis(ap=order.last[:, a:a + 1], axis=0)).then_inc(gathered, 16)

            @block.tensor
            def _(pe):
                nc.tensor.transpose(env.bank[0][0:HEADS, 0:P], tail[:, WIDE:], env.ident[:]).then_inc(turned, 1)
                pe.wait_ge(raised, 2)
                pe.wait_ge(shaped, 3)
                nc.tensor.transpose(env.bank[1][:, 0:HEADS], fall[0:HEADS, :], env.ident[0:HEADS, 0:HEADS]).then_inc(expanded, 1)
                nc.tensor.transpose(env.bank[1][:, HEADS:2 * HEADS], top_in[0:HEADS, 0:P], env.ident[0:HEADS, 0:HEADS]).then_inc(expanded, 1)
                for s in range(3):
                    nc.tensor.matmul(env.bank[2][0:third, s * P:(s + 1) * P], spread_heads[0:HEADS, s * third:(s + 1) * third],
                                     rise[0:HEADS, :], start=True, stop=True).then_inc(expanded, 1)
                pe.wait_ge(step, 9)
                for s in range(3):
                    nc.tensor.transpose(env.bank[3][0:third, s * P:(s + 1) * P], tail[:, s * third:(s + 1) * third], env.ident[:]).then_inc(turned, 1)
                pe.wait_ge(step, 12)
                for s in range(3):
                    last = nc.tensor.transpose(env.bank[4][:, s * third:(s + 1) * third], prefix[0:third, s * (P + 1):s * (P + 1) + P],
                                               env.ident[0:third, 0:third])
                last.then_inc(back, 1)
                pe.wait_ge(carried, 2)

                def body(i, h):
                    pe.wait_ge(marked, 2 * i + h + 1)
                    pe.sem_inc(held, 1)
                    if not isinstance(i, int) or i > 0:
                        pe.wait_ge(kept, 2 * i + h - 1)
                        pe.sem_inc(held, 1)
                    nc.tensor.matmul(env.bank[5 + h][:, 0:STATE], hot[h][:], carry[:], start=True, stop=True).then_inc(picked, 1)
                pairs(pe, body)

            @block.scalar
            def _(act):
                act.wait_ge(step, 6)
                nc.scalar.activation(rise[0:HEADS, :], rise[0:HEADS, :], ACT.Exp).then_inc(raised, 1)
                nc.scalar.activation(fall[0:HEADS, :], fall[0:HEADS, :], ACT.Exp).then_inc(raised, 1)

                def body(i, h):
                    act.wait_ge(picked, 2 * i + h + 1)
                    act.sem_inc(held, 1)
                    nc.scalar.copy(other[:, bass.ds((2 * i + h) * STATE, STATE)], env.bank[5 + h][:, 0:STATE]).then_inc(kept, 1)
                pairs(act, body)
                act.wait_ge(step, 16)
                nc.scalar.activation(tops[:], tops[:], ACT.Exp).then_inc(exped, 1)

            @block.vector
            def _(dve):
                nc.vector.memset(top_in[:], NEG).then_inc(step, 1)
                nc.vector.memset(prefix[:], 0.0).then_inc(step, 1)
                dve.wait_ge(turned, 1)
                dve.wait_ge(step, 2)
                nc.vector.tensor_tensor_scan(out=top_in[0:HEADS, 1:], data0=order.shut_row[0:HEADS, :], data1=env.bank[0][0:HEADS, 0:P],
                                             initial=NEG, op0=ALU.add, op1=ALU.max).then_inc(step, 1)
                dve.wait_ge(step, 3)
                nc.vector.tensor_tensor(out=fall[0:HEADS, :], in0=env.bank[0][0:HEADS, 0:P], in1=top_in[0:HEADS, 1:],
                                        op=ALU.subtract).then_inc(step, 1)
                nc.vector.tensor_tensor(out=rise[0:HEADS, :], in0=top_in[0:HEADS, 0:P], in1=top_in[0:HEADS, 1:],
                                        op=ALU.subtract).then_inc(step, 1)
                dve.wait_ge(step, 5)
                nc.vector.tensor_tensor(out=rise[0:HEADS, :], in0=rise[0:HEADS, :], in1=order.shut_row[0:HEADS, :], op=ALU.add).then_inc(step, 1)
                dve.wait_ge(expanded, 5)
                nc.vector.tensor_copy(into[:], env.bank[1][:, 0:HEADS]).then_inc(step, 1)
                nc.vector.tensor_copy(carry[:, WIDE:], env.bank[1][:, HEADS:2 * HEADS]).then_inc(carried, 1)
                nc.vector.tensor_copy(factors[0:third, :], env.bank[2][0:third, 0:3 * P]).then_inc(step, 1)
                dve.wait_ge(step, 8)
                nc.vector.tensor_tensor(out=by_head(tail[:, 0:WIDE]), in0=by_head(tail[:, 0:WIDE]),
                                        in1=into[:].unsqueeze(2).broadcast_to([P, HEADS, DH + 1]), op=ALU.mult).then_inc(step, 1)
                dve.wait_ge(turned, 4)
                for s in range(3):
                    nc.vector.tensor_tensor_scan(out=prefix[0:third, s * (P + 1) + 1:(s + 1) * (P + 1)], data0=factors[0:third, s * P:(s + 1) * P],
                                                 data1=env.bank[3][0:third, s * P:(s + 1) * P], initial=0.0,
                                                 op0=ALU.mult, op1=ALU.add).then_inc(step, 1)
                dve.wait_ge(back, 1)
                nc.vector.tensor_copy(carry[:, 0:WIDE], env.bank[4][:, 0:WIDE]).then_inc(carried, 1)

                def mark(i, h):
                    if not isinstance(i, int) or i > 0:
                        dve.wait_ge(picked, 2 * i + h - 1)
                        dve.sem_inc(held, 1)
                    nc.vector.tensor_scalar(out=hot[h][:], in0=order.end_row[:, bass.ds((2 * i + h) * P, P)],
                                            scalar1=env.own[:, 0:1], scalar2=None, op0=ALU.is_equal).then_inc(marked, 1)
                pairs(dve, mark)
                dve.wait_ge(gathered, 16 * TILES)
                dve.wait_ge(kept, TILES)
                of_tile = lambda t: t.rearrange("p (a c) -> p a c", a=TILES)
                own_top, other_top = of_tile(own[:])[:, :, WIDE:], of_tile(other[:])[:, :, WIDE:]
                own_part, other_part = of_tile(tops[:, 0:TILES * HEADS]), of_tile(tops[:, TILES * HEADS:])
                nc.vector.tensor_tensor(out=other_top, in0=other_top, in1=order.stays[:].unsqueeze(2).broadcast_to([P, TILES, HEADS]),
                                        op=ALU.add).then_inc(step, 1)
                dve.wait_ge(step, 13)
                nc.vector.tensor_tensor(out=of_tile(part[:]), in0=own_top, in1=other_top, op=ALU.max).then_inc(step, 1)
                dve.wait_ge(step, 14)
                nc.vector.tensor_tensor(out=own_part, in0=own_top, in1=of_tile(part[:]), op=ALU.subtract).then_inc(step, 1)
                nc.vector.tensor_tensor(out=other_part, in0=other_top, in1=of_tile(part[:]), op=ALU.subtract).then_inc(step, 1)
                dve.wait_ge(exped, 1)
                for values, scale in ((own, tops[:, 0:TILES * HEADS]), (other, tops[:, TILES * HEADS:])):
                    for a in range(TILES):
                        wide = by_head(values[:, a * STATE:a * STATE + WIDE])
                        last = nc.vector.tensor_tensor(out=wide, in0=wide, in1=scale[:, a * HEADS:(a + 1) * HEADS].unsqueeze(2)
                                                       .broadcast_to([P, HEADS, DH + 1]), op=ALU.mult)
                    last.then_inc(step, 1)
                dve.wait_ge(step, 18)
                nc.vector.tensor_tensor(out=of_tile(own[:])[:, :, 0:WIDE], in0=of_tile(own[:])[:, :, 0:WIDE],
                                        in1=of_tile(other[:])[:, :, 0:WIDE], op=ALU.add).then_inc(step, 1)
                dve.wait_ge(step, 19)
                sums = of_tile(own[:])[:, :, DH:WIDE:DH + 1]
                nc.vector.tensor_scalar(out=of_tile(part[:]), in0=sums, scalar1=0.5, scalar2=None, op0=ALU.max).then_inc(step, 1)
                dve.wait_ge(step, 20)
                nc.vector.reciprocal(part[:], part[:]).then_inc(step, 1)
                dve.wait_ge(step, 21)
                nc.vector.tensor_tensor(out=of_tile(part[:]), in0=of_tile(part[:]),
                                        in1=order.some[:].unsqueeze(2).broadcast_to([P, TILES, HEADS]), op=ALU.mult).then_inc(step, 1)
                dve.wait_ge(step, 22)
                for a in range(TILES):
                    wide = by_head(own[:, a * STATE:a * STATE + WIDE])[:, :, 0:DH]
                    last = nc.vector.tensor_tensor(out=wide, in0=wide, in1=part[:, a * HEADS:(a + 1) * HEADS].unsqueeze(2)
                                                   .broadcast_to([P, HEADS, DH]), op=ALU.mult)
                last.then_inc(step, 1)
                dve.wait_ge(step, 23)
                for a in range(TILES):
                    x_a = x[:, a * D:(a + 1) * D].rearrange("p (h d) -> p h d", h=HEADS)
                    nc.vector.tensor_tensor(out=x_a, in0=x_a, in1=by_head(own[:, a * STATE:a * STATE + WIDE])[:, :, 0:DH], op=ALU.add)


def feed_forward(nc, env, y, out, w_in_dram, b_in_dram, w_out_dram):
    blocks, hidden = TILES // 4, DFF // P
    with ExitStack() as stack:
        def sb(name, cols):
            return buffer(stack, nc, name, cols)
        w_in, w_out, b_in = sb("w_in", 2 * DFF), sb("w_out", hidden * D), sb("b_in", hidden)
        staged_y, yt, ht = sb("staged_y", 4 * D), sb("yt", 2 * 4 * P), sb("ht", hidden * 4 * P)
        load_all(nc, (halves(w_in, DFF), by_halves(w_in_dram)), (w_out[:].rearrange("p (f o) -> p f o", o=D), w_out_dram.rearrange("(f p) o -> p f o", p=P)),
                 (b_in[:], b_in_dram))
        with phase(nc, "staged", "turned", "copied", "made", "bent", "multiplied", "kept", "held") as \
                (staged, turned, copied, made, bent, multiplied, kept, held), nc.Block() as block:
            def over_blocks(engine, body):
                body(0, 4)
                with engine.Fori(1, blocks) as i:
                    body(i, 4)
                body(blocks, TILES - 4 * blocks)

            def later(i):
                return not isinstance(i, int) or i > 0

            @block.gpsimd
            def _(pool):
                def body(i, n):
                    if later(i):
                        pool.wait_ge(turned, 2 * i)
                        pool.sem_inc(held, 1)
                    pool.tensor_copy(staged_y[:, 0:n * D], y[:, bass.ds(i * (4 * D), n * D)]).then_inc(staged, 1)
                over_blocks(pool, body)

            @block.tensor
            def _(pe):
                def body(i, n):
                    pe.wait_ge(staged, i + 1)
                    pe.sem_inc(held, 1)
                    if later(i):
                        pe.wait_ge(copied, 2 * i)
                        pe.sem_inc(held, 1)
                    for s in range(2):
                        for t in range(n):
                            last = nc.tensor.transpose(env.bank[s][:, t * P:(t + 1) * P], staged_y[:, t * D + s * P:t * D + (s + 1) * P], env.ident[:])
                        last.then_inc(turned, 1)
                    pe.wait_ge(copied, 2 * i + 2)
                    pe.sem_inc(held, 1)
                    for f in range(hidden):
                        bank = env.bank[2 + f % 4]
                        if later(i) or f >= 4:
                            pe.wait_ge(bent, i * hidden + f - 3)
                            pe.sem_inc(held, 1)
                        for s in range(2):
                            last = nc.tensor.matmul(bank[:, 0:n * P], w_in[:, s * DFF + f * P:s * DFF + (f + 1) * P],
                                                    yt[:, s * 4 * P:s * 4 * P + n * P], start=s == 0, stop=s == 1)
                        last.then_inc(made, 1)
                    pe.wait_ge(bent, (i + 1) * hidden)
                    pe.sem_inc(held, 1)
                    for t in range(n):
                        if later(i) or t >= 2:
                            pe.wait_ge(kept, 4 * i + t - 1)
                            pe.sem_inc(held, 1)
                        for f in range(hidden):
                            last = nc.tensor.matmul(env.bank[6 + t % 2][:, 0:D], ht[:, (f * 4 + t) * P:(f * 4 + t + 1) * P],
                                                    w_out[:, f * D:(f + 1) * D], start=f == 0, stop=f == hidden - 1)
                        last.then_inc(multiplied, 1)
                over_blocks(pe, body)

            @block.scalar
            def _(act):
                def body(i, n):
                    if later(i):
                        act.wait_ge(multiplied, 4 * i)
                        act.sem_inc(held, 1)
                    for f in range(hidden):
                        act.wait_ge(made, i * hidden + f + 1)
                        act.sem_inc(held, 1)
                        nc.scalar.activation(ht[:, f * 4 * P:f * 4 * P + n * P], env.bank[2 + f % 4][:, 0:n * P], ACT.Gelu,
                                             bias=b_in[:, f:f + 1]).then_inc(bent, 1)
                over_blocks(act, body)

            @block.vector
            def _(dve):
                def body(i, n):
                    if later(i):
                        dve.wait_ge(made, i * hidden)
                        dve.sem_inc(held, 1)
                    for s in range(2):
                        dve.wait_ge(turned, 2 * i + s + 1)
                        dve.sem_inc(held, 1)
                        nc.vector.tensor_copy(yt[:, s * 4 * P:s * 4 * P + n * P], env.bank[s][:, 0:n * P]).then_inc(copied, 1)
                    for t in range(n):
                        dve.wait_ge(multiplied, 4 * i + t + 1)
                        dve.sem_inc(held, 1)
                        nc.vector.tensor_copy(out[:, bass.ds((4 * i + t) * D, D)], env.bank[6 + t % 2][:, 0:D]).then_inc(kept, 1)
                over_blocks(dve, body)


def attention_layer(nc, env, order, x, y, given, qv_table, k_table, states):
    w_qkv, b_qkv, attn_gain, attn_shift, res_gain, res_shift, w_in, b_in, w_out, b_out = given
    with ExitStack() as stack:
        weights, bias = buffer(stack, nc, "weights", 2 * 3 * D), buffer(stack, nc, "bias", 3 * D)
        gain, shift = buffer(stack, nc, "gain", D), buffer(stack, nc, "shift", D)
        load_all(nc, (halves(weights, 3 * D), by_halves(w_qkv)), (bias[:], spread(b_qkv)), (gain[:], spread(attn_gain)), (shift[:], spread(attn_shift)))
        row_norm(nc, x, y, gain[:], shift[:])
        staged_qv = [buffer(stack, nc, "staged_qv", QV) for _ in range(2)]
        staged_k = [buffer(stack, nc, "staged_k", D) for _ in range(2)]
        scale = float(D) ** -0.5
        with phase(nc, "step") as (step,), nc.Block() as block:
            @block.vector
            def _(dve):
                nc.vector.tensor_scalar(out=bias[:, 0:D], in0=bias[:, 0:D], scalar1=scale, scalar2=None, op0=ALU.mult).then_inc(step, 1)
                for h in range(2):
                    nc.vector.memset(staged_qv[h][:], 1.0).then_inc(step, 1)
                dve.wait_ge(step, 3)

        def use_q(engine, i, h, bank, after):
            return nc.vector.scalar_tensor_tensor(out=staged_qv[h][:, 0:D], in0=bank, scalar=scale, in1=bias[:, 0:D], op0=ALU.mult, op1=ALU.add)

        def use_k(engine, i, h, bank, after):
            return nc.vector.tensor_tensor(out=staged_k[h][:], in0=bank, in1=bias[:, D:2 * D], op=ALU.add)

        def use_v(engine, i, h, bank, after):
            return nc.vector.tensor_tensor(out=by_head(staged_qv[h][:, D:])[:, :, 0:DH], in0=bank.rearrange("p (h d) -> p h d", h=HEADS),
                                           in1=bias[:, 2 * D:].rearrange("p (h d) -> p h d", h=HEADS), op=ALU.add)
        qv_of, k_of = (t.rearrange("(a p) d -> a p d", p=P) for t in (qv_table, k_table))
        project(nc, env, y, weights, 3 * D, [(0, D, "vector", use_q), (D, D, "vector", use_k), (2 * D, D, "vector", use_v)],
                [([0, 2], lambda k: qv_of[bass.ds(k, 1)].squeeze(0), lambda h: staged_qv[h][:]),
                 ([1], lambda k: k_of[bass.ds(k, 1)].squeeze(0), lambda h: staged_k[h][:])], 6)
    with ExitStack() as stack:
        tail = buffer(stack, nc, "tail", STATE)
        attention_pass(nc, env, order, qv_table, k_table, states, tail, y)
        with phase(nc, "copied") as (copied,), nc.Block() as block:
            @block.vector
            def _(dve):
                nc.vector.tensor_copy(y[:], x[:]).then_inc(copied, 1)
                dve.wait_ge(copied, 1)
        attention_collect(nc, env, order, states, tail, y)
    with ExitStack() as stack:
        gain, shift, bias = (buffer(stack, nc, n, D) for n in ("gain", "shift", "bias"))
        hidden_in, hidden_out = buffer(stack, nc, "hidden_in", TILES * D), buffer(stack, nc, "hidden_out", TILES * D)
        load_all(nc, (gain[:], spread(res_gain)), (shift[:], spread(res_shift)), (bias[:], spread(b_out)))
        row_norm(nc, y, hidden_in, gain[:], shift[:])
        feed_forward(nc, env, hidden_in, hidden_out, w_in, b_in, w_out)
        add_all(nc, hidden_out, (over_tiles(bias[:]), ALU.add), (bulk(y[:]), ALU.add), (bulk(x[:]), ALU.add))
        row_norm(nc, hidden_out, x)


NAMES = ["x", "src", "dst", "edge_type_16", "edge_weight", "L0_gnn_thetas", "L0_gnn_phis", "L0_gnn_gammas", "L0_gnn_betas",
         "L1_gnn_basis1", "L1_gnn_att1", "L1_gnn_root1", "L1_gnn_bias1", "L1_gnn_ln1_g", "L1_gnn_ln1_b",
         "L1_gnn_basis2", "L1_gnn_att2", "L1_gnn_root2", "L1_gnn_bias2", "L1_gnn_ln2_g", "L1_gnn_ln2_b",
         "L2_gnn_W", "L2_gnn_b", "L3_gnn_Wqkv", "L3_gnn_bqkv", "L3_gnn_ln_attn_g", "L3_gnn_ln_attn_b",
         "L3_gnn_ln_res_g", "L3_gnn_ln_res_b", "L3_gnn_W_in", "L3_gnn_b_in", "L3_gnn_W_out", "L3_gnn_b_out"]


def graph_program(nc, given, out):
    def scratch(name, rows, cols):
        return nc.dram_tensor(name, (rows, cols), FP32, kind="Internal").ap()
    states = scratch("states", SLOTS, D)
    wide_states = scratch("wide_states", SLOTS, STATE)
    table, typed_table = scratch("table", ROWS, D), scratch("typed_table", ROWS * TYPES, D)
    qv_table, k_table = scratch("qv_table", ROWS, QV), scratch("k_table", ROWS, D)
    with ExitStack() as stack:
        env = shared(stack, nc)
        constants(nc, env)
        by_source, by_target = BySource(stack, nc, "by_source"), ByTarget(stack, nc, "by_target")
        with ExitStack() as inner:
            env.records = buffer(inner, nc, "records", 2 * STEPS)
            by_target.scatter = scatter = Scatter(inner, nc, env.records, scratch("records_sorted", SLOTS, 2))
            edge_buffers(inner, nc, env)
            edge_columns(nc, env, given["dst"], given["src"], given["edge_type_16"], given["edge_weight"])
            edge_order(nc, env, by_target, NOTHING)
            env.piece = [buffer(inner, nc, f"piece{i}", STEPS) for i in range(2)]
            edge_columns(nc, env, given["src"], given["dst"])
            edge_order(nc, env, by_source, scatter)
            by_target.take(nc, env)
        by_source.spread_ends(stack, nc, env)
        by_target.spread_ends(stack, nc, env)
        x, y = buffer(stack, nc, "x", TILES * D), buffer(stack, nc, "y", TILES * D)
        load_nodes(nc, given["x"], x)
        with ExitStack() as inner:
            out_of, own = buffer(inner, nc, "out_of", TILES * D), buffer(inner, nc, "own", TILES * D)

            def copy_x():
                with phase(nc, "copied") as (copied,), nc.Block() as block:
                    @block.vector
                    def _(dve):
                        nc.vector.tensor_copy(y[:], x[:]).then_inc(copied, 1)
                        dve.wait_ge(copied, 1)

            def join():
                add_all(nc, y, (bulk(x[:]), ALU.add))
                row_norm(nc, y, x)
            copy_x()
            relative_block(nc, env, by_source, y, out_of, own, given["L0_gnn_thetas"], given["L0_gnn_phis"],
                           given["L0_gnn_gammas"], given["L0_gnn_betas"], table, states)
            join()
            copy_x()
            for n in "12":
                relational_layer(nc, env, by_target, y, out_of, own, *(given["L1_gnn_" + w] for w in (
                    "basis" + n, "att" + n, "root" + n, "bias" + n, f"ln{n}_g", f"ln{n}_b")), typed_table, states)
            join()
            normalised_layer(nc, env, by_target, x, out_of, own, given["L2_gnn_W"], given["L2_gnn_b"], table, states)
        attention_layer(nc, env, by_target, x, y, [given["L3_gnn_" + w] for w in (
            "Wqkv", "bqkv", "ln_attn_g", "ln_attn_b", "ln_res_g", "ln_res_b", "W_in", "b_in", "W_out", "b_out")],
            qv_table, k_table, wide_states)
        store_nodes(nc, x, out)


def kernel(**inputs):
    import numpy as _np
    import concourse.bacc as _bacc
    from concourse import mybir as _mybir
    from concourse.bass_utils import run_bass_kernel_spmd as _run

    nc = _bacc.Bacc("TRN2", target_bir_lowering=False, num_devices=1)
    arrays, given = {}, {}
    for name in NAMES:
        a = _np.asarray(inputs[name])
        if name in ("L0_gnn_thetas", "L0_gnn_phis"):
            a = a.transpose(0, 2, 1)
        if name == "L3_gnn_b_in":
            a = a.reshape(DFF // P, P).T
        a = _np.ascontiguousarray(a)
        arrays[f"in_{name}"] = a
        given[name] = nc.dram_tensor(f"in_{name}", a.shape, _mybir.dt.from_np(a.dtype), kind="ExternalInput").ap()
    out = nc.dram_tensor("out", (N, D), FP32, kind="ExternalOutput").ap()
    graph_program(nc, given, out)
    result = _run(nc, [arrays], core_ids=[0])
    return result.results[0]["out"]
```

```python
import itertools
from contextlib import ExitStack, contextmanager

import numpy as np

import concourse.bass as bass
from concourse import mybir
from concourse.alu_op_type import AluOpType as ALU

FP32 = mybir.dt.float32
BF16 = mybir.dt.bfloat16
FP16 = mybir.dt.float16
I32 = mybir.dt.int32
ACT = mybir.ActivationFunctionType
AX = mybir.AxisListType

P = 128
N = 3125
D = 256
E = 53125
TILES = -(-N // P)
ROWS = TILES * P
LAST = N - (TILES - 1) * P
STEPS = -(-E // P // 8) * 8
SLOTS = P * STEPS
TAIL = E - (P - 1) * STEPS
GROUP = 8
GROUPS = STEPS // GROUP
RING = 4
LAYERS = 3
CHUNK = 5
TYPES = 16
BASES = 8
HEADS = 8
DH = D // HEADS
DFF = 4 * D
EPS = 1e-5
NEG = -1e30
ROUND = 12582912.0


SERIAL = itertools.count()


def buffer(stack, nc, name, cols, dt=FP32):
    return stack.enter_context(nc.sbuf_tensor(f"{name}_{next(SERIAL)}", [P, cols], dt))


class Env:
    pass


@contextmanager
def phase(nc, *names):
    with ExitStack() as stack:
        sems = [stack.enter_context(nc.semaphore(f"{n}_{next(SERIAL)}")) for n in names]
        yield sems
        with nc.Block() as block:
            @block.gpsimd
            def _(pool):
                pool.dma_reset(range(min(s.num for s in sems), max(s.num for s in sems) + 1))
                for s in sems:
                    pool.sem_clear(s)


def counted_steps(engine, sem):
    done = itertools.count(1)

    def then(instruction):
        instruction.then_inc(sem, 1)
        engine.wait_ge(sem, next(done))
    return then


def later(g):
    return not isinstance(g, int) or g >= 2


def bulk(ap, tiles=TILES):
    return ap.rearrange("p (a d) -> p a d", a=tiles)


def constants(nc, env):
    with phase(nc, "filled", "shaped") as (filled, shaped), nc.Block() as block:
        @block.gpsimd
        def _(pool):
            pool.memset(env.ident[:], 0.0).then_inc(filled, 1)
            pool.memset(env.ones[:], 1.0).then_inc(filled, 1)
            pool.iota(env.iota_p[:], pattern=[[1, P]], base=0, channel_multiplier=0,
                      allow_small_or_imprecise_dtypes=True).then_inc(filled, 1)
            pool.iota(env.iota_steps[:], pattern=[[1, STEPS]], base=0, channel_multiplier=0,
                      allow_small_or_imprecise_dtypes=True).then_inc(filled, 1)
            pool.iota(env.iota_a1[:], pattern=[[1, TILES]], base=1, channel_multiplier=0,
                      allow_small_or_imprecise_dtypes=True).then_inc(filled, 1)
            pool.iota(env.own[:], pattern=[[0, 1]], base=0, channel_multiplier=1,
                      allow_small_or_imprecise_dtypes=True).then_inc(filled, 1)
            pool.wait_ge(filled, 6)
            pool.affine_select(out=env.ident[:], in_=env.ident[:], compare_op=ALU.not_equal, fill=1.0,
                               base=0, pattern=[[-1, P]], channel_multiplier=1).then_inc(shaped, 1)
            pool.affine_select(out=env.after[:], in_=env.ones[:], compare_op=ALU.is_gt, fill=0.0,
                               base=0, pattern=[[1, P]], channel_multiplier=-1).then_inc(shaped, 1)
            pool.affine_select(out=env.before[:], in_=env.ones[:], compare_op=ALU.is_gt, fill=0.0,
                               base=0, pattern=[[-1, P]], channel_multiplier=1).then_inc(shaped, 1)

        @block.scalar
        def _(act):
            act.wait_ge(shaped, 3)
            nc.scalar.copy(env.ident16[:], env.ident[:])

        @block.vector
        def _(dve):
            dve.wait_ge(filled, 6)
            nc.vector.reciprocal(env.inv_a1[:], env.iota_a1[:])


def edge_columns(nc, env, node_dram, other_dram, type_dram=None, weight_dram=None):
    typed = type_dram is not None
    with ExitStack() as stack:
        node, other, part = (buffer(stack, nc, n, STEPS, I32) for n in ("node", "other", "part"))
        loads = [(node, node_dram), (other, other_dram)]
        if typed:
            kind = buffer(stack, nc, "kind", STEPS, I32)
            weight = buffer(stack, nc, "weight", STEPS)
            loads += [(kind, type_dram), (weight, weight_dram)]
        with phase(nc, "padded", "loaded", "step") as (padded, loaded, step), nc.Block() as block:
            @block.sync
            def _(sp):
                sp.wait_ge(padded, len(loads))
                for tile, dram in loads:
                    sp.dma_start(tile[0:P - 1, :], dram[0:(P - 1) * STEPS].rearrange("(p t) -> p t", t=STEPS)).then_inc(loaded, 16)
                    sp.dma_start(tile[P - 1:P, 0:TAIL], dram[(P - 1) * STEPS:E].unsqueeze(0)).then_inc(loaded, 16)

            @block.vector
            def _(dve):
                then = counted_steps(dve, step)

                nc.vector.memset(node[:], ROWS - 1).then_inc(padded, 1)
                nc.vector.memset(other[:], ROWS - 1).then_inc(padded, 1)
                if typed:
                    nc.vector.memset(kind[:], 0).then_inc(padded, 1)
                    nc.vector.memset(weight[:], 0.0).then_inc(padded, 1)
                dve.wait_ge(loaded, 2 * len(loads) * 16)
                then(nc.vector.tensor_single_scalar(part[:], node[:], 7, op=ALU.logical_shift_right))
                then(nc.vector.tensor_scalar(out=env.col_a1[:], in0=part[:], scalar1=1.0, scalar2=None, op0=ALU.add))
                then(nc.vector.tensor_single_scalar(part[:], node[:], 127, op=ALU.bitwise_and))
                then(nc.vector.tensor_copy(env.col_b[:], part[:]))
                if typed:
                    record = env.records[:].rearrange("p (t c) -> p t c", c=2)
                    then(nc.vector.tensor_single_scalar(other[:], other[:], 4, op=ALU.logical_shift_left))
                    then(nc.vector.tensor_tensor(out=other[:], in0=other[:], in1=kind[:], op=ALU.bitwise_or))
                    then(nc.vector.tensor_copy(record[:, :, 0], other[:]))
                    then(nc.vector.tensor_copy(record[:, :, 1], weight[:]))
                else:
                    then(nc.vector.tensor_single_scalar(part[:], other[:], 8, op=ALU.logical_shift_right))
                    then(nc.vector.tensor_copy(env.piece[0][:], part[:]))
                    then(nc.vector.tensor_single_scalar(part[:], other[:], 255, op=ALU.bitwise_and))
                    then(nc.vector.tensor_copy(env.piece[1][:], part[:]))


SCATTER_GROUP = 16
SCATTER_SEMS = ("scatter_staged", "landed0", "landed1", "scatter_held")


class Nothing:

    def share(self, nc, block, sems, groups):
        pass


NOTHING = Nothing()


class Scatter:

    def __init__(self, stack, nc, records, dram):
        self.records, self.dram, self.done = records, dram, 0
        self.place = buffer(stack, nc, "scatter_place", STEPS, I32)
        self.index = [buffer(stack, nc, "scatter_index", SCATTER_GROUP, I32) for _ in range(2)]
        self.record = [buffer(stack, nc, "scatter_record", 2 * SCATTER_GROUP) for _ in range(2)]

    def share(self, nc, block, sems, groups):
        staged, landed = sems[0], sems[1:3]
        first = self.done
        self.done += groups

        @block.gpsimd
        def _(pool):
            def send(g, h, n):
                at = (first + g) * SCATTER_GROUP
                if not isinstance(n, int) or n > 0:
                    pool.wait_ge(landed[h], n * (16 * SCATTER_GROUP))
                    pool.sem_inc(sems[3], 1)
                pool.tensor_copy(self.index[h][:], self.place[:, bass.ds(at, SCATTER_GROUP)]).then_inc(staged, 1)
                pool.tensor_copy(self.record[h][:], self.records[:, bass.ds(at * 2, 2 * SCATTER_GROUP)]).then_inc(staged, 1)
                pool.wait_ge(staged, 2 * g + 2)
                pool.sem_inc(sems[3], 1)
                for u in range(SCATTER_GROUP):
                    pool.indirect_dma_start(
                        out=self.dram, out_offset=bass.IndirectOffsetOnAxis(ap=self.index[h][:, u:u + 1], axis=0),
                        in_=self.record[h][:, 2 * u:2 * u + 2], in_offset=None).then_inc(landed[h], 16)
            for g in range(min(2, groups)):
                send(g, g, 0)
            if groups // 2 > 1:
                with pool.Fori(1, groups // 2) as i:
                    for h in range(2):
                        send(2 * i + h, h, i)
            if groups % 2 and groups > 2:
                send(groups - 1, 0, groups // 2)
            for h in range(2):
                if (groups + 1 - h) // 2:
                    pool.wait_ge(landed[h], (groups + 1 - h) // 2 * 16 * SCATTER_GROUP)


def edge_order(nc, env, order, beside):
    col_a1, col_b = env.col_a1, env.col_b
    with ExitStack() as stack:
        rank, place, sq = order.keep, order.anew, env.tmp
        counting = stack.enter_context(ExitStack())
        def sc(name, shape, dt=FP32):
            return buffer(counting, nc, name, shape[1], dt)
        wt = sc("wt", [P, STEPS * P], BF16)
        count = sc("count", [P, STEPS * TILES])
        hot_a = sc("hot_a", [P, STEPS * TILES], BF16)
        ring = stack.enter_context(ExitStack())
        w = buffer(ring, nc, "w", 2 * GROUP * P, BF16)

        def tile_of(buffer, g, u, width):
            return buffer[:, bass.ds(g * (GROUP * width) + u * width, width)]

        names = ("hot", "w_ready", "turned", "copied", "counted", "count_kept", "compared", "ranked", "held") + SCATTER_SEMS
        with phase(nc, *names) as (hot, w_ready, turned, copied, counted, count_kept, compared, ranked, held, *scatter_sems), \
                nc.Block() as block:
            beside.share(nc, block, scatter_sems, 13)
            turn_bank = [env.bank[h][:].bitcast(BF16) for h in range(2)]
            count_bank = [env.bank[2 + h] for h in range(2)]
            eq_bank = [env.bank[4:6], env.bank[6:8]]

            @block.vector
            def _(dve):
                def make_w(g, h):
                    if later(g):
                        dve.wait_ge(counted, g - 1)
                    for u in range(GROUP):
                        t = g * GROUP + u
                        last = nc.vector.tensor_scalar(
                            out=w[:, (h * GROUP + u) * P:(h * GROUP + u + 1) * P], in0=env.iota_p[:],
                            scalar1=col_b[:, bass.ds(t, 1)], scalar2=col_a1[:, bass.ds(t, 1)],
                            op0=ALU.is_equal, op1=ALU.mult)
                    last.then_inc(w_ready, 1)

                def finish(g, h):
                    dve.wait_ge(counted, g + 1)
                    nc.vector.tensor_tensor(
                        out=bulk(count[:, bass.ds(g * (GROUP * TILES), GROUP * TILES)], GROUP),
                        in0=bulk(count_bank[h][:, 0:GROUP * TILES], GROUP),
                        in1=env.inv_a1[:].unsqueeze(1).broadcast_to([P, GROUP, TILES]), op=ALU.mult).then_inc(count_kept, 1)
                    dve.wait_ge(compared, g + 1)
                    for u in range(GROUP):
                        t = g * GROUP + u
                        products = eq_bank[h][u // 4][:, (u % 4) * P:(u % 4 + 1) * P]
                        last = nc.vector.scalar_tensor_tensor(
                            out=products, in0=products, scalar=sq[:, bass.ds(t, 1)],
                            in1=env.after[:], op0=ALU.is_equal, op1=ALU.mult,
                            accum_out=rank[:, bass.ds(t, 1)])
                    last.then_inc(ranked, 1)

                nc.vector.tensor_tensor(out=sq[:], in0=col_a1[:], in1=col_a1[:], op=ALU.mult).then_inc(hot, 1)
                nc.vector.tensor_tensor(
                    out=bulk(hot_a[:], STEPS), in0=col_a1[:].unsqueeze(2).broadcast_to([P, STEPS, TILES]),
                    in1=env.iota_a1[:].unsqueeze(1).broadcast_to([P, STEPS, TILES]), op=ALU.is_equal).then_inc(hot, 1)
                dve.wait_ge(hot, 2)
                make_w(0, 0)
                make_w(1, 1)
                finish(0, 0)
                with dve.Fori(1, GROUPS // 2) as i:
                    make_w(2 * i, 0)
                    finish(2 * i - 1, 1)
                    make_w(2 * i + 1, 1)
                    finish(2 * i, 0)
                finish(GROUPS - 1, 1)

            @block.tensor
            def _(pe):
                def turn(g, h):
                    pe.wait_ge(w_ready, g + 1)
                    pe.sem_inc(held, 1)
                    if later(g):
                        pe.wait_ge(copied, g - 1)
                        pe.sem_inc(held, 1)
                        pe.wait_ge(count_kept, g - 1)
                        pe.sem_inc(held, 1)
                    for u in range(GROUP):
                        wu = w[:, (h * GROUP + u) * P:(h * GROUP + u + 1) * P]
                        last = nc.tensor.transpose(turn_bank[h][:, u * P:(u + 1) * P], wu, env.ident16[:])
                    last.then_inc(turned, 1)
                    for u in range(GROUP):
                        wu = w[:, (h * GROUP + u) * P:(h * GROUP + u + 1) * P]
                        last = nc.tensor.matmul(count_bank[h][:, u * TILES:(u + 1) * TILES], wu,
                                                tile_of(hot_a, g, u, TILES), start=True, stop=True)
                    last.then_inc(counted, 1)

                def compare(g, h):
                    pe.wait_ge(copied, g + 1)
                    pe.sem_inc(held, 1)
                    if later(g):
                        pe.wait_ge(ranked, g - 1)
                        pe.sem_inc(held, 1)
                    for u in range(GROUP):
                        wtu = tile_of(wt, g, u, P)
                        last = nc.tensor.matmul(eq_bank[h][u // 4][:, (u % 4) * P:(u % 4 + 1) * P], wtu, wtu,
                                                start=True, stop=True)
                    last.then_inc(compared, 1)

                pe.wait_ge(hot, 2)
                for g in range(2):
                    turn(g, g)
                    compare(g, g)
                with pe.Fori(1, GROUPS // 2) as i:
                    for h in range(2):
                        turn(2 * i + h, h)
                        compare(2 * i + h, h)

            @block.scalar
            def _(act):
                with act.Fori(0, GROUPS // 2) as i:
                    for h in range(2):
                        g = 2 * i + h
                        act.wait_ge(turned, g + 1)
                        act.sem_inc(held, 1)
                        nc.scalar.copy(wt[:, bass.ds(g * (GROUP * P), GROUP * P)], turn_bank[h][:, 0:GROUP * P]).then_inc(copied, 1)

        ring.close()
        with ExitStack() as inner:
            total = buffer(inner, nc, "total", TILES, FP32)
            base = order.start
            with phase(nc, "summed", "totalled", "step") as (summed, totalled, step), nc.Block() as block:
                @block.vector
                def _(dve):
                    nc.vector.tensor_scalar(out=count[:], in0=count[:], scalar1=ROUND, scalar2=ROUND,
                                            op0=ALU.add, op1=ALU.subtract).then_inc(step, 1)
                    dve.wait_ge(step, 1)
                    cols = count[:].rearrange("p (t a) -> p a t", a=TILES)
                    for a in range(TILES):
                        nc.vector.tensor_tensor_scan(
                            out=cols[:, a, :], data0=env.ones[:, 0:1].broadcast_to([P, STEPS]),
                            data1=cols[:, a, :], initial=0.0, op0=ALU.mult, op1=ALU.add).then_inc(step, 1)
                    dve.wait_ge(step, 1 + TILES)
                    nc.vector.tensor_copy(total[:], count[:, (STEPS - 1) * TILES:]).then_inc(summed, 1)
                    dve.wait_ge(totalled, 1)
                    nc.vector.tensor_tensor_scan(
                        out=base[:], data0=env.ones[:, 0:TILES], data1=env.bank[1][:, 0:TILES], initial=0.0,
                        op0=ALU.mult, op1=ALU.add).then_inc(step, 1)
                    dve.wait_ge(step, 2 + TILES)
                    nc.vector.tensor_tensor(out=base[:], in0=base[:], in1=env.bank[1][:, 0:TILES], op=ALU.subtract).then_inc(step, 1)
                    dve.wait_ge(step, 3 + TILES)
                    nc.vector.tensor_tensor(out=base[:], in0=base[:], in1=env.bank[0][:, 0:TILES], op=ALU.add).then_inc(step, 1)
                    nc.vector.tensor_copy(order.count[:], total[:]).then_inc(step, 1)

                @block.tensor
                def _(pe):
                    pe.wait_ge(summed, 1)
                    nc.tensor.matmul(env.bank[0][:, 0:TILES], env.after[:], total[:], start=True, stop=True)
                    nc.tensor.matmul(env.bank[1][:, 0:TILES], env.ones[:], total[:], start=True, stop=True).then_inc(totalled, 1)

        with ExitStack() as inner:
            W1, W2 = GROUP * TILES, GROUP * 2 * TILES
            part = buffer(inner, nc, "part", 2 * W1)
            high_low = buffer(inner, nc, "high_low", 2 * W2, BF16)
            found = buffer(inner, nc, "found", 2 * W2)
            names = ("added", "cut_high", "cut", "looked_up", "picked", "placed", "held") + SCATTER_SEMS
            with phase(nc, *names) as (added, cut_high, cut, looked_up, picked, placed, held, *scatter_sems), \
                    nc.Block() as block:
                beside.share(nc, block, scatter_sems, 5)

                def part_of(h):
                    return bulk(part[:, h * W1:(h + 1) * W1], GROUP)

                def high_low_of(h):
                    return bulk(high_low[:, h * W2:(h + 1) * W2], GROUP)

                @block.vector
                def _(dve):
                    def add(g, h):
                        if later(g):
                            dve.wait_ge(cut, g - 1)
                        nc.vector.tensor_tensor(
                            out=part_of(h), in0=bulk(count[:, bass.ds(g * W1, W1)], GROUP),
                            in1=base[:].unsqueeze(1).broadcast_to([P, GROUP, TILES]), op=ALU.add).then_inc(added, 1)

                    def low(g, h):
                        dve.wait_ge(cut_high, g + 1)
                        nc.vector.tensor_tensor(out=high_low_of(h)[:, :, TILES:], in0=part_of(h), in1=high_low_of(h)[:, :, 0:TILES],
                                                op=ALU.subtract).then_inc(cut, 1)

                    def pick(g, h):
                        dve.wait_ge(looked_up, g + 1)
                        if later(g):
                            dve.wait_ge(placed, g - 1)
                        nc.vector.tensor_tensor(
                            out=found[:, h * W2:(h + 1) * W2].rearrange("p (u s a) -> p u s a", u=GROUP, s=2),
                            in0=env.bank[h][:, 0:W2].rearrange("p (u s a) -> p u s a", u=GROUP, s=2),
                            in1=bulk(hot_a[:, bass.ds(g * W1, W1)], GROUP).unsqueeze(2).broadcast_to([P, GROUP, 2, TILES]),
                            op=ALU.mult).then_inc(picked, 1)

                    def total_up(g, h):
                        dve.wait_ge(picked, g + 1)
                        nc.vector.tensor_reduce(out=place[:, bass.ds(g * GROUP, GROUP)], in_=bulk(found[:, h * W2:(h + 1) * W2], GROUP),
                                                axis=AX.X, op=ALU.add).then_inc(placed, 1)

                    def turn(g, h, before=True, ahead=True):
                        if ahead:
                            add(g + 2, h)
                        low(g + 1, 1 - h)
                        pick(g, h)
                        if before:
                            total_up(g - 1, 1 - h)

                    add(0, 0)
                    add(1, 1)
                    low(0, 0)
                    turn(0, 0, before=False)
                    turn(1, 1)
                    with dve.Fori(1, GROUPS // 2 - 1) as i:
                        for h in range(2):
                            turn(2 * i + h, h)
                    turn(GROUPS - 2, 0, ahead=False)
                    pick(GROUPS - 1, 1)
                    total_up(GROUPS - 2, 0)
                    total_up(GROUPS - 1, 1)

                @block.scalar
                def _(act):
                    def high(g, h):
                        act.wait_ge(added, g + 1)
                        act.sem_inc(held, 1)
                        if later(g):
                            act.wait_ge(looked_up, g - 1)
                            act.sem_inc(held, 1)
                        nc.scalar.copy(high_low_of(h)[:, :, 0:TILES], part_of(h)).then_inc(cut_high, 1)
                    for g in range(2):
                        high(g, g)
                    with act.Fori(1, GROUPS // 2) as i:
                        for h in range(2):
                            high(2 * i + h, h)

                @block.tensor
                def _(pe):
                    def look_up(g, h):
                        pe.wait_ge(cut, g + 1)
                        pe.sem_inc(held, 1)
                        if later(g):
                            pe.wait_ge(picked, g - 1)
                            pe.sem_inc(held, 1)
                        for u in range(GROUP):
                            last = nc.tensor.matmul(
                                env.bank[h][:, u * 2 * TILES:(u + 1) * 2 * TILES], tile_of(wt, g, u, P),
                                high_low[:, h * W2 + u * 2 * TILES:h * W2 + (u + 1) * 2 * TILES], start=True, stop=True)
                        last.then_inc(looked_up, 1)
                    for g in range(2):
                        look_up(g, g)
                    with pe.Fori(1, GROUPS // 2) as i:
                        for h in range(2):
                            look_up(2 * i + h, h)
        counting.close()

        with ExitStack() as inner:
            def si(name, shape, dt=FP32):
                return buffer(inner, nc, name, shape[1], dt)
            blk, stp = si("blk", [P, STEPS]), si("stp", [P, STEPS])
            n_blk, n_stp = si("n_blk", [P, TILES]), si("n_stp", [P, TILES])
            l_blk, l_stp = si("l_blk", [P, TILES]), si("l_stp", [P, TILES])
            last, crosses = si("last", [P, TILES]), si("crosses", [P, TILES])
            piece_a = si("piece_a", [P, TILES])
            with phase(nc, "step") as (step,), nc.Block() as block:
                @block.vector
                def _(dve):
                    then = counted_steps(dve, step)

                    def locate(at, b, s):
                        then(nc.vector.tensor_scalar(out=b[:], in0=at[:], scalar1=0.5, scalar2=1.0 / STEPS, op0=ALU.add, op1=ALU.mult))
                        then(nc.vector.tensor_scalar(out=b[:], in0=b[:], scalar1=-0.5, scalar2=ROUND, op0=ALU.add, op1=ALU.add))
                        then(nc.vector.tensor_scalar(out=b[:], in0=b[:], scalar1=-ROUND, scalar2=None, op0=ALU.add))
                        then(nc.vector.scalar_tensor_tensor(out=s[:], in0=b[:], scalar=-float(STEPS), in1=at[:], op0=ALU.mult, op1=ALU.add))

                    then(nc.vector.reciprocal(blk[:], col_a1[:]))
                    then(nc.vector.tensor_tensor(out=place[:], in0=place[:], in1=blk[:], op=ALU.mult))
                    then(nc.vector.tensor_scalar(out=place[:], in0=place[:], scalar1=ROUND, scalar2=-ROUND, op0=ALU.add, op1=ALU.add))
                    then(nc.vector.scalar_tensor_tensor(out=place[:], in0=place[:], scalar=-1.0, in1=rank[:], op0=ALU.add, op1=ALU.subtract))
                    locate(place, blk, stp)
                    locate(order.start, n_blk, n_stp)
                    then(nc.vector.tensor_scalar(out=order.some[:], in0=order.count[:], scalar1=1.0, scalar2=None, op0=ALU.min))
                    then(nc.vector.tensor_tensor(out=last[:], in0=order.start[:], in1=order.count[:], op=ALU.add))
                    then(nc.vector.tensor_scalar(out=last[:], in0=last[:], scalar1=-1.0, scalar2=0.0, op0=ALU.add, op1=ALU.max))
                    locate(last, l_blk, l_stp)
                    then(nc.vector.tensor_copy(order.last[:], last[:]))
                    then(nc.vector.tensor_tensor(out=crosses[:], in0=l_blk[:], in1=n_blk[:], op=ALU.is_gt))
                    then(nc.vector.tensor_tensor(out=crosses[:], in0=crosses[:], in1=order.some[:], op=ALU.mult))
                    then(nc.vector.tensor_scalar(out=order.stays[:], in0=crosses[:], scalar1=-1.0, scalar2=-NEG, op0=ALU.add, op1=ALU.mult))
                    then(nc.vector.scalar_tensor_tensor(out=l_blk[:], in0=l_blk[:], scalar=1.0, in1=crosses[:], op0=ALU.add, op1=ALU.mult))
                    then(nc.vector.tensor_scalar(out=order.end_block[:], in0=l_blk[:], scalar1=-1.0, scalar2=None, op0=ALU.add))
                    then(nc.vector.tensor_scalar(out=piece_a[:], in0=env.iota_a1[:], scalar1=-1.0, scalar2=None, op0=ALU.add))
                    then(nc.vector.tensor_tensor(out=piece_a[:], in0=piece_a[:], in1=order.some[:], op=ALU.mult))
                    then(nc.vector.tensor_scalar(out=last[:], in0=order.some[:], scalar1=env.own[:, 0:1], scalar2=None, op0=ALU.mult))

            order.place_edges(nc, env, place, blk, stp, beside)
            permute(nc, env, n_blk, n_stp, [order.some, piece_a, last], TILES, 1, NOTHING, 0)
            segments(nc, env, order)


def permute(nc, env, blk, stp, pieces, tiles, group, beside, shares):
    n = len(pieces)
    body = RING * group
    by_act = group - 1
    whole = tiles // body
    rest = range(tiles % body // group)

    def over_groups(engine, do):
        for h in range(RING):
            do(h, h)
        with engine.Fori(1, whole) as i:
            for h in range(RING):
                do(RING * i + h, h)
        for h in rest:
            do(RING * whole + h, h)

    with ExitStack() as stack:
        hot_step = buffer(stack, nc, "hot_step", body * STEPS, BF16)
        hot_block = buffer(stack, nc, "hot_block", body * P, BF16)
        marked_piece = buffer(stack, nc, "marked_piece", body * n * P, BF16)
        with phase(nc, "hot", "marked", "used", "held", *SCATTER_SEMS) as (hot, marked, used, held, *scatter_sems), nc.Block() as block:
            beside.share(nc, block, scatter_sems, shares)

            @block.vector
            def _(dve):
                def make(g, h):
                    if not isinstance(g, int) or g >= RING:
                        dve.wait_ge(used, g - RING + 1)
                    for u in range(group):
                        t = g * group + u
                        v = h * group + u
                        nc.vector.tensor_scalar(out=hot_step[:, v * STEPS:(v + 1) * STEPS], in0=env.iota_steps[:],
                                                scalar1=stp[:, bass.ds(t, 1)], scalar2=None, op0=ALU.is_equal)
                        if u < by_act:
                            last = nc.vector.tensor_scalar(out=hot_block[:, v * P:(v + 1) * P], in0=env.iota_p[:],
                                                           scalar1=blk[:, bass.ds(t, 1)], scalar2=None, op0=ALU.is_equal)
                        else:
                            for i, piece in enumerate(pieces):
                                last = nc.vector.tensor_scalar(
                                    out=marked_piece[:, (v * n + i) * P:(v * n + i + 1) * P], in0=env.iota_p[:],
                                    scalar1=blk[:, bass.ds(t, 1)], scalar2=piece[:, bass.ds(t, 1)],
                                    op0=ALU.is_equal, op1=ALU.mult)
                    last.then_inc(hot, 1)

                over_groups(dve, make)

            @block.scalar
            def _(act):
                if not by_act:
                    return

                def mark(g, h):
                    act.wait_ge(hot, g + 1)
                    act.sem_inc(held, 1)
                    for u in range(by_act):
                        v = h * group + u
                        for i, piece in enumerate(pieces):
                            last = nc.scalar.activation(
                                marked_piece[:, (v * n + i) * P:(v * n + i + 1) * P], hot_block[:, v * P:(v + 1) * P],
                                ACT.Copy, scale=piece[:, bass.ds(g * group + u, 1)])
                    last.then_inc(marked, 1)

                over_groups(act, mark)

            @block.tensor
            def _(pe):
                def add(g, h, first=False, final=False):
                    pe.wait_ge(hot, g + 1)
                    if by_act:
                        pe.sem_inc(held, 1)
                        pe.wait_ge(marked, g + 1)
                    pe.sem_inc(held, 1)
                    for u in range(group):
                        v = h * group + u
                        for i in range(n):
                            last = nc.tensor.matmul(
                                env.bank[i][:, 0:STEPS], marked_piece[:, (v * n + i) * P:(v * n + i + 1) * P],
                                hot_step[:, v * STEPS:(v + 1) * STEPS], start=first and u == 0, stop=final and u == group - 1)
                    last.then_inc(used, 1)

                groups = tiles // group
                for h in range(RING):
                    add(h, h, first=h == 0)
                with pe.Fori(1, whole - 1) as i:
                    for h in range(RING):
                        add(RING * i + h, h)
                for g in range(RING * (whole - 1), groups):
                    add(g, g % RING, final=g == groups - 1)


def segments(nc, env, order):
    with ExitStack() as stack:
        def sb(name, shape, dt=FP32):
            return buffer(stack, nc, name, shape[1], dt)
        ident_v, row = sb("ident_v", [P, 2 * P]), sb("row", [P, P])
        open_all, carry = sb("open_all", [P, 1]), sb("carry", [P, 1])
        node, at = sb("node", [P, STEPS]), sb("at", [P, STEPS])
        with phase(nc, "step", "spread", "spread_done") as (step, spread, spread_done), nc.Block() as block:
            @block.vector
            def _(dve):
                then = counted_steps(dve, step)

                first, node_a, node_b = (env.bank[i][:, 0:STEPS] for i in range(3))
                then(nc.vector.tensor_scalar(out=order.keep[:], in0=first, scalar1=-1.0, scalar2=1.0, op0=ALU.mult, op1=ALU.add))
                then(nc.vector.tensor_scalar(out=order.anew[:], in0=first, scalar1=NEG, scalar2=None, op0=ALU.mult))
                then(nc.vector.tensor_reduce(out=open_all[:], in_=order.keep[:], axis=AX.X, op=ALU.min))
                then(nc.vector.tensor_copy(at[:], node_b))
                then(nc.vector.scalar_tensor_tensor(out=at[:], in0=node_a, scalar=float(P), in1=at[:], op0=ALU.mult, op1=ALU.add))
                then(nc.vector.tensor_tensor_scan(out=node[:], data0=at[:], data1=at[:], initial=0.0, op0=ALU.max, op1=ALU.max))
                nc.vector.tensor_scalar(out=ident_v[:, 0:P], in0=env.ident[:], scalar1=open_all[:, 0:1], scalar2=None, op0=ALU.mult).then_inc(spread, 1)
                nc.vector.tensor_scalar(out=ident_v[:, P:], in0=env.ident[:], scalar1=node[:, STEPS - 1:STEPS], scalar2=None, op0=ALU.mult).then_inc(spread, 1)
                dve.wait_ge(spread_done, 1)
                then(nc.vector.tensor_copy(order.open_row[:], env.bank[4][:, 0:P]))
                then(nc.vector.tensor_scalar(out=order.shut_row[:], in0=order.open_row[:], scalar1=-1.0, scalar2=-NEG, op0=ALU.add, op1=ALU.mult))
                then(nc.vector.tensor_tensor(out=row[:], in0=env.bank[5][:, 0:P], in1=env.before[:], op=ALU.mult))
                then(nc.vector.tensor_reduce(out=carry[:], in_=row[:], axis=AX.X, op=ALU.max))
                if order.node is not None:
                    then(nc.vector.tensor_scalar(out=order.node[:], in0=node[:], scalar1=carry[:, 0:1], scalar2=None, op0=ALU.max))

            @block.tensor
            def _(pe):
                pe.wait_ge(spread, 2)
                nc.tensor.matmul(env.bank[4][:, 0:P], env.ones[:], ident_v[:, 0:P], start=True, stop=True)
                nc.tensor.matmul(env.bank[5][:, 0:P], env.ones[:], ident_v[:, P:], start=True, stop=True).then_inc(spread_done, 1)


class Order:

    def __init__(self, stack, nc, name):
        def sb(what, cols, dt=FP32):
            return buffer(stack, nc, f"{name}_{what}", cols, dt)
        self.start = sb("start", TILES)
        self.count = sb("count", TILES)
        self.some = sb("some", TILES)
        self.last = sb("last", TILES, I32)
        self.stays = sb("stays", TILES)
        self.end_block = sb("end_block", TILES)
        self.keep = sb("keep", STEPS)
        self.anew = sb("anew", STEPS)
        self.open_row = sb("open_row", P)
        self.shut_row = sb("shut_row", P)
        self.node = None
        self.row = sb("row", STEPS, I32)
        self.name = name

    def spread_ends(self, nc, env, dram=None, nodes=()):
        order = self
        with ExitStack() as inner:
            spread_v = buffer(inner, nc, "spread_v", TILES * P)
            with phase(nc, "spread", "summed", "kept", "cleared", "loaded") as (spread, summed, kept, cleared, loaded), nc.Block() as block:
                if nodes:
                    @block.sync
                    def _(sp):
                        for x in nodes:
                            sp.dma_start(bulk(x[:, 0:(TILES - 1) * D], TILES - 1),
                                         dram[0:(TILES - 1) * P, :].rearrange("(a p) d -> p a d", p=P)).then_inc(loaded, 16)
                        sp.wait_ge(cleared, len(nodes))
                        for x in nodes:
                            sp.dma_start(x[0:LAST, (TILES - 1) * D:], dram[(TILES - 1) * P:N, :]).then_inc(loaded, 16)
                        sp.wait_ge(loaded, 32 * len(nodes))

                @block.vector
                def _(dve):
                    for x in nodes:
                        nc.vector.memset(x[:, (TILES - 1) * D:], 0.0).then_inc(cleared, 1)
                    nc.vector.tensor_tensor(out=bulk(spread_v[:]), in0=env.ident[:].unsqueeze(1).broadcast_to([P, TILES, P]),
                                            in1=order.end_block[:].unsqueeze(2).broadcast_to([P, TILES, P]), op=ALU.mult).then_inc(spread, 1)

                @block.tensor
                def _(pe):
                    pe.wait_ge(spread, 1)
                    for b, at_col in enumerate(range(0, TILES * P, 512)):
                        width = min(512, TILES * P - at_col)
                        nc.tensor.matmul(env.bank[b][:, 0:width], env.ones[:], spread_v[:, at_col:at_col + width],
                                         start=True, stop=True).then_inc(summed, 1)

                @block.scalar
                def _(act):
                    for b, at_col in enumerate(range(0, TILES * P, 512)):
                        width = min(512, TILES * P - at_col)
                        act.wait_ge(summed, b + 1)
                        nc.scalar.copy(order.end_row[:, at_col:at_col + width], env.bank[b][:, 0:width]).then_inc(kept, 1)


class BySource(Order):
    def place_edges(self, nc, env, place, blk, stp, beside):
        permute(nc, env, blk, stp, env.piece, STEPS, 4, beside, STEPS // SCATTER_GROUP - 18)
        with phase(nc, "step") as (step,), nc.Block() as block:
            @block.vector
            def _(dve):
                then = counted_steps(dve, step)
                then(nc.vector.tensor_copy(env.tmp[:], env.bank[1][:, 0:STEPS]))
                then(nc.vector.scalar_tensor_tensor(out=self.row[:], in0=env.bank[0][:, 0:STEPS], scalar=256.0, in1=env.tmp[:],
                                                    op0=ALU.mult, op1=ALU.add))


class ByTarget(Order):
    def __init__(self, stack, nc, name):
        super().__init__(stack, nc, name)
        self.node = buffer(stack, nc, f"{name}_node", STEPS, I32)
        self.source = buffer(stack, nc, f"{name}_source", STEPS, I32)
        self.weight = buffer(stack, nc, f"{name}_weight", STEPS)
        self.inverse = buffer(stack, nc, f"{name}_inverse", TILES)
        self.root_inverse = buffer(stack, nc, f"{name}_root_inverse", TILES)

    def place_edges(self, nc, env, place, blk, stp, beside):
        with phase(nc, "step") as (step,), nc.Block() as block:
            @block.vector
            def _(dve):
                counted_steps(dve, step)(nc.vector.tensor_copy(self.scatter.place[:], place[:]))

    def take(self, nc, env):
        with phase(nc, "loaded", "step", "rooted") as (loaded, step, rooted), nc.Block() as block:
            records = self.scatter.records

            @block.sync
            def _(sp):
                sp.dma_start(records[:], self.scatter.dram.rearrange("(p t) c -> p (t c)", t=STEPS)).then_inc(loaded, 16)

            @block.vector
            def _(dve):
                then = counted_steps(dve, step)
                then(nc.vector.tensor_scalar(out=self.inverse[:], in0=self.count[:], scalar1=1.0, scalar2=None, op0=ALU.add))
                then(nc.vector.reciprocal(self.inverse[:], self.inverse[:]))
                dve.wait_ge(loaded, 16)
                then(nc.vector.tensor_copy(self.row[:], records[:].rearrange("p (t c) -> p t c", c=2)[:, :, 0]))
                then(nc.vector.tensor_copy(self.weight[:], records[:].rearrange("p (t c) -> p t c", c=2)[:, :, 1]))
                then(nc.vector.tensor_single_scalar(self.source[:], self.row[:], 4, op=ALU.logical_shift_right))

            @block.scalar
            def _(act):
                act.wait_ge(step, 2)
                nc.scalar.activation(self.root_inverse[:], self.inverse[:], ACT.Sqrt).then_inc(rooted, 1)


def shared(stack, nc):
    env = Env()

    def sb(name, cols, dt=FP32):
        return buffer(stack, nc, name, cols, dt)
    env.bank = [stack.enter_context(nc.psum_tensor(f"bank{i}", [P, 512], FP32)) for i in range(8)]
    env.ident, env.ident16, env.ones = sb("ident", P), sb("ident16", P, BF16), sb("ones", P)
    env.after, env.before = sb("after", P), sb("before", P)
    env.iota_p, env.iota_steps, env.own = sb("iota_p", P, BF16), sb("iota_steps", STEPS, FP16), sb("own", 1)
    env.iota_a1, env.inv_a1 = sb("iota_a1", TILES), sb("inv_a1", TILES)
    env.tmp = sb("tmp", STEPS)
    return env


def edge_buffers(stack, nc, env):
    env.col_a1, env.col_b = buffer(stack, nc, "col_a1", STEPS), buffer(stack, nc, "col_b", STEPS)


def ring_use(i, h, chunk, chunks, banks):
    at = h * chunks + chunk
    return at % banks, i * (2 * chunks // banks) + at // banks


def pairs(engine, body):
    body(0, 0)
    body(0, 1)
    with engine.Fori(1, TILES // 2) as i:
        body(i, 0)
        body(i, 1)
    body(TILES // 2, 0)


def project(nc, env, x, w, cols, chunks, stores, banks):
    n = len(chunks)
    with ExitStack() as stack:
        staged_x = [buffer(stack, nc, "staged_x", D) for _ in range(2)]
        xt = [buffer(stack, nc, "xt", D) for _ in range(2)]
        names = ["staged", "turned", "copied", "held"] + [f"filled{b}" for b in range(banks)] \
            + [f"read{b}" for b in range(banks)] + ["stored0", "stored1"]
        with phase(nc, *names) as sems, nc.Block() as block:
            staged, turned, copied, held = sems[:4]
            filled, read, stored = sems[4:4 + banks], sems[4 + banks:4 + 2 * banks], sems[4 + 2 * banks:]

            @block.gpsimd
            def _(pool):
                def stage(i, h):
                    if not isinstance(i, int) or i > 0:
                        pool.wait_ge(turned, 2 * i + h - 1)
                        pool.sem_inc(held, 1)
                    pool.tensor_copy(staged_x[h][:], x[:, bass.ds((2 * i + h) * D, D)]).then_inc(staged, 1)
                pairs(pool, stage)

            @block.tensor
            def _(pe):
                def turn(i, h):
                    pe.wait_ge(staged, 2 * i + h + 1)
                    pe.sem_inc(held, 1)
                    if not isinstance(i, int) or i > 0:
                        pe.wait_ge(copied, 2 * i + h - 1)
                        pe.sem_inc(held, 1)
                    for s in range(2):
                        last = nc.tensor.transpose(env.bank[6 + h][:, s * P:(s + 1) * P], staged_x[h][:, s * P:(s + 1) * P], env.ident[:])
                    last.then_inc(turned, 1)

                def multiply(i, h):
                    pe.wait_ge(copied, 2 * i + h + 1)
                    pe.sem_inc(held, 1)
                    for c, (at, width, _, _) in enumerate(chunks):
                        b, uses = ring_use(i, h, c, n, banks)
                        if not isinstance(uses, int) or uses > 0:
                            pe.wait_ge(read[b], uses)
                            pe.sem_inc(held, 1)
                        nc.tensor.matmul(env.bank[b][:, 0:width], xt[h][:, 0:P], w[:, at:at + width], start=True, stop=False)
                        nc.tensor.matmul(env.bank[b][:, 0:width], xt[h][:, P:], w[:, cols + at:cols + at + width],
                                         start=False, stop=True).then_inc(filled[b], 1)

                turn(0, 0)
                turn(0, 1)
                multiply(0, 0)
                with pe.Fori(1, TILES // 2) as i:
                    turn(i, 0)
                    multiply(i - 1, 1)
                    turn(i, 1)
                    multiply(i, 0)
                turn(TILES // 2, 0)
                multiply(TILES // 2 - 1, 1)
                multiply(TILES // 2, 0)

            def consume(engine, name, i, h):
                first_tile = isinstance(i, int) and i == 0
                if stores and not first_tile:
                    engine.wait_ge(stored[h], i * (16 * len(stores)))
                    engine.sem_inc(held, 1)
                for c, (_, width, who, use) in enumerate(chunks):
                    if who == name:
                        b, uses = ring_use(i, h, c, n, banks)
                        engine.wait_ge(filled[b], uses + 1)
                        engine.sem_inc(held, 1)
                        use(engine, i, h, env.bank[b][:, 0:width], lambda cc: after(engine, i, h, cc)).then_inc(read[b], 1)

            def after(engine, i, h, c):
                b, uses = ring_use(i, h, c, n, banks)
                engine.wait_ge(read[b], uses + 1)
                engine.sem_inc(held, 1)

            @block.vector
            def _(dve):
                pairs(dve, lambda i, h: consume(dve, "vector", i, h))

            @block.scalar
            def _(act):
                def body(i, h):
                    act.wait_ge(turned, 2 * i + h + 1)
                    act.sem_inc(held, 1)
                    if not isinstance(i, int) or i > 0:
                        b, uses = ring_use(i - 1, h, n - 1, n, banks)
                        act.wait_ge(filled[b], uses + 1)
                        act.sem_inc(held, 1)
                    nc.scalar.copy(xt[h][:], env.bank[6 + h][:, 0:D]).then_inc(copied, 1)
                    if not (isinstance(i, int) and i == 0 and h == 0):
                        back = (i, 0) if h else (i - 1, 1)
                        consume(act, "scalar", *back)
                pairs(act, body)
                consume(act, "scalar", TILES // 2, 0)

            @block.sync
            def _(sp):
                def body(i, h):
                    for needs, dram, sbuf in stores:
                        for c in needs:
                            after(sp, i, h, c)
                        sp.dma_start(dram(2 * i + h), sbuf(h)).then_inc(stored[h], 16)
                pairs(sp, body)
                for h in range(2):
                    if stores:
                        sp.wait_ge(stored[h], 16 * len(stores) * (TILES // 2 + (1 - h)))


def edge_pass(nc, env, order, table, states, fold, tail, loads=(), product=None, prepare=None):
    with ExitStack() as stack:
        index = [buffer(stack, nc, "index", GROUP, I32) for _ in range(RING)]
        rows = [buffer(stack, nc, "rows", GROUP * D) for _ in range(RING)]
        state = [buffer(stack, nc, "state", GROUP * D) for _ in range(RING)]
        rounds = GROUPS // RING
        marks, op0, op1, start = (order.anew, ALU.add, ALU.max, NEG) if fold == "max" else (order.keep, ALU.mult, ALU.add, 0.0)
        index_of = order.source if fold == "sum" else order.row
        names = ["indexed", "weighed", "chain", "loaded", "made", "kept", "step", "held"] + [f"gathered{b}" for b in range(RING)] + [f"stored{b}" for b in range(RING)]
        with phase(nc, *names) as sems, nc.Block() as block:
            indexed, weighed, chain, loaded, made, kept, step, held = sems[:8]
            gathered, stored = sems[8:8 + RING], sems[8 + RING:]

            @block.gpsimd
            def _(pool):
                def gather(i, h):
                    pool.wait_ge(indexed, RING * i + h + 1)
                    pool.sem_inc(held, 1)
                    for u in range(GROUP):
                        pool.indirect_dma_start(
                            out=rows[h][:, u * D:(u + 1) * D], out_offset=None, in_=table,
                            in_offset=bass.IndirectOffsetOnAxis(ap=index[h][:, u:u + 1], axis=0)).then_inc(gathered[h], 16)
                for h in range(RING):
                    gather(0, h)
                with pool.Fori(1, rounds) as i:
                    for h in range(RING):
                        gather(i, h)

            if product:
                turned_y, weights, own = product

                @block.tensor
                def _(pe):
                    for a in range(TILES):
                        if a >= len(env.bank):
                            pe.wait_ge(kept, a - len(env.bank) + 1)
                        half_product(nc, env.bank[a % len(env.bank)], turned_y, weights, 2, a, 1).then_inc(made, 1)

                @block.scalar
                def _(act):
                    for a in range(TILES):
                        act.wait_ge(made, a + 1)
                        nc.scalar.copy(tile_at(own, a), env.bank[a % len(env.bank)][:, 0:D]).then_inc(kept, 1)

            if fold == "weighted":
                @block.scalar
                def _(act):
                    with act.Fori(0, rounds) as i:
                        for h in range(RING):
                            act.wait_ge(gathered[h], (i + 1) * (16 * GROUP))
                            act.sem_inc(held, 1)
                            for u in range(GROUP):
                                row = rows[h][:, u * D:(u + 1) * D]
                                nc.scalar.activation(row, row, ACT.Copy, scale=order.weight[:, bass.ds((RING * i + h) * GROUP + u, 1)]
                                                     ).then_inc(weighed, 1)

            @block.vector
            def _(dve):
                def look(g, h):
                    nc.vector.tensor_copy(index[h][:], index_of[:, bass.ds(g * GROUP, GROUP)]).then_inc(indexed, 1)

                def fold_group(i, h, more=True):
                    g = RING * i + h
                    dve.wait_ge(gathered[h], (i + 1) * (16 * GROUP))
                    dve.sem_inc(held, 1)
                    if not isinstance(i, int) or i > 0:
                        dve.wait_ge(stored[h], i * 16)
                        dve.sem_inc(held, 1)
                    for u in range(GROUP):
                        before = state[h][:, (u - 1) * D:u * D] if u else state[h - 1][:, (GROUP - 1) * D:]
                        if fold == "weighted":
                            dve.wait_ge(weighed, g * GROUP + u + 1)
                            dve.sem_inc(held, 1)
                        dve.wait_ge(chain, g * GROUP + u + 1)
                        nc.vector.scalar_tensor_tensor(
                            out=state[h][:, u * D:(u + 1) * D], in0=before, scalar=marks[:, bass.ds(g * GROUP + u, 1)],
                            in1=rows[h][:, u * D:(u + 1) * D], op0=op0, op1=op1).then_inc(chain, 1)
                    if more:
                        look(g + RING, h)

                nc.vector.memset(state[RING - 1][:, (GROUP - 1) * D:], start).then_inc(chain, 1)
                for h in range(RING):
                    look(h, h)
                if prepare:
                    dve.wait_ge(loaded, 16 * len(loads))
                    prepare(counted_steps(dve, step))
                for h in range(RING):
                    fold_group(0, h)
                with dve.Fori(1, rounds - 1) as i:
                    for h in range(RING):
                        fold_group(i, h)
                for h in range(RING):
                    fold_group(rounds - 1, h, more=False)
                dve.wait_ge(chain, STEPS + 1)
                nc.vector.tensor_copy(tail[:], state[RING - 1][:, (GROUP - 1) * D:])

            @block.sync
            def _(sp):
                for sbuf, dram in loads:
                    sp.dma_start(sbuf, dram).then_inc(loaded, 16)
                blocks = states.rearrange("(p t) d -> p (t d)", t=STEPS)
                with sp.Fori(0, rounds) as i:
                    for h in range(RING):
                        sp.wait_ge(chain, (RING * i + h + 1) * GROUP + 1)
                        sp.sem_inc(held, 1)
                        sp.dma_start(blocks[:, bass.ds((RING * i + h) * (GROUP * D), GROUP * D)], state[h][:]).then_inc(stored[h], 16)
                for h in range(RING):
                    sp.wait_ge(stored[h], rounds * 16)
                if loads:
                    sp.wait_ge(loaded, 16 * len(loads))


def tile_at(values, a, tiles=1):
    return values[:, a * D:(a + tiles) * D]


class Finish:
    lags = ()
    has_bent = False
    has_total = False

    @property
    def steps(self):
        return len(self.lags)


class FinishRelative(Finish):
    lags, has_bent, has_total = (1,), True, True

    def __init__(self, nc, env, order, own):
        self.nc, self.env, self.order, self.own = nc, env, order, own

    def step(self, out, a, k):
        return self.nc.vector.tensor_tensor(out=tile_at(out, a), in0=tile_at(out, a), in1=tile_at(self.own, a), op=ALU.add)

    def bent(self, out, a):
        return self.nc.scalar.activation(tile_at(out, a), tile_at(out, a), ACT.Relu, scale=self.order.some[:, a:a + 1])

    def total(self, out, a):
        return column_sum(self.nc, self.env, self.env.bank[0], out, a)


class FinishRelational(Finish):
    lags = (1, 2)

    def __init__(self, nc, order, own, bias, y, stats):
        self.nc, self.order, self.own, self.bias, self.y, self.stats = nc, order, own, bias, y, stats

    def prepare(self, then):
        then(self.nc.vector.tensor_tensor(out=bulk(self.own[:]), in0=bulk(self.own[:]), in1=over_tiles(self.bias[:]), op=ALU.add))
        then(self.nc.vector.tensor_tensor(out=self.own[:], in0=self.own[:], in1=self.y[:], op=ALU.add))

    def step(self, out, a, k):
        if k == 0:
            return self.nc.vector.scalar_tensor_tensor(out=tile_at(out, a), in0=tile_at(out, a), scalar=self.order.inverse[:, a:a + 1],
                                                       in1=tile_at(self.own, a), op0=ALU.mult, op1=ALU.add)
        return self.nc.vector.bn_stats(self.stats[:, a * 6:(a + 1) * 6], tile_at(out, a))


class FinishNormalised(Finish):
    lags, has_bent = (1, 4, 5), True

    def __init__(self, nc, order, own, bias, x, stats):
        self.nc, self.order, self.own, self.bias, self.x, self.stats = nc, order, own, bias, x, stats

    def prepare(self, then):
        then(self.nc.vector.tensor_tensor(out=bulk(self.own[:]), in0=bulk(self.own[:]), in1=over_row(self.order.root_inverse[:]), op=ALU.mult))
        then(self.nc.vector.tensor_tensor(out=bulk(self.own[:]), in0=bulk(self.own[:]), in1=over_tiles(self.bias[:]), op=ALU.add))

    def step(self, out, a, k):
        tile = tile_at(out, a)
        if k == 0:
            return self.nc.vector.scalar_tensor_tensor(out=tile, in0=tile, scalar=self.order.root_inverse[:, a:a + 1],
                                                       in1=tile_at(self.own, a), op0=ALU.mult, op1=ALU.add)
        if k == 1:
            return self.nc.vector.tensor_tensor(out=tile, in0=tile, in1=tile_at(self.x, a), op=ALU.add)
        return self.nc.vector.bn_stats(self.stats[:, a * 6:(a + 1) * 6], tile)

    def bent(self, out, a):
        return self.nc.scalar.activation(tile_at(out, a), tile_at(out, a), ACT.Relu)


def column_sum(nc, env, bank, values, a):
    valid = P if a < TILES - 1 else LAST
    return nc.tensor.matmul(bank[:, 0:D], env.ones[0:valid, :], values[0:valid, a * D:(a + 1) * D], start=a == 0, stop=a == TILES - 1)


def collect(nc, env, order, states, fold, tail, out, finish):
    with ExitStack() as stack:
        prefix = buffer(stack, nc, "prefix", 2 * (P + 1))
        carry = buffer(stack, nc, "carry", D)
        hot = buffer(stack, nc, "hot", ROWS)
        row, op0, op1, start = (order.shut_row, ALU.add, ALU.max, NEG) if fold == "max" else (order.open_row, ALU.mult, ALU.add, 0.0)
        acts = finish.has_bent
        names = ["turned", "cleared", "scanned", "back", "carried", "marked", "picked", "joined", "curved", "totalled"] \
            + [f"stepped{k}" for k in range(finish.steps)] + [f"gathered{c}" for c in range(TILES // CHUNK)]
        slots = 6

        def slot(a):
            return env.bank[2 + a % slots][:, 0:D]

        with phase(nc, *names) as sems, nc.Block() as block:
            turned, cleared, scanned, back, carried, marked, picked, joined, curved, totalled = sems[:10]
            stepped, gathered = sems[10:10 + finish.steps], sems[10 + finish.steps:]

            @block.gpsimd
            def _(pool):
                for a in range(TILES):
                    pool.indirect_dma_start(out=tile_at(out, a), out_offset=None, in_=states,
                                            in_offset=bass.IndirectOffsetOnAxis(ap=order.last[:, a:a + 1], axis=0)
                                            ).then_inc(gathered[a // CHUNK], 16)

            @block.tensor
            def _(pe):
                for s in range(2):
                    last = nc.tensor.transpose(env.bank[0][:, s * P:(s + 1) * P], tail[:, s * P:(s + 1) * P], env.ident[:])
                last.then_inc(turned, 1)
                pe.wait_ge(scanned, 2)
                for s in range(2):
                    last = nc.tensor.transpose(env.bank[1][:, s * P:(s + 1) * P], prefix[:, s * (P + 1):s * (P + 1) + P], env.ident[:])
                last.then_inc(back, 1)
                pe.wait_ge(carried, 1)
                pe.wait_ge(marked, 1)
                for a in range(TILES):
                    if a >= slots:
                        pe.wait_ge(joined, a - slots + 1)
                    nc.tensor.matmul(slot(a), hot[:, a * P:(a + 1) * P], carry[:], start=True, stop=True).then_inc(picked, 1)
                if finish.has_total:
                    for a in range(TILES):
                        pe.wait_ge(curved, a + 1)
                        last = finish.total(out, a)
                    last.then_inc(totalled, 1)

            if acts:
                @block.scalar
                def _(act):
                    for a in range(TILES):
                        act.wait_ge(stepped[0], a + 1)
                        finish.bent(out, a).then_inc(curved, 1)

            @block.vector
            def _(dve):
                nc.vector.memset(prefix[:], start).then_inc(cleared, 1)
                dve.wait_ge(turned, 1)
                dve.wait_ge(cleared, 1)
                for s in range(2):
                    nc.vector.tensor_tensor_scan(
                        out=prefix[:, s * (P + 1) + 1:(s + 1) * (P + 1)], data0=row[:], data1=env.bank[0][:, s * P:(s + 1) * P],
                        initial=start, op0=op0, op1=op1).then_inc(scanned, 1)
                nc.vector.tensor_scalar(out=hot[:], in0=order.end_row[:], scalar1=env.own[:, 0:1], scalar2=None, op0=ALU.is_equal).then_inc(marked, 1)
                dve.wait_ge(back, 1)
                nc.vector.tensor_copy(carry[:], env.bank[1][:, 0:D]).then_inc(carried, 1)

                def join(a):
                    if a % CHUNK == 0:
                        dve.wait_ge(gathered[a // CHUNK], 16 * CHUNK)
                    dve.wait_ge(picked, a + 1)
                    own = tile_at(out, a)
                    if fold == "max":
                        nc.vector.scalar_tensor_tensor(out=own, in0=slot(a), scalar=order.stays[:, a:a + 1],
                                                       in1=own, op0=ALU.add, op1=ALU.max).then_inc(joined, 1)
                    else:
                        nc.vector.scalar_tensor_tensor(out=own, in0=own, scalar=order.some[:, a:a + 1],
                                                       in1=slot(a), op0=ALU.mult, op1=ALU.add).then_inc(joined, 1)

                lags = finish.lags
                for a in range(TILES + lags[-1]):
                    if a < TILES:
                        join(a)
                    for k, lag in enumerate(lags):
                        if 0 <= a - lag < TILES:
                            if k == 0:
                                dve.wait_ge(joined, a - lag + 1)
                            elif acts and k == 1:
                                dve.wait_ge(curved, a - lag + 1)
                            else:
                                dve.wait_ge(stepped[k - 1], a - lag + 1)
                            finish.step(out, a - lag, k).then_inc(stepped[k], 1)


def over_tiles(row, tiles=TILES):
    return row.unsqueeze(1).broadcast_to([P, tiles, D])


def over_row(column):
    return column.unsqueeze(2).broadcast_to([P, TILES, D])


def load_beside(sp, loaded, loads):
    for tile, dram in loads:
        sp.dma_start(tile, dram).then_inc(loaded, 16)
    sp.wait_ge(loaded, 16 * len(loads))


def load_all(nc, *loads):
    with phase(nc, "loaded") as (loaded,), nc.Block() as block:
        @block.sync
        def _(sp):
            load_beside(sp, loaded, loads)


def halves(w, cols):
    return w[:].rearrange("p (s o) -> p s o", s=2)


def by_halves(dram):
    return dram.rearrange("(s p) o -> p s o", p=P)


def spread(dram):
    return dram.partition_broadcast(P)


def row_norm(nc, x, out, gain=None, shift=None, relu=False, stats=None, dram=None, loads=()):
    with ExitStack() as stack:
        given = stats is not None
        if not given:
            stats = buffer(stack, nc, "stats", TILES * 6)
        moments = buffer(stack, nc, "moments", TILES * 2)
        factor, offset = buffer(stack, nc, "factor", TILES), buffer(stack, nc, "offset", TILES)
        chunks = TILES // CHUNK
        by_act = TILES if gain is not None else 2 * CHUNK
        with phase(nc, "variance", "rooted", "step", "ready", "normed", "shaped", "scaled", "stored", "loaded") as \
                (variance, rooted, step, ready, normed, shaped, scaled, stored, loaded), \
                nc.Block() as block:
            mom = moments[:].rearrange("p (a m) -> p a m", m=2)

            @block.vector
            def _(dve):
                if not given:
                    for a in range(TILES):
                        nc.vector.bn_stats(stats[:, a * 6:(a + 1) * 6], tile_at(x, a)).then_inc(step, 1)
                for a in range(TILES):
                    if not given:
                        dve.wait_ge(step, a + 1)
                    last = nc.vector.bn_aggr(moments[:, a * 2:(a + 1) * 2], stats[:, a * 6:(a + 1) * 6])
                done = (0 if given else TILES) + 1
                last.then_inc(step, 1)
                dve.wait_ge(step, done)
                nc.vector.tensor_scalar(out=factor[:], in0=mom[:, :, 1], scalar1=EPS, scalar2=None, op0=ALU.add).then_inc(variance, 1)
                dve.wait_ge(rooted, 1)
                nc.vector.reciprocal(factor[:], factor[:]).then_inc(step, 1)
                dve.wait_ge(step, done + 1)
                nc.vector.scalar_tensor_tensor(out=offset[:], in0=mom[:, :, 0], scalar=-1.0, in1=factor[:], op0=ALU.mult, op1=ALU.mult).then_inc(ready, 1)
                for a in range(by_act, TILES):
                    nc.vector.tensor_scalar(out=tile_at(out, a), in0=tile_at(x, a), scalar1=moments[:, 2 * a:2 * a + 1],
                                            scalar2=factor[:, a:a + 1], op0=ALU.subtract, op1=ALU.mult).then_inc(scaled, 1)
                if gain is not None:
                    for c in range(chunks):
                        part = bulk(tile_at(out, c * CHUNK, CHUNK), CHUNK)
                        dve.wait_ge(normed, (c + 1) * CHUNK)
                        nc.vector.tensor_tensor(out=part, in0=part, in1=over_tiles(gain, CHUNK), op=ALU.mult).then_inc(step, 1)
                        dve.wait_ge(step, done + 2 + c)
                        nc.vector.tensor_tensor(out=part, in0=part, in1=over_tiles(shift, CHUNK), op=ALU.add).then_inc(shaped, 1)

            if loads:
                @block.sync
                def _(sp):
                    load_beside(sp, loaded, loads)

            if dram is not None:
                @block.sync
                def _(sp):
                    by_dve = [(at, scaled, at + CHUNK - by_act) for at in range(by_act, TILES, CHUNK)]
                    of_act = [(at, normed, at + CHUNK) for at in range(0, by_act, CHUNK)]
                    for at, done, count in sorted(by_dve + of_act, key=lambda part: part[2]):
                        sp.wait_ge(done, count)
                        whole = min(CHUNK, TILES - 1 - at)
                        sp.dma_start(dram[at * P:(at + whole) * P, :].rearrange("(a p) d -> p a d", p=P),
                                     bulk(tile_at(out, at, whole), whole)).then_inc(stored, 16)
                    sp.dma_start(dram[(TILES - 1) * P:N, :], tile_at(out, TILES - 1)[0:LAST, :]).then_inc(stored, 16)
                    sp.wait_ge(stored, 16 * (TILES // CHUNK + 1))

            @block.scalar
            def _(act):
                act.wait_ge(variance, 1)
                nc.scalar.activation(factor[:], factor[:], ACT.Sqrt).then_inc(rooted, 1)
                act.wait_ge(ready, 1)

                def rectify(c):
                    act.wait_ge(shaped, c + 1)
                    nc.scalar.activation(tile_at(out, c * CHUNK, CHUNK), tile_at(out, c * CHUNK, CHUNK), ACT.Relu)
                for a in range(by_act):
                    nc.scalar.activation(tile_at(out, a), tile_at(x, a), ACT.Identity, bias=offset[:, a:a + 1],
                                         scale=factor[:, a:a + 1]).then_inc(normed, 1)
                if relu:
                    for c in range(chunks):
                        rectify(c)


def add_all(nc, out, *steps):
    with phase(nc, "step") as (step,), nc.Block() as block:
        @block.vector
        def _(dve):
            then = counted_steps(dve, step)
            for other, op in steps:
                then(nc.vector.tensor_tensor(out=bulk(out[:]), in0=bulk(out[:]), in1=other, op=op))


def neighbour_rows(nc, env, y, turned_y, weights, parts, table, own=None, factor=None):
    depth = 4
    with ExitStack() as stack:
        ring = [] if own is not None else [buffer(stack, nc, "staged", D) for _ in range(depth)]

        def staged(a):
            return tile_at(own, a) if own is not None else ring[a % depth][:]

        with phase(nc, "turned", "copied", "filled", "kept", *[f"stored{b}" for b in range(depth)]) as \
                (turned, copied, filled, kept, *stored), nc.Block() as block:
            @block.tensor
            def _(pe):
                def turn(a):
                    if a >= depth:
                        pe.wait_ge(copied, a - depth + 1)
                    for s in range(2):
                        last = nc.tensor.transpose(env.bank[a % depth][:, s * P:(s + 1) * P], y[:, a * D + s * P:a * D + (s + 1) * P], env.ident[:])
                    last.then_inc(turned, 1)

                turn(0)
                for a in range(TILES):
                    if a + 1 < TILES:
                        turn(a + 1)
                    pe.wait_ge(copied, a + 1)
                    if a >= depth:
                        pe.wait_ge(kept, a - depth + 1)
                    half_product(nc, env.bank[depth + a % depth], turned_y, weights, parts, a, 0).then_inc(filled, 1)

            @block.scalar
            def _(act):
                for a in range(TILES):
                    act.wait_ge(turned, a + 1)
                    nc.scalar.copy(tile_at(turned_y, a), env.bank[a % depth][:, 0:D]).then_inc(copied, 1)

            @block.vector
            def _(dve):
                for a in range(TILES):
                    dve.wait_ge(filled, a + 1)
                    rows = env.bank[depth + a % depth][:, 0:D]
                    if own is not None:
                        nc.vector.tensor_scalar(out=staged(a), in0=rows, scalar1=factor[:, a:a + 1], scalar2=None, op0=ALU.mult).then_inc(kept, 1)
                        continue
                    if a >= depth:
                        dve.wait_ge(stored[a % depth], 16 * (a // depth))
                    nc.vector.tensor_copy(staged(a), rows).then_inc(kept, 1)

            @block.sync
            def _(sp):
                for a in range(TILES):
                    sp.wait_ge(kept, a + 1)
                    sp.dma_start(table[a * P:(a + 1) * P, :], staged(a)).then_inc(stored[a % depth], 16)
                for b in range(depth):
                    sp.wait_ge(stored[b], 16 * len(range(b, TILES, depth)))


def half_product(nc, bank, turned_y, weights, parts, a, part):
    for s in range(2):
        last = nc.tensor.matmul(bank[:, 0:D], turned_y[:, a * D + s * P:a * D + (s + 1) * P],
                                weights[:, (parts * s + part) * D:(parts * s + part + 1) * D], start=s == 0, stop=s == 1)
    return last


def relative_layer(nc, env, order, y, best, own, weights, gain, shift, table, states, loads):
    neighbour_rows(nc, env, y, best, weights, 2, table)
    with ExitStack() as stack:
        tail = buffer(stack, nc, "tail", D)
        edge_pass(nc, env, order, table, states, "max", tail, loads, (best, weights, own))
        collect(nc, env, order, states, "max", tail, best, FinishRelative(nc, env, order, own))
    with ExitStack() as stack:
        mean, scale = buffer(stack, nc, "mean", D), buffer(stack, nc, "scale", D)
        chunks = TILES // CHUNK
        with phase(nc, "centred", "squared", "summed", "variance", "rooted", "step", "shaped") as \
                (centred, squared, summed, variance, rooted, step, shaped), nc.Block() as block:
            @block.vector
            def _(dve):
                then = counted_steps(dve, step)
                then(nc.vector.tensor_scalar(out=mean[:], in0=env.bank[0][:, 0:D], scalar1=1.0 / N, scalar2=None, op0=ALU.mult))
                for c in range(chunks):
                    part = bulk(tile_at(best, c * CHUNK, CHUNK), CHUNK)
                    nc.vector.tensor_tensor(out=part, in0=part, in1=over_tiles(mean[:], CHUNK), op=ALU.subtract).then_inc(centred, 1)
                dve.wait_ge(summed, 1)
                nc.vector.tensor_scalar(out=scale[:], in0=env.bank[1][:, 0:D], scalar1=1.0 / N, scalar2=EPS, op0=ALU.mult, op1=ALU.add).then_inc(variance, 1)
                dve.wait_ge(rooted, 1)
                then(nc.vector.reciprocal(scale[:], scale[:]))
                then(nc.vector.tensor_tensor(out=scale[:], in0=scale[:], in1=gain[:], op=ALU.mult))
                for c in range(chunks):
                    part = bulk(tile_at(best, c * CHUNK, CHUNK), CHUNK)
                    then(nc.vector.tensor_tensor(out=part, in0=part, in1=over_tiles(scale[:], CHUNK), op=ALU.mult))
                    nc.vector.tensor_tensor(out=part, in0=part, in1=over_tiles(shift[:], CHUNK), op=ALU.add).then_inc(shaped, 1)

            @block.tensor
            def _(pe):
                for a in range(TILES):
                    pe.wait_ge(squared, a // CHUNK + 1)
                    last = column_sum(nc, env, env.bank[1], own, a)
                last.then_inc(summed, 1)

            @block.scalar
            def _(act):
                for c in range(chunks):
                    act.wait_ge(centred, c + 1)
                    nc.scalar.activation(tile_at(own, c * CHUNK, CHUNK), tile_at(best, c * CHUNK, CHUNK), ACT.Square).then_inc(squared, 1)
                act.wait_ge(variance, 1)
                nc.scalar.activation(scale[:], scale[:], ACT.Sqrt).then_inc(rooted, 1)
                for c in range(chunks):
                    act.wait_ge(shaped, c + 1)
                    nc.scalar.activation(tile_at(y, c * CHUNK, CHUNK), tile_at(best, c * CHUNK, CHUNK), ACT.Relu)


def relative_block(nc, env, order, y, best, own, theta_dram, phi_dram, gains, shifts, table, states, layers=LAYERS):
    with ExitStack() as stack:
        weights = buffer(stack, nc, "weights", 2 * 2 * D)
        gain, shift = buffer(stack, nc, "gain", D), buffer(stack, nc, "shift", D)
        halves_of = weights[:].rearrange("p (s o) -> p s o", s=2)
        with nc.Fori(0, layers) as layer:
            def of_layer(dram):
                return dram[bass.ds(layer, 1)].squeeze(0)
            with phase(nc, "loaded", "step") as (loaded, step), nc.Block() as block:
                @block.sync
                def _(sp):
                    sp.dma_start(halves_of[:, :, 0:D], by_halves(of_layer(theta_dram))).then_inc(loaded, 16)
                    sp.dma_start(halves_of[:, :, D:], by_halves(of_layer(phi_dram))).then_inc(loaded, 16)

                @block.vector
                def _(dve):
                    dve.wait_ge(loaded, 32)
                    nc.vector.tensor_tensor(out=halves_of[:, :, D:], in0=halves_of[:, :, D:], in1=halves_of[:, :, 0:D], op=ALU.subtract).then_inc(step, 1)
                    dve.wait_ge(step, 1)
            relative_layer(nc, env, order, y, best, own, weights, gain, shift, table, states,
                           [(gain[:], spread(of_layer(gains))), (shift[:], spread(of_layer(shifts)))])


def typed_rows(nc, env, y, turned_y, own, inverse, basis_dram, att_dram, root_dram, table):
    pair, banks, slots = 2 * D, 5, 10
    chunks = TYPES // 2
    reads = TILES
    with ExitStack() as stack:
        basis, att = buffer(stack, nc, "basis", BASES * 2 * D), buffer(stack, nc, "att", TYPES * BASES)
        weights = [buffer(stack, nc, "weights", 2 * pair) for _ in range(2)]
        root = buffer(stack, nc, "root", 2 * D)
        staged = [buffer(stack, nc, "staged", pair) for _ in range(slots)]
        names = ["loaded", "root_loaded", "turned", "copied", "mixed", "filled", "read_act", "read_dve", "scaled",
                 "rooted", "joined", "held"] + [f"stored{s}" for s in range(slots)]
        with phase(nc, *names) as sems, nc.Block() as block:
            loaded, root_loaded, turned, copied, mixed, filled, read_act, read_dve, scaled, rooted, joined, held = sems[:12]
            stored = sems[12:]
            last_pair = chunks // 2 - 1

            def first(i):
                return isinstance(i, int) and i == 0

            def over_pairs(engine, body):
                body(0)
                with engine.Fori(1, last_pair) as i:
                    body(i)
                body(last_pair)

            def wait_read(engine, i, m):
                if m >= 0:
                    engine.wait_ge((read_act, read_dve)[m % 2], i * reads + m // 2 + 1)
                    engine.sem_inc(held, 1)

            @block.sync
            def _(sp):
                sp.dma_start(att[:], spread(att_dram.rearrange("r b -> (r b)"))).then_inc(loaded, 16)
                sp.dma_start(basis[:].rearrange("p (b s o) -> p b s o", b=BASES, s=2), basis_dram.rearrange("b (s p) o -> p b s o", p=P)).then_inc(loaded, 16)
                sp.dma_start(halves(root, D), by_halves(root_dram)).then_inc(root_loaded, 16)
                rows_of = table.rearrange("(a p r) o -> a p (r o)", p=P, r=TYPES)

                def body(i):
                    for h in range(2):
                        for a in range(TILES):
                            m = h * TILES + a
                            wait_read(sp, i, m)
                            sp.dma_start(rows_of[a][:, bass.ds((2 * i + h) * pair, pair)], staged[m % slots][:]).then_inc(stored[m % slots], 16)
                with sp.Fori(0, chunks // 2) as i:
                    body(i)
                for s in range(slots):
                    sp.wait_ge(stored[s], 16 * (chunks * TILES // slots))
                sp.wait_ge(root_loaded, 16)

            @block.tensor
            def _(pe):
                for a in range(TILES):
                    if a >= banks:
                        pe.wait_ge(copied, a - banks + 1)
                    for s in range(2):
                        last = nc.tensor.transpose(env.bank[a % banks][:, s * P:(s + 1) * P], y[:, a * D + s * P:a * D + (s + 1) * P], env.ident[:])
                    last.then_inc(turned, 1)
                pe.wait_ge(copied, TILES)
                pe.wait_ge(root_loaded, 16)

                def body(i):
                    final = isinstance(i, int) and i == last_pair
                    for h in range(2):
                        pe.wait_ge(mixed, (2 * i + h + 1) * (2 * BASES))
                        pe.sem_inc(held, 1)
                        for a in range(TILES):
                            m = h * TILES + a
                            bank = env.bank[a % banks]
                            if m >= banks:
                                wait_read(pe, i, m - banks)
                            elif not first(i):
                                wait_read(pe, i - 1, m - banks + 2 * TILES)
                            if final and h == 1 and a >= banks:
                                pe.wait_ge(scaled, a - banks + 1)
                            for s in range(2):
                                last = nc.tensor.matmul(bank[:, 0:pair], turned_y[:, a * D + s * P:a * D + (s + 1) * P],
                                                        weights[h][:, s * pair:(s + 1) * pair], start=s == 0, stop=s == 1)
                            last.then_inc(filled, 1)
                            if final and h == 1:
                                if a >= 2:
                                    pe.wait_ge(joined, a - 1)
                                for s in range(2):
                                    last = nc.tensor.matmul(env.bank[banks + a % 2][:, 0:D], turned_y[:, a * D + s * P:a * D + (s + 1) * P],
                                                            root[:, s * D:(s + 1) * D], start=s == 0, stop=s == 1)
                                last.then_inc(rooted, 1)
                over_pairs(pe, body)

            def copy_out(engine, copy, read, i, h, a):
                m = h * TILES + a
                engine.wait_ge(filled, i * (2 * TILES) + m + 1)
                engine.sem_inc(held, 1)
                if m >= slots or not first(i):
                    engine.wait_ge(stored[m % slots], (i * (2 * TILES // slots) + m // slots) * 16)
                    engine.sem_inc(held, 1)
                copy(staged[m % slots][:], env.bank[a % banks][:, 0:pair]).then_inc(read, 1)

            @block.scalar
            def _(act):
                for a in range(TILES):
                    act.wait_ge(turned, a + 1)
                    nc.scalar.copy(tile_at(turned_y, a), env.bank[a % banks][:, 0:D]).then_inc(copied, 1)

                def body(i):
                    for m in range(0, 2 * TILES, 2):
                        copy_out(act, nc.scalar.copy, read_act, i, m // TILES, m % TILES)
                over_pairs(act, body)

            @block.vector
            def _(dve):
                def mix(c, h, k):
                    b, r = k // 2, k % 2
                    if k == 0 and (not isinstance(c, int) or c >= 2):
                        dve.wait_ge(filled, (c - 1) * TILES)
                        dve.sem_inc(held, 1)
                    w_r = weights[h][:].rearrange("p (s o) -> p s o", s=2)[:, :, r * D:(r + 1) * D]
                    basis_b = basis[:, b * 2 * D:(b + 1) * 2 * D].rearrange("p (s o) -> p s o", s=2)
                    factor = att[:, bass.ds(c * (2 * BASES) + r * BASES + b, 1)]
                    if b == 0:
                        nc.vector.tensor_scalar(out=w_r, in0=basis_b, scalar1=factor, scalar2=None, op0=ALU.mult).then_inc(mixed, 1)
                    else:
                        dve.wait_ge(mixed, c * (2 * BASES) + k - 1)
                        nc.vector.scalar_tensor_tensor(out=w_r, in0=basis_b, scalar=factor, in1=w_r,
                                                       op0=ALU.mult, op1=ALU.add).then_inc(mixed, 1)

                def body(i):
                    final = isinstance(i, int) and i == last_pair
                    for h in range(2):
                        ahead = iter(range(0 if final and h == 1 else 2 * BASES))
                        for a in range(TILES):
                            if (h * TILES + a) % 2:
                                copy_out(dve, nc.vector.tensor_copy, read_dve, i, h, a)
                                for k in itertools.islice(ahead, 2):
                                    mix(2 * i + h + 1, 1 - h, k)
                            if final and h == 1:
                                wait_read(dve, i, TILES + a)
                                nc.vector.tensor_scalar(out=tile_at(own, a), in0=env.bank[a % banks][:, D:pair], scalar1=inverse[:, a:a + 1],
                                                        scalar2=None, op0=ALU.mult).then_inc(scaled, 1)
                                dve.wait_ge(rooted, a + 1)
                                dve.wait_ge(scaled, a + 1)
                                nc.vector.tensor_tensor(out=tile_at(own, a), in0=tile_at(own, a), in1=env.bank[banks + a % 2][:, 0:D],
                                                        op=ALU.add).then_inc(joined, 1)
                dve.wait_ge(loaded, 32)
                for k in range(2 * BASES):
                    mix(0, 0, k)
                over_pairs(dve, body)


def relational_layer(nc, env, order, y, out, own, basis_dram, att_dram, root_dram, bias_dram, gain_dram, shift_dram,
                     table, states):
    typed_rows(nc, env, y, out, own, order.inverse, basis_dram, att_dram, root_dram, table)
    with ExitStack() as stack:
        tail = buffer(stack, nc, "tail", D)
        bias, gain, shift = (buffer(stack, nc, n, D) for n in ("bias", "gain", "shift"))
        stats = buffer(stack, nc, "stats", TILES * 6)
        finish = FinishRelational(nc, order, own, bias, y, stats)
        edge_pass(nc, env, order, table, states, "weighted", tail,
                  [(bias[:], spread(bias_dram)), (gain[:], spread(gain_dram)), (shift[:], spread(shift_dram))], prepare=finish.prepare)
        collect(nc, env, order, states, "weighted", tail, out, finish)
        row_norm(nc, out, y, gain[:], shift[:], relu=True, stats=stats)


def normalised_layer(nc, env, order, x, out, own, w_dram, bias_dram, table, states):
    with ExitStack() as stack:
        weights, bias, tail = buffer(stack, nc, "weights", 2 * D), buffer(stack, nc, "bias", D), buffer(stack, nc, "tail", D)
        load_all(nc, (halves(weights, D), by_halves(w_dram)))
        neighbour_rows(nc, env, x, out, weights, 1, table, own, order.root_inverse)
        stats = buffer(stack, nc, "stats", TILES * 6)
        finish = FinishNormalised(nc, order, own, bias, x, stats)
        edge_pass(nc, env, order, table, states, "sum", tail, [(bias[:], spread(bias_dram))], prepare=finish.prepare)
        collect(nc, env, order, states, "sum", tail, out, finish)
        row_norm(nc, out, x, stats=stats)


WIDE = HEADS * (DH + 1)
STATE = WIDE + HEADS
QV = D + WIDE
FEW = 8


def by_head(ap, rows=1):
    return ap.rearrange("p (h d) -> p h d", d=DH + 1)


def attention_pass(nc, env, order, qv_table, k_table, states, tail, spare):
    with ExitStack() as stack:
        def ring(name, cols, count=RING, dt=FP32):
            return [buffer(stack, nc, name, cols, dt) for _ in range(count)]
        index, qv, k = ring("index", 2 * FEW, dt=I32), ring("qv", FEW * QV), ring("k", FEW * D)
        lent = spare[:].shape[1] // (FEW * STATE)
        state = [spare[:, b * FEW * STATE:(b + 1) * FEW * STATE] for b in range(lent)] + ring("state", FEW * STATE, RING - lent)
        top, score, power = ring("top", (FEW + 1) * HEADS), ring("score", FEW * HEADS), ring("power", 2 * FEW * HEADS)
        groups = STEPS // FEW
        body = groups // RING
        names = ["indexed", "scores", "topped", "differed", "raised", "chain", "marked", "held", "copied"] \
            + [f"gathered{b}" for b in range(RING)] + [f"stored{b}" for b in range(RING)]
        with phase(nc, *names) as sems, nc.Block() as block:
            indexed, scores, topped, differed, raised, chain, marked, held, copied = sems[:9]
            gathered, stored = sems[9:9 + RING], sems[9 + RING:]

            def first(i):
                return isinstance(i, int) and i == 0

            @block.gpsimd
            def _(pool):
                def gather(i, b):
                    g = RING * i + b
                    pool.wait_ge(indexed, g + 1)
                    pool.sem_inc(held, 1)
                    for u in range(FEW):
                        pool.indirect_dma_start(
                            out=qv[b][:, u * QV:(u + 1) * QV], out_offset=None, in_=qv_table,
                            in_offset=bass.IndirectOffsetOnAxis(ap=index[b][:, u:u + 1], axis=0)).then_inc(gathered[b], 16)
                        pool.indirect_dma_start(
                            out=k[b][:, u * D:(u + 1) * D], out_offset=None, in_=k_table,
                            in_offset=bass.IndirectOffsetOnAxis(ap=index[b][:, FEW + u:FEW + u + 1], axis=0)).then_inc(gathered[b], 16)
                for b in range(RING):
                    gather(0, b)
                with pool.Fori(1, body) as i:
                    for b in range(RING):
                        gather(i, b)

            @block.vector
            def _(dve):
                def look(g, b):
                    nc.vector.tensor_copy(index[b][:, 0:FEW], order.source[:, bass.ds(g * FEW, FEW)])
                    nc.vector.tensor_copy(index[b][:, FEW:], order.node[:, bass.ds(g * FEW, FEW)]).then_inc(indexed, 1)

                def multiply_scores(i, b):
                    g = RING * i + b
                    dve.wait_ge(gathered[b], (i + 1) * (2 * FEW * 16))
                    dve.sem_inc(held, 1)
                    q3 = qv[b][:].rearrange("p (u c) -> p u c", u=FEW)[:, :, 0:D]
                    nc.vector.tensor_tensor(out=bulk(k[b][:], FEW), in0=bulk(k[b][:], FEW), in1=q3, op=ALU.mult).then_inc(scores, 1)
                    if not first(i):
                        dve.wait_ge(copied, g - RING + 1)
                        dve.sem_inc(held, 1)
                    dve.wait_ge(scores, 2 * g + 1)
                    nc.vector.tensor_reduce(out=score[b][:], in_=k[b][:].rearrange("p (s d) -> p s d", d=DH), axis=AX.X, op=ALU.add).then_inc(scores, 1)

                def top_step(i, b, u):
                    g = RING * i + b
                    if u == 0:
                        dve.wait_ge(scores, 2 * g + 2)
                        dve.sem_inc(held, 1)
                    dve.wait_ge(topped, (FEW + 1) * g + u + 1)
                    before = top[b][:, u * HEADS:(u + 1) * HEADS] if u else top[b - 1][:, FEW * HEADS:]
                    nc.vector.scalar_tensor_tensor(
                        out=top[b][:, (u + 1) * HEADS:(u + 2) * HEADS], in0=before, scalar=order.anew[:, bass.ds(g * FEW + u, 1)],
                        in1=score[b][:, u * HEADS:(u + 1) * HEADS], op0=ALU.add, op1=ALU.max).then_inc(topped, 1)

                def exponents(i, b):
                    g = RING * i + b
                    nc.vector.tensor_copy(top[b][:, 0:HEADS], top[b - 1][:, FEW * HEADS:]).then_inc(topped, 1)
                    dve.wait_ge(topped, (FEW + 1) * (g + 1) + 1)
                    new = top[b][:, HEADS:]
                    nc.vector.tensor_tensor(out=power[b][:, 0:FEW * HEADS], in0=top[b][:, 0:FEW * HEADS], in1=new, op=ALU.subtract).then_inc(marked, 1)
                    nc.vector.tensor_tensor(out=power[b][:, FEW * HEADS:], in0=score[b][:], in1=new, op=ALU.subtract).then_inc(differed, 1)
                    dve.wait_ge(marked, g + 1)
                    scale = power[b][:, 0:FEW * HEADS].rearrange("p (u h) -> p u h", u=FEW)
                    nc.vector.tensor_tensor(out=scale, in0=scale,
                                            in1=order.anew[:, bass.ds(g * FEW, FEW)].unsqueeze(2).broadcast_to([P, FEW, HEADS]),
                                            op=ALU.add).then_inc(differed, 1)

                def weigh(b, u):
                    value = by_head(qv[b][:, u * QV + D:(u + 1) * QV])
                    nc.vector.tensor_tensor(
                        out=value, in0=value,
                        in1=power[b][:, (FEW + u) * HEADS:(FEW + u + 1) * HEADS].unsqueeze(2).broadcast_to([P, HEADS, DH + 1]),
                        op=ALU.mult).then_inc(chain, 1)

                def steps(scored, folded, more=True):
                    if scored:
                        multiply_scores(*scored)
                    if folded:
                        i, b = folded
                        g = RING * i + b
                        dve.wait_ge(raised, g + 1)
                        dve.sem_inc(held, 1)
                        if not first(i):
                            dve.wait_ge(stored[b], i * 16)
                            dve.sem_inc(held, 1)
                        weigh(b, 0)
                    for u in range(FEW):
                        if folded:
                            before = state[b][:, (u - 1) * STATE:(u - 1) * STATE + WIDE] if u else state[b - 1][:, (FEW - 1) * STATE:(FEW - 1) * STATE + WIDE]
                            now = state[b][:, u * STATE:u * STATE + WIDE]
                            dve.wait_ge(chain, g * (3 * FEW) + 3 * u + 1)
                            nc.vector.tensor_tensor(out=by_head(now), in0=by_head(before),
                                                    in1=power[b][:, u * HEADS:(u + 1) * HEADS].unsqueeze(2).broadcast_to([P, HEADS, DH + 1]),
                                                    op=ALU.mult).then_inc(chain, 1)
                        if scored:
                            top_step(*scored, u)
                        if folded:
                            dve.wait_ge(chain, g * (3 * FEW) + 3 * u + 3)
                            nc.vector.tensor_tensor(out=now, in0=now, in1=qv[b][:, u * QV + D:(u + 1) * QV], op=ALU.add).then_inc(chain, 1)
                            if u < FEW - 1:
                                weigh(b, u + 1)
                    if folded and more:
                        look(g + RING, b)
                    if scored:
                        exponents(*scored)

                nc.vector.memset(state[RING - 1][:, (FEW - 1) * STATE:], 0.0).then_inc(chain, 1)
                nc.vector.memset(top[RING - 1][:, FEW * HEADS:], NEG).then_inc(topped, 1)
                for b in range(RING):
                    look(b, b)
                steps((0, 0), None)
                for b in range(1, RING):
                    steps((0, b), (0, b - 1))
                with dve.Fori(1, body - 1) as i:
                    steps((i, 0), (i - 1, RING - 1))
                    for b in range(1, RING):
                        steps((i, b), (i, b - 1))
                steps((body - 1, 0), (body - 2, RING - 1))
                for b in range(1, RING):
                    steps((body - 1, b), (body - 1, b - 1), more=False)
                steps(None, (body - 1, RING - 1), more=False)
                dve.wait_ge(chain, 3 * STEPS + 1)
                dve.wait_ge(copied, groups)
                nc.vector.tensor_copy(tail[:], state[RING - 1][:, (FEW - 1) * STATE:])

            @block.scalar
            def _(act):
                def raise_group(i, b):
                    g = RING * i + b
                    act.wait_ge(differed, 2 * g + 2)
                    act.sem_inc(held, 1)
                    nc.scalar.activation(power[b][:], power[b][:], ACT.Exp).then_inc(raised, 1)
                    if not first(i):
                        act.wait_ge(stored[b], i * 16)
                        act.sem_inc(held, 1)
                    nc.scalar.copy(state[b][:].rearrange("p (u c) -> p u c", u=FEW)[:, :, WIDE:],
                                   top[b][:, HEADS:].rearrange("p (u h) -> p u h", u=FEW)).then_inc(copied, 1)
                for b in range(RING):
                    raise_group(0, b)
                with act.Fori(1, body) as i:
                    for b in range(RING):
                        raise_group(i, b)

            @block.sync
            def _(sp):
                blocks = states.rearrange("(p t) d -> p (t d)", t=STEPS)
                with sp.Fori(0, body) as i:
                    for b in range(RING):
                        g = RING * i + b
                        sp.wait_ge(chain, (g + 1) * (3 * FEW) + 1)
                        sp.sem_inc(held, 1)
                        sp.wait_ge(copied, g + 1)
                        sp.sem_inc(held, 1)
                        sp.dma_start(blocks[:, bass.ds(g * (FEW * STATE), FEW * STATE)], state[b][:]).then_inc(stored[b], 16)
                for b in range(RING):
                    sp.wait_ge(stored[b], body * 16)


def attention_collect(nc, env, order, states, tail, x, out, loads):
    third = WIDE // 3
    with ExitStack() as stack:
        def sb(name, cols, dt=FP32):
            return buffer(stack, nc, name, cols, dt)
        own, other = sb("own", TILES * STATE), sb("other", TILES * STATE)
        top_in, rise, fall = sb("top_in", P + 1), sb("rise", P), sb("fall", P)
        spread_heads, factors, prefix = sb("spread_heads", WIDE), sb("factors", 3 * P), sb("prefix", 3 * (P + 1))
        carry, into = sb("carry", STATE), sb("into", HEADS)
        tops, part = sb("tops", 2 * TILES * HEADS), sb("part", TILES * HEADS)
        hot = sb("hot", ROWS)
        picks = 3

        names = ("differed", "shaped", "turned", "step", "raised", "expanded", "back", "carried", "marked", "picked", "kept", "exped", "loaded") + tuple(f"gathered{c}" for c in range(TILES // CHUNK))
        with phase(nc, *names) as (differed, shaped, turned, step, raised, expanded, back, carried, marked, picked, kept, exped, loaded, *gathered_chunks), \
                nc.Block() as block:
            @block.sync
            def _(sp):
                load_beside(sp, loaded, loads)

            @block.gpsimd
            def _(pool):
                pool.memset(spread_heads[0:HEADS, :], 1.0).then_inc(shaped, 1)
                pool.wait_ge(shaped, 1)
                pool.affine_select(out=spread_heads[0:HEADS, :], in_=spread_heads[0:HEADS, :], compare_op=ALU.is_ge, fill=0.0,
                                   base=0, pattern=[[1, WIDE]], channel_multiplier=-(DH + 1)).then_inc(shaped, 1)
                pool.wait_ge(shaped, 2)
                pool.affine_select(out=spread_heads[0:HEADS, :], in_=spread_heads[0:HEADS, :], compare_op=ALU.is_ge, fill=0.0,
                                   base=DH, pattern=[[-1, WIDE]], channel_multiplier=DH + 1).then_inc(shaped, 1)
                for a in range(TILES):
                    pool.indirect_dma_start(out=own[:, a * STATE:(a + 1) * STATE], out_offset=None, in_=states,
                                            in_offset=bass.IndirectOffsetOnAxis(ap=order.last[:, a:a + 1], axis=0)).then_inc(gathered_chunks[a // CHUNK], 16)

            @block.tensor
            def _(pe):
                nc.tensor.transpose(env.bank[0][0:HEADS, 0:P], tail[:, WIDE:], env.ident[:]).then_inc(turned, 1)
                pe.wait_ge(raised, 2)
                pe.wait_ge(shaped, 3)
                nc.tensor.transpose(env.bank[1][:, 0:HEADS], fall[0:HEADS, :], env.ident[0:HEADS, 0:HEADS]).then_inc(expanded, 1)
                nc.tensor.transpose(env.bank[1][:, HEADS:2 * HEADS], top_in[0:HEADS, 0:P], env.ident[0:HEADS, 0:HEADS]).then_inc(expanded, 1)
                for s in range(3):
                    nc.tensor.matmul(env.bank[2][0:third, s * P:(s + 1) * P], spread_heads[0:HEADS, s * third:(s + 1) * third],
                                     rise[0:HEADS, :], start=True, stop=True).then_inc(expanded, 1)
                pe.wait_ge(step, 9)
                for s in range(3):
                    nc.tensor.transpose(env.bank[3][0:third, s * P:(s + 1) * P], tail[:, s * third:(s + 1) * third], env.ident[:]).then_inc(turned, 1)
                pe.wait_ge(step, 12)
                for s in range(3):
                    last = nc.tensor.transpose(env.bank[4][:, s * third:(s + 1) * third], prefix[0:third, s * (P + 1):s * (P + 1) + P],
                                               env.ident[0:third, 0:third])
                last.then_inc(back, 1)
                pe.wait_ge(carried, 2)
                pe.wait_ge(marked, 1)
                for a in range(TILES):
                    if a >= picks:
                        pe.wait_ge(kept, a - picks + 1)
                    nc.tensor.matmul(env.bank[5 + a % picks][:, 0:STATE], hot[:, a * P:(a + 1) * P], carry[:], start=True, stop=True).then_inc(picked, 1)

            @block.scalar
            def _(act):
                act.wait_ge(step, 6)
                nc.scalar.activation(rise[0:HEADS, :], rise[0:HEADS, :], ACT.Exp).then_inc(raised, 1)
                nc.scalar.activation(fall[0:HEADS, :], fall[0:HEADS, :], ACT.Exp).then_inc(raised, 1)

                def raise_tops(c):
                    act.wait_ge(differed, c + 1)
                    chunk = tops[:, c * 2 * CHUNK * HEADS:(c + 1) * 2 * CHUNK * HEADS]
                    nc.scalar.activation(chunk, chunk, ACT.Exp).then_inc(exped, 1)
                for a in range(TILES):
                    act.wait_ge(picked, a + 1)
                    nc.scalar.copy(other[:, a * STATE:(a + 1) * STATE], env.bank[5 + a % picks][:, 0:STATE]).then_inc(kept, 1)
                    if a >= CHUNK and a % CHUNK == 1:
                        raise_tops(a // CHUNK - 1)
                raise_tops(TILES // CHUNK - 1)

            @block.vector
            def _(dve):
                nc.vector.memset(top_in[:], NEG).then_inc(step, 1)
                nc.vector.memset(prefix[:], 0.0).then_inc(step, 1)
                nc.vector.tensor_scalar(out=hot[:], in0=order.end_row[:], scalar1=env.own[:, 0:1], scalar2=None, op0=ALU.is_equal).then_inc(marked, 1)
                dve.wait_ge(turned, 1)
                dve.wait_ge(step, 2)
                nc.vector.tensor_tensor_scan(out=top_in[0:HEADS, 1:], data0=order.shut_row[0:HEADS, :], data1=env.bank[0][0:HEADS, 0:P],
                                             initial=NEG, op0=ALU.add, op1=ALU.max).then_inc(step, 1)
                dve.wait_ge(step, 3)
                nc.vector.tensor_tensor(out=fall[0:HEADS, :], in0=env.bank[0][0:HEADS, 0:P], in1=top_in[0:HEADS, 1:],
                                        op=ALU.subtract).then_inc(step, 1)
                nc.vector.tensor_tensor(out=rise[0:HEADS, :], in0=top_in[0:HEADS, 0:P], in1=top_in[0:HEADS, 1:],
                                        op=ALU.subtract).then_inc(step, 1)
                dve.wait_ge(step, 5)
                nc.vector.tensor_tensor(out=rise[0:HEADS, :], in0=rise[0:HEADS, :], in1=order.shut_row[0:HEADS, :], op=ALU.add).then_inc(step, 1)
                dve.wait_ge(expanded, 5)
                nc.vector.tensor_copy(into[:], env.bank[1][:, 0:HEADS]).then_inc(step, 1)
                nc.vector.tensor_copy(carry[:, WIDE:], env.bank[1][:, HEADS:2 * HEADS]).then_inc(carried, 1)
                nc.vector.tensor_copy(factors[0:third, :], env.bank[2][0:third, 0:3 * P]).then_inc(step, 1)
                dve.wait_ge(step, 8)
                nc.vector.tensor_tensor(out=by_head(tail[:, 0:WIDE]), in0=by_head(tail[:, 0:WIDE]),
                                        in1=into[:].unsqueeze(2).broadcast_to([P, HEADS, DH + 1]), op=ALU.mult).then_inc(step, 1)
                dve.wait_ge(turned, 4)
                for s in range(3):
                    nc.vector.tensor_tensor_scan(out=prefix[0:third, s * (P + 1) + 1:(s + 1) * (P + 1)], data0=factors[0:third, s * P:(s + 1) * P],
                                                 data1=env.bank[3][0:third, s * P:(s + 1) * P], initial=0.0,
                                                 op0=ALU.mult, op1=ALU.add).then_inc(step, 1)
                dve.wait_ge(back, 1)
                nc.vector.tensor_copy(carry[:, 0:WIDE], env.bank[4][:, 0:WIDE]).then_inc(carried, 1)

                of_tile = lambda t, c, width: t[:, c * CHUNK * width:(c + 1) * CHUNK * width].rearrange("p (a c) -> p a c", a=CHUNK)
                count = 12
                done = {}

                def counted(instruction, c, what):
                    nonlocal count
                    instruction.then_inc(step, 1)
                    count += 1
                    done[c, what] = count

                def compare_tops(c):
                    dve.wait_ge(gathered_chunks[c], 16 * CHUNK)
                    dve.wait_ge(kept, (c + 1) * CHUNK)
                    own_top, other_top = of_tile(own, c, STATE)[:, :, WIDE:], of_tile(other, c, STATE)[:, :, WIDE:]
                    larger = of_tile(part, c, HEADS)
                    counted(nc.vector.tensor_tensor(out=other_top, in0=other_top,
                                                    in1=order.stays[:, c * CHUNK:(c + 1) * CHUNK].unsqueeze(2).broadcast_to([P, CHUNK, HEADS]),
                                                    op=ALU.add), c, "stays")
                    dve.wait_ge(step, done[c, "stays"])
                    counted(nc.vector.tensor_tensor(out=larger, in0=own_top, in1=other_top, op=ALU.max), c, "larger")
                    dve.wait_ge(step, done[c, "larger"])
                    nc.vector.tensor_tensor(out=of_tile(tops, c, 2 * HEADS)[:, :, 0:HEADS], in0=own_top, in1=larger, op=ALU.subtract)
                    nc.vector.tensor_tensor(out=of_tile(tops, c, 2 * HEADS)[:, :, HEADS:], in0=other_top, in1=larger, op=ALU.subtract).then_inc(differed, 1)

                def add_up(c):
                    dve.wait_ge(exped, c + 1)
                    wide = [by_head4(t, c) for t in (own, other)]
                    for s, t in enumerate(wide):
                        last = nc.vector.tensor_tensor(out=t, in0=t, in1=of_tile(tops, c, 2 * HEADS)[:, :, s * HEADS:(s + 1) * HEADS]
                                                       .unsqueeze(3).broadcast_to([P, CHUNK, HEADS, DH + 1]), op=ALU.mult)
                    counted(last, c, "scaled")
                    dve.wait_ge(step, done[c, "scaled"])
                    counted(nc.vector.tensor_tensor(out=of_tile(own, c, STATE)[:, :, 0:WIDE], in0=of_tile(own, c, STATE)[:, :, 0:WIDE],
                                                    in1=of_tile(other, c, STATE)[:, :, 0:WIDE], op=ALU.add), c, "added")
                    dve.wait_ge(step, done[c, "added"])
                    sums, inverse = of_tile(own, c, STATE)[:, :, DH:WIDE:DH + 1], of_tile(part, c, HEADS)
                    counted(nc.vector.tensor_scalar(out=inverse, in0=sums, scalar1=0.5, scalar2=None, op0=ALU.max), c, "sums")
                    dve.wait_ge(step, done[c, "sums"])
                    counted(nc.vector.reciprocal(inverse, inverse), c, "inverse")
                    dve.wait_ge(step, done[c, "inverse"])
                    counted(nc.vector.tensor_tensor(out=inverse, in0=inverse, in1=order.some[:, c * CHUNK:(c + 1) * CHUNK]
                                                    .unsqueeze(2).broadcast_to([P, CHUNK, HEADS]), op=ALU.mult), c, "some")
                    dve.wait_ge(step, done[c, "some"])
                    values = wide[0][:, :, :, 0:DH]
                    counted(nc.vector.tensor_tensor(out=values, in0=values, in1=inverse.unsqueeze(3).broadcast_to([P, CHUNK, HEADS, DH]),
                                                    op=ALU.mult), c, "divided")
                    dve.wait_ge(step, done[c, "divided"])
                    x_c, out_c = (tile_at(t, c * CHUNK, CHUNK).rearrange("p (a h d) -> p a h d", a=CHUNK, h=HEADS) for t in (x, out))
                    nc.vector.tensor_tensor(out=out_c, in0=x_c, in1=values, op=ALU.add)

                def by_head4(t, c):
                    return of_tile(t, c, STATE)[:, :, 0:WIDE].rearrange("p a (h d) -> p a h d", d=DH + 1)

                compare_tops(0)
                for c in range(TILES // CHUNK):
                    if c + 1 < TILES // CHUNK:
                        compare_tops(c + 1)
                    add_up(c)


def feed_forward(nc, env, y, out, rest, x, bias, w_in, b_in, w_out):
    blocks, hidden = TILES // 4, DFF // P
    with ExitStack() as stack:
        def sb(name, cols):
            return buffer(stack, nc, name, cols)
        staged_y, yt, ht = sb("staged_y", 4 * D), sb("yt", 2 * 4 * P), sb("ht", hidden * 4 * P)
        with phase(nc, "staged", "turned", "copied", "made", "bent", "multiplied", "kept", "summed", "held") as \
                (staged, turned, copied, made, bent, multiplied, kept, summed, held), nc.Block() as block:
            def over_blocks(engine, body):
                body(0, 4)
                with engine.Fori(1, blocks) as i:
                    body(i, 4)
                body(blocks, TILES - 4 * blocks)

            def later(i):
                return not isinstance(i, int) or i > 0

            @block.gpsimd
            def _(pool):
                def body(i, n):
                    if later(i):
                        pool.wait_ge(turned, 2 * i)
                        pool.sem_inc(held, 1)
                    pool.tensor_copy(staged_y[:, 0:n * D], y[:, bass.ds(i * (4 * D), n * D)]).then_inc(staged, 1)
                over_blocks(pool, body)

            @block.tensor
            def _(pe):
                def turn(i, n):
                    pe.wait_ge(staged, i + 1)
                    pe.sem_inc(held, 1)
                    if later(i):
                        pe.wait_ge(copied, 2 * i)
                        pe.sem_inc(held, 1)
                    for s in range(2):
                        for t in range(n):
                            last = nc.tensor.transpose(env.bank[s][:, t * P:(t + 1) * P], staged_y[:, t * D + s * P:t * D + (s + 1) * P], env.ident[:])
                        last.then_inc(turned, 1)

                def hide(i, n):
                    pe.wait_ge(copied, 2 * i + 2)
                    pe.sem_inc(held, 1)
                    for f in range(hidden):
                        bank = env.bank[2 + f % 4]
                        if later(i) or f >= 4:
                            pe.wait_ge(bent, i * hidden + f - 3)
                            pe.sem_inc(held, 1)
                        for s in range(2):
                            last = nc.tensor.matmul(bank[:, 0:n * P], w_in[:, s * DFF + f * P:s * DFF + (f + 1) * P],
                                                    yt[:, s * 4 * P:s * 4 * P + n * P], start=s == 0, stop=s == 1)
                        last.then_inc(made, 1)

                def multiply(i, n):
                    pe.wait_ge(bent, (i + 1) * hidden)
                    pe.sem_inc(held, 1)
                    for t in range(n):
                        if later(i) or t >= 2:
                            pe.wait_ge(kept, 4 * i + t - 1)
                            pe.sem_inc(held, 1)
                        for f in range(hidden):
                            last = nc.tensor.matmul(env.bank[6 + t % 2][:, 0:D], ht[:, (f * 4 + t) * P:(f * 4 + t + 1) * P],
                                                    w_out[:, f * D:(f + 1) * D], start=f == 0, stop=f == hidden - 1)
                        last.then_inc(multiplied, 1)

                def body(i, n, n_next):
                    hide(i, n)
                    turn(i + 1, n_next)
                    multiply(i, n)
                turn(0, 4)
                body(0, 4, 4)
                with pe.Fori(1, blocks - 1) as i:
                    body(i, 4, 4)
                body(blocks - 1, 4, TILES - 4 * blocks)
                hide(blocks, TILES - 4 * blocks)
                multiply(blocks, TILES - 4 * blocks)

            @block.scalar
            def _(act):
                def body(i, n):
                    if later(i):
                        act.wait_ge(multiplied, 4 * i)
                        act.sem_inc(held, 1)
                    for f in range(hidden):
                        act.wait_ge(made, i * hidden + f + 1)
                        act.sem_inc(held, 1)
                        nc.scalar.activation(ht[:, f * 4 * P:f * 4 * P + n * P], env.bank[2 + f % 4][:, 0:n * P], ACT.Gelu,
                                             bias=b_in[:, f:f + 1]).then_inc(bent, 1)
                over_blocks(act, body)

            @block.vector
            def _(dve):
                def take(i, n):
                    if later(i):
                        dve.wait_ge(made, i * hidden)
                        dve.sem_inc(held, 1)
                    for s in range(2):
                        dve.wait_ge(turned, 2 * i + s + 1)
                        dve.sem_inc(held, 1)
                        nc.vector.tensor_copy(yt[:, s * 4 * P:s * 4 * P + n * P], env.bank[s][:, 0:n * P]).then_inc(copied, 1)

                def keep(i, n):
                    for t in range(n):
                        dve.wait_ge(multiplied, 4 * i + t + 1)
                        dve.sem_inc(held, 1)
                        at = (4 * i + t) * D
                        nc.vector.tensor_tensor(out=out[:, bass.ds(at, D)], in0=env.bank[6 + t % 2][:, 0:D],
                                                in1=rest[:, bass.ds(at, D)], op=ALU.add).then_inc(kept, 1)

                take(0, 4)
                nc.vector.tensor_tensor(out=rest[:], in0=rest[:], in1=x[:], op=ALU.add).then_inc(summed, 1)
                dve.wait_ge(summed, 1)
                nc.vector.tensor_tensor(out=bulk(rest[:]), in0=bulk(rest[:]), in1=over_tiles(bias[:]), op=ALU.add).then_inc(summed, 1)
                take(1, 4)
                dve.wait_ge(summed, 2)
                dve.sem_inc(held, 1)
                keep(0, 4)
                with dve.Fori(1, blocks - 1) as i:
                    take(i + 1, 4)
                    keep(i, 4)
                take(blocks, TILES - 4 * blocks)
                keep(blocks - 1, 4)
                keep(blocks, TILES - 4 * blocks)


def attention_layer(outer, nc, env, order, x, y, given, qv_table, k_table, states, out):
    w_qkv, b_qkv, attn_gain, attn_shift, res_gain, res_shift, w_in, b_in, w_out, b_out = given
    gain, shift = buffer(outer, nc, "gain", D), buffer(outer, nc, "shift", D)
    with ExitStack() as stack:
        weights, bias = buffer(stack, nc, "weights", 2 * 3 * D), buffer(stack, nc, "bias", 3 * D)
        load_all(nc, (halves(weights, 3 * D), by_halves(w_qkv)), (bias[:], spread(b_qkv)), (gain[:], spread(attn_gain)), (shift[:], spread(attn_shift)))
        row_norm(nc, x, y, gain[:], shift[:])
        staged_qv = [buffer(stack, nc, "staged_qv", QV) for _ in range(2)]
        staged_k = [buffer(stack, nc, "staged_k", D) for _ in range(2)]
        scale = float(D) ** -0.5
        with phase(nc, "step") as (step,), nc.Block() as block:
            @block.vector
            def _(dve):
                nc.vector.tensor_scalar(out=bias[:, 0:D], in0=bias[:, 0:D], scalar1=scale, scalar2=None, op0=ALU.mult).then_inc(step, 1)
                for h in range(2):
                    nc.vector.memset(staged_qv[h][:], 1.0).then_inc(step, 1)
                dve.wait_ge(step, 3)

        def use_q(engine, i, h, bank, after):
            return nc.vector.scalar_tensor_tensor(out=staged_qv[h][:, 0:D], in0=bank, scalar=scale, in1=bias[:, 0:D], op0=ALU.mult, op1=ALU.add)

        def use_k(engine, i, h, bank, after):
            return nc.vector.tensor_tensor(out=staged_k[h][:], in0=bank, in1=bias[:, D:2 * D], op=ALU.add)

        def use_v(engine, i, h, bank, after):
            return nc.vector.tensor_tensor(out=by_head(staged_qv[h][:, D:])[:, :, 0:DH], in0=bank.rearrange("p (h d) -> p h d", h=HEADS),
                                           in1=bias[:, 2 * D:].rearrange("p (h d) -> p h d", h=HEADS), op=ALU.add)
        qv_of, k_of = (t.rearrange("(a p) d -> a p d", p=P) for t in (qv_table, k_table))
        project(nc, env, y, weights, 3 * D, [(0, D, "vector", use_q), (D, D, "vector", use_k), (2 * D, D, "vector", use_v)],
                [([0, 2], lambda k: qv_of[bass.ds(k, 1)].squeeze(0), lambda h: staged_qv[h][:]),
                 ([1], lambda k: k_of[bass.ds(k, 1)].squeeze(0), lambda h: staged_k[h][:])], 6)
    with ExitStack() as stack:
        tail = buffer(stack, nc, "tail", STATE)
        attention_pass(nc, env, order, qv_table, k_table, states, tail, y)
        attention_collect(nc, env, order, states, tail, x, y, [(gain[:], spread(res_gain)), (shift[:], spread(res_shift))])
    with ExitStack() as stack:
        bias = buffer(stack, nc, "bias", D)
        hidden_in, hidden_out = buffer(stack, nc, "hidden_in", TILES * D), buffer(stack, nc, "hidden_out", TILES * D)
        tile_in, tile_out, tile_b = buffer(stack, nc, "w_in", 2 * DFF), buffer(stack, nc, "w_out", DFF // P * D), buffer(stack, nc, "b_in", DFF // P)
        row_norm(nc, y, hidden_in, gain[:], shift[:], loads=[
            (halves(tile_in, DFF), by_halves(w_in)), (tile_out[:].rearrange("p (f o) -> p f o", o=D), w_out.rearrange("(f p) o -> p f o", p=P)),
            (tile_b[:], b_in), (bias[:], spread(b_out))])
        feed_forward(nc, env, hidden_in, hidden_out, y, x, bias, tile_in, tile_b, tile_out)
        row_norm(nc, hidden_out, x, dram=out)


NAMES = ["x", "src", "dst", "edge_type_16", "edge_weight", "L0_gnn_thetas", "L0_gnn_phis", "L0_gnn_gammas", "L0_gnn_betas",
         "L1_gnn_basis1", "L1_gnn_att1", "L1_gnn_root1", "L1_gnn_bias1", "L1_gnn_ln1_g", "L1_gnn_ln1_b",
         "L1_gnn_basis2", "L1_gnn_att2", "L1_gnn_root2", "L1_gnn_bias2", "L1_gnn_ln2_g", "L1_gnn_ln2_b",
         "L2_gnn_W", "L2_gnn_b", "L3_gnn_Wqkv", "L3_gnn_bqkv", "L3_gnn_ln_attn_g", "L3_gnn_ln_attn_b",
         "L3_gnn_ln_res_g", "L3_gnn_ln_res_b", "L3_gnn_W_in", "L3_gnn_b_in", "L3_gnn_W_out", "L3_gnn_b_out"]


def graph_program(nc, given, out):
    def scratch(name, rows, cols):
        return nc.dram_tensor(name, (rows, cols), FP32, kind="Internal").ap()
    states = scratch("states", SLOTS, D)
    wide_states = scratch("wide_states", SLOTS, STATE)
    table, typed_table = scratch("table", ROWS, D), scratch("typed_table", ROWS * TYPES, D)
    qv_table, k_table = scratch("qv_table", ROWS, QV), scratch("k_table", ROWS, D)
    with ExitStack() as stack:
        env = shared(stack, nc)
        constants(nc, env)
        by_source, by_target = BySource(stack, nc, "by_source"), ByTarget(stack, nc, "by_target")
        with ExitStack() as inner:
            env.records = buffer(inner, nc, "records", 2 * STEPS)
            by_target.scatter = scatter = Scatter(inner, nc, env.records, scratch("records_sorted", SLOTS, 2))
            edge_buffers(inner, nc, env)
            edge_columns(nc, env, given["dst"], given["src"], given["edge_type_16"], given["edge_weight"])
            edge_order(nc, env, by_target, NOTHING)
            env.piece = [buffer(inner, nc, f"piece{i}", STEPS) for i in range(2)]
            edge_columns(nc, env, given["src"], given["dst"])
            edge_order(nc, env, by_source, scatter)
            by_target.take(nc, env)
        for order in (by_source, by_target):
            order.end_row = buffer(stack, nc, "end_row", ROWS, BF16)
        x, y = buffer(stack, nc, "x", TILES * D), buffer(stack, nc, "y", TILES * D)
        by_source.spread_ends(nc, env, given["x"], (x,))
        by_target.spread_ends(nc, env, given["x"], (y,))
        with ExitStack() as inner:
            out_of, own = buffer(inner, nc, "out_of", TILES * D), buffer(inner, nc, "own", TILES * D)

            def copy_x():
                with phase(nc, "copied") as (copied,), nc.Block() as block:
                    @block.vector
                    def _(dve):
                        nc.vector.tensor_copy(y[:], x[:]).then_inc(copied, 1)
                        dve.wait_ge(copied, 1)

            def join():
                add_all(nc, y, (bulk(x[:]), ALU.add))
                row_norm(nc, y, x)
            relative_block(nc, env, by_source, y, out_of, own, given["L0_gnn_thetas"], given["L0_gnn_phis"],
                           given["L0_gnn_gammas"], given["L0_gnn_betas"], table, states)
            join()
            copy_x()
            for n in "12":
                relational_layer(nc, env, by_target, y, out_of, own, *(given["L1_gnn_" + w] for w in (
                    "basis" + n, "att" + n, "root" + n, "bias" + n, f"ln{n}_g", f"ln{n}_b")), typed_table, states)
            join()
            normalised_layer(nc, env, by_target, x, out_of, own, given["L2_gnn_W"], given["L2_gnn_b"], table, states)
        attention_layer(stack, nc, env, by_target, x, y, [given["L3_gnn_" + w] for w in (
            "Wqkv", "bqkv", "ln_attn_g", "ln_attn_b", "ln_res_g", "ln_res_b", "W_in", "b_in", "W_out", "b_out")],
            qv_table, k_table, wide_states, out)


def kernel(**inputs):
    import numpy as _np
    import concourse.bacc as _bacc
    from concourse import mybir as _mybir
    from concourse.bass_utils import run_bass_kernel_spmd as _run

    nc = _bacc.Bacc("TRN2", target_bir_lowering=False, num_devices=1)
    arrays, given = {}, {}
    for name in NAMES:
        a = _np.asarray(inputs[name])
        if name in ("L0_gnn_thetas", "L0_gnn_phis"):
            a = a.transpose(0, 2, 1)
        if name == "L3_gnn_b_in":
            a = a.reshape(DFF // P, P).T
        a = _np.ascontiguousarray(a)
        arrays[f"in_{name}"] = a
        given[name] = nc.dram_tensor(f"in_{name}", a.shape, _mybir.dt.from_np(a.dtype), kind="ExternalInput").ap()
    out = nc.dram_tensor("out", (N, D), FP32, kind="ExternalOutput").ap()
    graph_program(nc, given, out)
    result = _run(nc, [arrays], core_ids=[0])
    return result.results[0]["out"]
```
